# Optimizing a Trainium2 kernel written in Bass

```python
import numpy as np
import jax
import jax.numpy as jnp

def _softmax(x, axis=-1):
    return jax.nn.softmax(x, axis=axis)

def _gelu(x):
    return jax.nn.gelu(x, approximate=True)

def _silu(x):
    return jax.nn.silu(x)

def _sigmoid(x):
    return jax.nn.sigmoid(x)

def _layernorm(x, axis=-1, eps=1e-05):
    m = jnp.mean(x, axis=axis, keepdims=True)
    v = jnp.var(x, axis=axis, keepdims=True)
    return (x - m) / jnp.sqrt(v + eps)

def _scatter_add(tgt, idx, src, axis=0):
    return tgt.at[idx].add(src)

def _segment_sum(src, seg, n):
    return jax.ops.segment_sum(src, seg, n)
kernel_name = 'mk_adj_preln_d4_adj_r2_50691f'

def setup_inputs(seed: int=0):
    np.random.seed(seed)
    _w = jnp.asarray

    def _rec_inputs():
        import jax
        import jax.numpy as jnp
        _gk = jax.random.key(seed)
        x = -0.0002928 + 1 * jax.random.normal(jax.random.fold_in(_gk, 1), (32, 256, 128), jnp.float32)
        _a = jax.random.bernoulli(jax.random.fold_in(_gk, 2), 0.03125, (32, 256, 256))
        _a = jnp.logical_or(_a, jnp.swapaxes(_a, -1, -2))
        _a = jnp.logical_or(_a, jnp.eye(256, dtype=bool))
        _af = _a.astype(jnp.float32)
        _af = _af * jax.random.uniform(jax.random.fold_in(_gk, 3), (32, 256, 256), jnp.float32, 0.05, 1)
        adj = _af
        return (x, adj)
    x, adj = _rec_inputs()

    def _L0_gnn_setup():
        import jax, jax.numpy as jnp
        import numpy as np
        B, N, D, H = (8, 1024, 128, 512)
        RMS_EPS = 1e-06

        def _rmsnorm(h, w, eps=RMS_EPS):
            var = jnp.mean(jnp.square(h), axis=-1, keepdims=True)
            return h * jax.lax.rsqrt(var + eps) * w
        key = jax.random.key(seed)
        ks = jax.random.split(key, 5)
        x = jax.random.normal(ks[0], (B, N, D), dtype=jnp.float32)
        adjacency = jax.random.uniform(ks[1], (B, N, N), dtype=jnp.float32)
        epsilon = jnp.zeros((), dtype=jnp.float32)
        W1 = jax.random.normal(ks[2], (D, H), dtype=jnp.float32) * (1.0 / np.sqrt(D))
        b1 = jnp.zeros((H,), dtype=jnp.float32)
        rms_weight = jnp.ones((H,), dtype=jnp.float32)
        W2 = jax.random.normal(ks[3], (H, D), dtype=jnp.float32) * (1.0 / np.sqrt(H))
        b2 = jnp.zeros((D,), dtype=jnp.float32)
        return {'x': x, 'adjacency': adjacency, 'epsilon': epsilon, 'W1': W1, 'b1': b1, 'rms_weight': rms_weight, 'W2': W2, 'b2': b2}
    _L0_gnn_all = _L0_gnn_setup()
    _L0_gnn_in = {k: v for k, v in _L0_gnn_all.items() if k in ('epsilon', 'W1', 'b1', 'rms_weight', 'W2', 'b2')}
    del _L0_gnn_all

    def _L1_gnn_setup():
        import jax, jax.numpy as jnp
        import numpy as np
        from jax import lax
        DIM = 128
        EPS = 1e-05

        def _bn(h, g, b, m, v):
            scale = g / jnp.sqrt(v + EPS)
            return h * scale[None, :, None] + (b - m * scale)[None, :, None]

        def _conv1d(h, w, pad):
            return lax.conv_general_dilated(h, w, window_strides=(1,), padding=[(pad, pad)], dimension_numbers=('NCH', 'OIH', 'NCH'))
        key = jax.random.key(seed)
        ks = jax.random.split(key, 16)
        bs, n, d = (16, 1024, DIM)
        s = 0.05
        return {'x': jax.random.normal(ks[0], (bs, n, d), jnp.float32), 'mask': jnp.ones((bs, n, n), jnp.float32), 'w_se': jax.random.normal(ks[1], (3, d), jnp.float32) * s, 'b_se': jnp.zeros((3,), jnp.float32), 'conv1_w': jax.random.normal(ks[2], (d, d, 1), jnp.float32) * s, 'bn1_g': jnp.ones((d,), jnp.float32), 'bn1_b': jnp.zeros((d,), jnp.float32), 'bn1_m': jnp.zeros((d,), jnp.float32), 'bn1_v': jnp.ones((d,), jnp.float32), 'conv2_w': jax.random.normal(ks[3], (d, d, 17), jnp.float32) * s, 'bn2_g': jnp.ones((d,), jnp.float32), 'bn2_b': jnp.zeros((d,), jnp.float32), 'bn2_m': jnp.zeros((d,), jnp.float32), 'bn2_v': jnp.ones((d,), jnp.float32), 'w_msg': jax.random.normal(ks[4], (d, d), jnp.float32) * s, 'b_msg': jnp.zeros((d,), jnp.float32), 'w_ih': jax.random.normal(ks[5], (3 * d, 2 * d), jnp.float32) * s, 'b_ih': jnp.zeros((3 * d,), jnp.float32), 'w_hh': jax.random.normal(ks[6], (3 * d, d), jnp.float32) * s, 'b_hh': jnp.zeros((3 * d,), jnp.float32)}
    _L1_gnn_all = _L1_gnn_setup()
    _L1_gnn_in = {k: v for k, v in _L1_gnn_all.items() if k in ('w_se', 'b_se', 'conv1_w', 'bn1_g', 'bn1_b', 'bn1_m', 'bn1_v', 'conv2_w', 'bn2_g', 'bn2_b', 'bn2_m', 'bn2_v', 'w_msg', 'b_msg', 'w_ih', 'b_ih', 'w_hh', 'b_hh')}
    del _L1_gnn_all

    def _L2_gnn_setup():
        import jax, jax.numpy as jnp
        import numpy as np
        GROUPS = [list(range(25)), [0, 1, 2, 3, 4, 5, 6, 7, 8], [0, 9, 10, 11, 12, 13, 14], [6, 7, 8, 12, 13, 14], [3, 4, 5, 9, 10, 11]]
        B, N, D_IN, D_HID = (4096, 25, 128, 256)

        def _graph_conv(x, adj, W, b):
            n = adj.shape[-1]
            A = adj + jnp.eye(n, dtype=adj.dtype)
            deg = jnp.sum(A, axis=-1)
            deg_safe = jnp.where(deg == 0, 1.0, deg)
            dinv = jnp.where(deg == 0, 0.0, deg_safe ** (-0.5))
            norm_adj = dinv[:, :, None] * A * dinv[:, None, :]
            support = jnp.einsum('bnd,de->bne', x, W)
            out = jnp.einsum('bnm,bme->bne', norm_adj, support) + b
            return jax.nn.relu(out)
        key = jax.random.key(seed)
        ks = jax.random.split(key, 7)
        s1 = float(np.sqrt(6.0 / (D_IN + D_HID)))
        s2 = float(np.sqrt(6.0 / (D_HID + D_IN)))
        return {'x': jax.random.normal(ks[0], (B, N, D_IN), dtype=jnp.float32), 'adj': jax.random.uniform(ks[1], (B, N, N), dtype=jnp.float32), 'W1': jax.random.uniform(ks[2], (5, D_IN, D_HID), jnp.float32, -s1, s1), 'b1': jnp.zeros((5, D_HID), dtype=jnp.float32), 'W2': jax.random.uniform(ks[3], (5, D_HID, D_IN), jnp.float32, -s2, s2), 'b2': jnp.zeros((5, D_IN), dtype=jnp.float32), 'fusion_w': jnp.ones((5,), dtype=jnp.float32)}
    _L2_gnn_all = _L2_gnn_setup()
    _L2_gnn_in = {k: v for k, v in _L2_gnn_all.items() if k in ('W1', 'b1', 'W2', 'b2', 'fusion_w')}
    del _L2_gnn_all

    def _L3_gnn_setup():
        import jax, jax.numpy as jnp
        import numpy as np
        B, N, D = (2, 2048, 128)
        key = jax.random.key(seed)
        ks = jax.random.split(key, 6)
        return {'hidden': jax.random.normal(ks[0], (B, N, D), dtype=jnp.float32), 'mask': jax.random.uniform(ks[1], (B, N, N), dtype=jnp.float32), 'W_w': jax.random.normal(ks[2], (D, D), dtype=jnp.float32) * 0.05, 'W_b': jax.random.normal(ks[3], (D,), dtype=jnp.float32) * 0.05, 'a_w': jax.random.normal(ks[4], (2 * D,), dtype=jnp.float32) * 0.05, 'a_b': jax.random.normal(ks[5], (1,), dtype=jnp.float32) * 0.05}
    _L3_gnn_all = _L3_gnn_setup()
    _L3_gnn_in = {k: v for k, v in _L3_gnn_all.items() if k in ('W_w', 'W_b', 'a_w', 'a_b')}
    del _L3_gnn_all
    return {'x': x, 'adj': adj, 'L0_gnn_epsilon': _L0_gnn_in['epsilon'], 'L0_gnn_W1': _L0_gnn_in['W1'], 'L0_gnn_b1': _L0_gnn_in['b1'], 'L0_gnn_rms_weight': _L0_gnn_in['rms_weight'], 'L0_gnn_W2': _L0_gnn_in['W2'], 'L0_gnn_b2': _L0_gnn_in['b2'], 'L1_gnn_w_se': _L1_gnn_in['w_se'], 'L1_gnn_b_se': _L1_gnn_in['b_se'], 'L1_gnn_conv1_w': _L1_gnn_in['conv1_w'], 'L1_gnn_bn1_g': _L1_gnn_in['bn1_g'], 'L1_gnn_bn1_b': _L1_gnn_in['bn1_b'], 'L1_gnn_bn1_m': _L1_gnn_in['bn1_m'], 'L1_gnn_bn1_v': _L1_gnn_in['bn1_v'], 'L1_gnn_conv2_w': _L1_gnn_in['conv2_w'], 'L1_gnn_bn2_g': _L1_gnn_in['bn2_g'], 'L1_gnn_bn2_b': _L1_gnn_in['bn2_b'], 'L1_gnn_bn2_m': _L1_gnn_in['bn2_m'], 'L1_gnn_bn2_v': _L1_gnn_in['bn2_v'], 'L1_gnn_w_msg': _L1_gnn_in['w_msg'], 'L1_gnn_b_msg': _L1_gnn_in['b_msg'], 'L1_gnn_w_ih': _L1_gnn_in['w_ih'], 'L1_gnn_b_ih': _L1_gnn_in['b_ih'], 'L1_gnn_w_hh': _L1_gnn_in['w_hh'], 'L1_gnn_b_hh': _L1_gnn_in['b_hh'], 'L2_gnn_W1': _L2_gnn_in['W1'], 'L2_gnn_b1': _L2_gnn_in['b1'], 'L2_gnn_W2': _L2_gnn_in['W2'], 'L2_gnn_b2': _L2_gnn_in['b2'], 'L2_gnn_fusion_w': _L2_gnn_in['fusion_w'], 'L3_gnn_W_w': _L3_gnn_in['W_w'], 'L3_gnn_W_b': _L3_gnn_in['W_b'], 'L3_gnn_a_w': _L3_gnn_in['a_w'], 'L3_gnn_a_b': _L3_gnn_in['a_b']}

def reference(x, adj, L0_gnn_epsilon, L0_gnn_W1, L0_gnn_b1, L0_gnn_rms_weight, L0_gnn_W2, L0_gnn_b2, L1_gnn_w_se, L1_gnn_b_se, L1_gnn_conv1_w, L1_gnn_bn1_g, L1_gnn_bn1_b, L1_gnn_bn1_m, L1_gnn_bn1_v, L1_gnn_conv2_w, L1_gnn_bn2_g, L1_gnn_bn2_b, L1_gnn_bn2_m, L1_gnn_bn2_v, L1_gnn_w_msg, L1_gnn_b_msg, L1_gnn_w_ih, L1_gnn_b_ih, L1_gnn_w_hh, L1_gnn_b_hh, L2_gnn_W1, L2_gnn_b1, L2_gnn_W2, L2_gnn_b2, L2_gnn_fusion_w, L3_gnn_W_w, L3_gnn_W_b, L3_gnn_a_w, L3_gnn_a_b):
    import jax
    import jax.numpy as jnp

    def _L0_gnn_ref(x, adjacency, epsilon, W1, b1, rms_weight, W2, b2):
        import jax, jax.numpy as jnp
        import numpy as np
        B, N, D, H = (8, 1024, 128, 512)
        RMS_EPS = 1e-06

        def _rmsnorm(h, w, eps=RMS_EPS):
            var = jnp.mean(jnp.square(h), axis=-1, keepdims=True)
            return h * jax.lax.rsqrt(var + eps) * w
        neighbor_sum = jnp.einsum('bnm,bmd->bnd', adjacency, x)
        agg = epsilon * x + neighbor_sum
        h = jnp.einsum('bnd,dh->bnh', agg, W1) + b1
        h = jax.nn.silu(_rmsnorm(h, rms_weight))
        out = jnp.einsum('bnh,hd->bnd', h, W2) + b2
        return out

    def _L1_gnn_ref(x, mask, w_se, b_se, conv1_w, bn1_g, bn1_b, bn1_m, bn1_v, conv2_w, bn2_g, bn2_b, bn2_m, bn2_v, w_msg, b_msg, w_ih, b_ih, w_hh, b_hh):
        import jax, jax.numpy as jnp
        import numpy as np
        from jax import lax
        DIM = 128
        EPS = 1e-05

        def _bn(h, g, b, m, v):
            scale = g / jnp.sqrt(v + EPS)
            return h * scale[None, :, None] + (b - m * scale)[None, :, None]

        def _conv1d(h, w, pad):
            return lax.conv_general_dilated(h, w, window_strides=(1,), padding=[(pad, pad)], dimension_numbers=('NCH', 'OIH', 'NCH'))
        d = x.shape[-1]
        xc = jnp.transpose(x, (0, 2, 1))
        h = _bn(_conv1d(xc, conv1_w, 0), bn1_g, bn1_b, bn1_m, bn1_v)
        h = jax.nn.relu(h)
        h = _bn(_conv1d(h, conv2_w, 8), bn2_g, bn2_b, bn2_m, bn2_v)
        x_conv = jnp.transpose(jax.nn.relu(h + xc), (0, 2, 1))
        s = x @ w_se.T + b_se
        sq = jnp.sum(s * s, axis=-1)
        dist = sq[:, :, None] + sq[:, None, :] - 2.0 * jnp.einsum('bnd,bmd->bnm', s, s)
        A = jnp.exp(-dist) * mask
        msg = jax.nn.relu(x @ w_msg.T + b_msg)
        x_nmp = jnp.einsum('bnm,bmd->bnd', A, msg)
        x_in = jnp.concatenate([x_conv, x_nmp], axis=-1)
        gi = x_in @ w_ih.T + b_ih
        gh = x @ w_hh.T + b_hh
        gi_r, gi_z, gi_n = (gi[..., :d], gi[..., d:2 * d], gi[..., 2 * d:])
        gh_r, gh_z, gh_n = (gh[..., :d], gh[..., d:2 * d], gh[..., 2 * d:])
        r = jax.nn.sigmoid(gi_r + gh_r)
        z = jax.nn.sigmoid(gi_z + gh_z)
        nn_ = jnp.tanh(gi_n + r * gh_n)
        return (1.0 - z) * nn_ + z * x

    def _L2_gnn_ref(x, adj, W1, b1, W2, b2, fusion_w):
        import jax, jax.numpy as jnp
        import numpy as np
        GROUPS = [list(range(25)), [0, 1, 2, 3, 4, 5, 6, 7, 8], [0, 9, 10, 11, 12, 13, 14], [6, 7, 8, 12, 13, 14], [3, 4, 5, 9, 10, 11]]
        B, N, D_IN, D_HID = (4096, 25, 128, 256)

        def _graph_conv(x, adj, W, b):
            n = adj.shape[-1]
            A = adj + jnp.eye(n, dtype=adj.dtype)
            deg = jnp.sum(A, axis=-1)
            deg_safe = jnp.where(deg == 0, 1.0, deg)
            dinv = jnp.where(deg == 0, 0.0, deg_safe ** (-0.5))
            norm_adj = dinv[:, :, None] * A * dinv[:, None, :]
            support = jnp.einsum('bnd,de->bne', x, W)
            out = jnp.einsum('bnm,bme->bne', norm_adj, support) + b
            return jax.nn.relu(out)
        norm_w = jax.nn.softmax(fusion_w)
        fused = jnp.zeros_like(x)
        for g, idx_list in enumerate(GROUPS):
            idx = jnp.asarray(idx_list)
            x_g = x[:, idx, :]
            adj_g = adj[:, idx][:, :, idx]
            h = _graph_conv(x_g, adj_g, W1[g], b1[g])
            out_g = _graph_conv(h, adj_g, W2[g], b2[g])
            fused = fused.at[:, idx, :].add(norm_w[g] * out_g)
        return fused

    def _L3_gnn_ref(hidden, mask, W_w, W_b, a_w, a_b):
        import jax, jax.numpy as jnp
        import numpy as np
        B, N, D = (2, 2048, 128)
        h = jnp.einsum('bnd,ed->bne', hidden, W_w) + W_b
        Dh = h.shape[-1]
        a1, a2 = (a_w[:Dh], a_w[Dh:])
        e = h @ a1
        f = h @ a2
        logits = e[:, :, None] + f[:, None, :] + a_b[0]
        u = mask * jnp.exp(logits)
        a = u / jnp.sum(u, axis=2, keepdims=True)
        h_prime = jnp.einsum('bnm,bmd->bnd', a, h)
        return h_prime
    h = jnp.maximum(_layernorm(x, axis=-1), 0.0)
    x = x + _L0_gnn_ref(h, adj, L0_gnn_epsilon, L0_gnn_W1, L0_gnn_b1, L0_gnn_rms_weight, L0_gnn_W2, L0_gnn_b2)
    h = jnp.maximum(_layernorm(x, axis=-1), 0.0)
    x = x + _L1_gnn_ref(h, adj, L1_gnn_w_se, L1_gnn_b_se, L1_gnn_conv1_w, L1_gnn_bn1_g, L1_gnn_bn1_b, L1_gnn_bn1_m, L1_gnn_bn1_v, L1_gnn_conv2_w, L1_gnn_bn2_g, L1_gnn_bn2_b, L1_gnn_bn2_m, L1_gnn_bn2_v, L1_gnn_w_msg, L1_gnn_b_msg, L1_gnn_w_ih, L1_gnn_b_ih, L1_gnn_w_hh, L1_gnn_b_hh)
    h = jnp.maximum(_layernorm(x, axis=-1), 0.0)
    x = x + _L2_gnn_ref(h, adj, L2_gnn_W1, L2_gnn_b1, L2_gnn_W2, L2_gnn_b2, L2_gnn_fusion_w)
    h = jnp.maximum(_layernorm(x, axis=-1), 0.0)
    x = x + _L3_gnn_ref(h, adj, L3_gnn_W_w, L3_gnn_W_b, L3_gnn_a_w, L3_gnn_a_b)
    return x

_drawn_inputs = setup_inputs


def setup_inputs(seed=0):
    import zlib

    import numpy as np

    out = dict(_drawn_inputs(seed))
    spreads = {'L0_gnn_b1': (0.0, 0.442),
     'L0_gnn_rms_weight': (1.0, 0.2),
     'L0_gnn_b2': (0.0, 0.1),
     'L1_gnn_b_se': (0.0, 2.0),
     'L1_gnn_bn1_g': (1.0, 0.6),
     'L1_gnn_bn1_b': (0.0, 0.4),
     'L1_gnn_bn1_m': (0.0, 0.393),
     'L1_gnn_bn1_v': (1.0, 0.6),
     'L1_gnn_bn2_g': (1.0, 0.6),
     'L1_gnn_bn2_b': (0.0, 0.653),
     'L1_gnn_bn2_m': (0.0, 0.562),
     'L1_gnn_bn2_v': (1.0, 0.6),
     'L1_gnn_b_msg': (0.0, 0.1),
     'L1_gnn_b_ih': (0.0, 0.29),
     'L1_gnn_b_hh': (0.0, 0.452),
     'L2_gnn_b1': (0.0, 0.8),
     'L2_gnn_b2': (0.0, 2.0),
     'L2_gnn_fusion_w': (1.0, 0.6)}
    factors = {'L2_gnn_W1': 4.56, 'L2_gnn_W2': 3.658, 'L3_gnn_a_w': 4.426}
    for name, (base, spread) in spreads.items():
        noise = np.random.default_rng([zlib.crc32(name.encode()), seed]).standard_normal(out[name].shape)
        drawn = base * np.exp(spread * noise) if base else spread * noise
        out[name] = jnp.asarray(drawn.astype(out[name].dtype))
    for name, factor in factors.items():
        out[name] = (out[name] * factor).astype(out[name].dtype)
    return out
```

```python
from contextlib import ExitStack

import concourse.bass as bass
from concourse import mybir

F32 = mybir.dt.float32
F32R = mybir.dt.float32r
ACT = mybir.ActivationFunctionType
ALU = mybir.AluOpType
AX = mybir.AxisListType

GRAPHS, NODES, D = 32, 256, 128
P = 128
TILES = NODES // P
PAIRS = GRAPHS // 2
RING = 4
Q = 2 * TILES
W = 2 * NODES
HID0 = 512
C0 = HID0 // P
TAPS, PAD = 17, 8
PADW = NODES + 2 * PAD
GROUPS = [list(range(25)), [0, 1, 2, 3, 4, 5, 6, 7, 8], [0, 9, 10, 11, 12, 13, 14], [6, 7, 8, 12, 13, 14],
          [3, 4, 5, 9, 10, 11]]
NG = len(GROUPS)
JOINTS = 25
HID2 = 256
C2 = HID2 // P
STACK = [(g, a, n) for g, nodes in enumerate(GROUPS) for a in range(2) for n in nodes]
NS = len(STACK)
G_START = [min(i for i, s in enumerate(STACK) if s[0] == g) for g in range(NG)]
G_SIZE = [2 * len(nodes) for nodes in GROUPS]
JP = 32 + JOINTS
K_DIST = 67
K_IDENT, K_SEL, K_SAME, K_BACK, K_GRP = 0, P, P + NS, P + 2 * NS, P + 2 * NS + 64
K_COLS = K_GRP + NG
VECTORS = {"rms_w": C0, "bn1": 4, "bn2": 4, "b_ih": 3, "b_hh": 3, "l2_b1": NG * C2, "b3": 1, "a3": 2, "b_se": 1}
V_AT = {k: sum(list(VECTORS.values())[:i]) for i, k in enumerate(VECTORS)}
V_COLS = sum(VECTORS.values())
LN_EPS, RMS_EPS, BN_EPS = 1e-5, 1e-6, 1e-5
CONV_CUTS = [0, 3, 6, 9, 12, 15, 17]


def build(nc, x, adj, eps0, w1, b1, w2, b2, w_seT, conv1T, conv2T, bn2, w_msgT, b_msg, w_ihT, w_hhT,
          l2_w1, l2_w2, l2_b2, fusion, w3, w3T, b3, ab3, consts, vectors, out):
    with ExitStack() as ctx:
        def sb(name, shape, dt=F32):
            return ctx.enter_context(nc.sbuf_tensor(name, shape, dt))

        def sem(name):
            return ctx.enter_context(nc.semaphore(name))

        def pair_of(name, shape):
            return sb(name + "_hi", shape, F32R), sb(name + "_lo", shape, F32R)

        x_all = sb("x_all", [P, PAIRS * W])
        adjT_all = sb("adjT_all", [P, RING * 2 * W])

        kst = sb("kst", [P, K_COLS])
        ident, sel = kst[:, K_IDENT:K_IDENT + P], kst[0:JP, K_SEL:K_SEL + NS]
        same = kst[0:NS, K_SAME:K_SAME + NS]
        grp = kst[0:NS, K_GRP:K_GRP + NG]
        identr = sb("identr", [P, P], F32R)
        eps_c = sb("eps_c", [P, 1])
        epsI = sb("epsI", [P, P])
        w1_hi, w1_lo = pair_of("w1", [P, HID0])
        w2_s = sb("w2_s", [P, C0, D])
        b1_r = sb("b1_r", [P, HID0])
        b2_r = sb("b2_r", [P, D])
        vec = sb("vec", [P, V_COLS])

        def vector(name):
            return vec[:, V_AT[name]:V_AT[name] + VECTORS[name]]

        rmsw_c, bn1_c, bn2_c, bih_c, bhh_c = (vector(n) for n in ("rms_w", "bn1", "bn2", "b_ih", "b_hh"))
        vb1_c = vector("l2_b1").rearrange("p (g c) -> p g c", g=NG)
        b3_c, a3_c, bse_c = vector("b3"), vector("a3"), vector("b_se")
        c1_hi, c1_lo = pair_of("c1", [P, D])
        c2_hi, c2_lo = pair_of("c2", [P, TAPS * D])
        stage = sb("stage", [P, TAPS * D])
        bn2_r = sb("bn2_r", [P, 2, D])
        bnt = sb("bnt", [P, 2, D])
        s1_c, o1_c, s2_c, o2_c = (sb(n, [P, 1]) for n in ("s1_c", "o1_c", "s2_c", "o2_c"))
        bnw = sb("bnw", [P, 4])
        wse_raw = sb("wse_raw", [P, P])
        se_hi, se_lo = pair_of("se", [P, P])
        msg_hi, msg_lo = pair_of("wmsg", [P, D])
        bmsg_r = sb("bmsg_r", [P, D])
        ih_hi, ih_lo = pair_of("ih", [P, 2, 3 * D])
        hh_hi, hh_lo = pair_of("hh", [P, 3 * D])
        brz_c, bhn_c = sb("brz_c", [P, 2]), sb("bhn_c", [P, 1])
        v1_s = sb("v1_s", [P, NG, HID2])
        v2_s = sb("v2_s", [P, NG, C2, D])
        hb_m = sb("hb_m", [P, C2, NS])
        zb_m = sb("zb_m", [NS, D])
        fw = sb("fw", [P, NG])
        fwm, fws, nw_row = sb("fwm", [P, 1]), sb("fws", [P, 1]), sb("nw_row", [P, 1])
        fwe = sb("fwe", [P, NG])
        w3_raw = sb("w3_raw", [P, D])
        w3x = sb("w3x", [P, D + 1])
        b3_r, b3rep = sb("b3_r", [P, D]), sb("b3rep", [P, P])
        a12_c, ab_c, v1col = sb("a12_c", [P, 1]), sb("ab_c", [P, 1]), sb("v1col", [P, 1])
        e_rep = sb("e_rep", [P, P])
        fconst = sb("fconst", [P, 1])
        mhalf = sb("mhalf", [P, D])
        ones = sb("ones", [P, P])
        epsln, epsrms = sb("epsln", [P, Q]), sb("epsrms", [P, Q])
        tick = sb("tick", [P, 8])

        adj_s = sb("adj_s", [P, Q, NODES])
        adjE = sb("adjE", [P, Q, P])
        ln_st = {k: sb("st" + k, [P, Q, 6]) for k in "1234"}
        ln_mv = {k: sb("mv" + k, [P, Q, 2]) for k in "1234"}
        ln_ve = {k: sb("ve" + k, [P, Q]) for k in "1234"}
        ln_rs = {k: sb("rs" + k, [P, Q]) for k in "1234"}
        h1n, h1 = sb("h1n", [P, W]), sb("h1", [P, W])
        ag_hi, ag_lo = pair_of("ag", [P, W])
        hb = stage[:, 0:Q * HID0].rearrange("p (q h) -> p q h", q=Q)
        hsq = sb("hsq", [P, HID0])
        ssq, sve, srs = sb("ssq", [P, Q]), sb("sve", [P, Q]), sb("srs", [P, Q])
        sT = sb("sT", [P, C0, W])
        xn2 = sb("xn2", [P, W])
        h2_hi, h2_lo = pair_of("h2", [P, W])
        y1_hi, y1_lo = pair_of("y1", [P, 2, PADW])
        y1_full = sb("y1_full", [P, W])
        dl, dr = sb("dl", [P, W]), sb("dr", [P, W])
        ex1 = sb("ex1", [P, 2, W])
        msg_t, msg = sb("msg_t", [P, W]), sb("msg", [P, W])
        nm_hi, nm_lo = pair_of("nm", [P, W])
        xc_hi, xc_lo = pair_of("xc", [P, W])
        xc_full = sb("xc_full", [P, W])
        tr, tz, gh, gm, gn = (sb(n, [P, W]) for n in ("tr", "tz", "gh", "gm", "gn"))
        gd, go = sb("gd", [P, W]), sb("go", [P, W])
        jadj = sb("jadj", [P, P])
        jq = sb("jq", [P, NS])
        nmat, nsc, nT = sb("nmat", [P, NS]), sb("nsc", [P, NS]), sb("nT", [P, NS])
        deg, isz, dsafe, dpow, dinv = (sb(n, [P, 1]) for n in ("deg", "isz", "dsafe", "dpow", "dinv"))
        xj = sb("xj", [P, D])
        xs, t1, hid = sb("xs", [P, D]), sb("t1", [P, NS]), sb("hid", [P, C2, NS])
        hidr = sb("hidr", [P, C2, NS])
        yT, ys, zb, zr = sb("yT", [P, NS]), sb("ys", [P, D]), sb("zb", [P, D]), sb("zr", [P, D])
        xn4, h4T = sb("xn4", [P, W]), sb("h4T", [P, W])
        hx = sb("hx", [P, Q, D + 1])
        fcol = sb("fcol", [P, Q])
        ex3 = sb("ex3", [P, 2, W])
        rec = sb("rec", [P, Q])

        pA = [ctx.enter_context(nc.psum_tensor(f"pA{k}", [P, W], F32)) for k in range(2)]
        pB = [ctx.enter_context(nc.psum_tensor(f"pB{k}", [P, W], F32)) for k in range(3)]
        pC = [ctx.enter_context(nc.psum_tensor(f"pC{k}", [P, W], F32)) for k in range(3)]

        names = """adj_loaded jadj_loaded x_loaded stored adj_transposed adjT adjE
            stats1 mean1 ve1 rstd1 xn1 h1 agg_mm agg_hi agg_lo w1_mm hb hsq sve srs u0 u_tr sT w2_mm x_b2 x1
            stats2 mean2 ve2 rstd2 xn2 h2_tr h2_hi h2_lo conv1_mm y1_hi y1_full y1_lo se_mm dl dr dist_mm ex1 amask1
            msg_mm msg_t msg nmp_mm nm_hi nm_lo conv2_mm xc_hi xc_full xc_lo r_mm tr ghn_mm gh gm1 gin_mm gm gn
            z_mm tz gd1 gd ge go go_tr x2
            jq_mm jq n0_mm nmask nmat dgz dsf dpw dinv nsc n_tr nT stats3 mean3 ve3 rstd3 xn3 xj xs_mm xs t1_mm t1
            hid_mm hid hidr y_mm yT y_tr ys z2_mm zb zr fus_mm x3
            stats4 mean4 ve4 rstd4 xn4 h4_tr h4T l3_mm fcol e_mm ex3 u3 u3_mm rec x4""".split()
        done = {n: sem(n) for n in names}
        loaded = sem("weights_loaded")
        prep_v, prep_s, prep_g, prep_t = sem("prep_v"), sem("prep_s"), sem("prep_g"), sem("prep_t")
        pool_ready = sem("pool_ready")
        weights = []

        def bc(src, n=P):
            return src.rearrange("(a c) -> a c", a=1).broadcast_to([n, src.shape[0]])

        weights += [(kst[:], consts), (vec[:], vectors), (eps_c[:], bc(eps0)), (b1_r[:], bc(b1)), (b2_r[:], bc(b2)),
                    (w2_s[:], w2.rearrange("(c p) d -> p c d", p=P)), (wse_raw[:], w_seT),
                    (bn2_r[:, 0, :], bc(bn2[0])), (bn2_r[:, 1, :], bc(bn2[1])), (bmsg_r[:], bc(b_msg)),
                    (v1_s[:], l2_w1.rearrange("g d h -> d g h")), (v2_s[:], l2_w2.rearrange("g (c p) d -> p g c d", p=P)),
                    (fw[:], bc(fusion)), (w3_raw[:], w3), (w3x[:, 0:D], w3T), (b3_r[:], bc(b3)), (ab_c[:], bc(ab3))]
        weights += [(zb_m[G_START[g]:G_START[g] + G_SIZE[g], :], bc(l2_b2[g], G_SIZE[g])) for g in range(NG)]
        splits = [(w1, w1_hi, w1_lo, HID0), (conv1T, c1_hi, c1_lo, D), (w_msgT, msg_hi, msg_lo, D),
                  (w_hhT, hh_hi, hh_lo, 3 * D), (w_ihT, ih_hi, ih_lo, 6 * D)]
        ST_AT = [0, 512, 640, 768, 1152]
        assert ST_AT[-1] + 6 * D <= TAPS * D
        split_in, conv2_in = sem("split_in"), sem("conv2_in")
        stage_free = sem("stage_free")
        link_sem, fw_ready, fw_exp, pool_mem = sem("link"), sem("fw_ready"), sem("fw_exp"), sem("pool_mem")

        def x_tile(p, q):
            return x_all[:, bass.ds(p * W + q * P, P)] if not isinstance(p, int) else x_all[:, p * W + q * P:p * W + q * P + P]

        def x_pair(p):
            return x_all[:, bass.ds(p * W, W)] if not isinstance(p, int) else x_all[:, p * W:p * W + W]

        def adjT(p, g, at=0, n=W):
            s = (p % RING) * (2 * W) + (g * W + at)
            return adjT_all[:, bass.ds(s, n)] if not isinstance(p, int) else adjT_all[:, s:s + n]

        def turns(eng, turn):
            turn(0, 0, None, None)
            turn(1, 1, 0, None)
            turn(2, 2, 1, 0)
            with eng.Fori(3, PAIRS) as t:
                turn(t, t, t - 1, t - 2)
            turn(PAIRS, None, PAIRS - 1, PAIRS - 2)
            turn(PAIRS + 1, None, None, PAIRS - 1)

        def before(eng, name, p, per=1):
            if not (isinstance(p, int) and p == 0):
                eng.wait_ge(done[name], p * per)

        block = ctx.enter_context(nc.Block())

        @block.sync
        def _(sp):
            for (src, _, _, n), at in zip(splits, ST_AT):
                if len(src.shape) == 2 and src.shape[0] == 2 * P:
                    sp.dma_start(stage[:, at:at + n].rearrange("p (k n) -> p k n", k=2),
                                 src.rearrange("(k p) n -> p k n", p=P)).then_inc(split_in, 16)
                else:
                    sp.dma_start(stage[:, at:at + n], src).then_inc(split_in, 16)
            sp.dma_start(x_all[:, 0:W].rearrange("p (q d) -> p q d", d=D),
                         x[0:2].rearrange("b (t p) d -> p (b t) d", p=P)).then_inc(done["x_loaded"], 16)
            sp.dma_start(adj_s[:], adj[0:2].rearrange("b (t p) m -> p (b t) m", p=P)).then_inc(done["adj_loaded"], 16)
            for dst, src in weights:
                sp.dma_start(dst, src).then_inc(loaded, 16)
            sp.wait_ge(stage_free, 1)
            sp.dma_start(stage[:], conv2T).then_inc(conv2_in, 16)

            def load_x(p):
                before(sp, "stats1", p)
                sp.dma_start(x_all[:, bass.ds(p * W, W)].rearrange("p (q d) -> p q d", d=D),
                             x[bass.ds(p * 2, 2)].rearrange("b (t p) d -> p (b t) d", p=P)
                             ).then_inc(done["x_loaded"], 16)

            def load_adj(p):
                before(sp, "adj_transposed", p)
                sp.dma_start(adj_s[:], adj[bass.ds(p * 2, 2)].rearrange("b (t p) m -> p (b t) m", p=P)
                             ).then_inc(done["adj_loaded"], 16)

            def load_joints(p):
                before(sp, "jq_mm", p)
                for a in range(2):
                    sp.dma_start(jadj[32 * a:32 * a + JOINTS, 32 * a:32 * a + JOINTS],
                                 adj[bass.ds(p * 2 + a, 1), 0:JOINTS, 0:JOINTS].rearrange("b n m -> (b n) m")
                                 ).then_inc(done["jadj_loaded"], 16)

            def store(p):
                sp.wait_ge(done["x4"], p + 1)
                src = x_all[:, bass.ds(p * W, W)]
                sp.dma_start(out[bass.ds(p * 2, 2)].rearrange("b (t p) d -> p (b t) d", p=P),
                             src.rearrange("p (q d) -> p q d", d=D)).then_inc(done["stored"], 16)

            sp.wait_ge(pool_ready, 1)
            load_joints(0)
            load_x(1)
            load_adj(1)
            load_x(2)
            load_adj(2)
            load_joints(1)
            load_x(3)
            load_adj(3)
            load_joints(2)
            with sp.Fori(4, PAIRS) as t:
                load_x(t)
                load_adj(t)
                load_joints(t - 1)
                store(t - 4)
            load_joints(PAIRS - 1)
            for p in range(PAIRS - 4, PAIRS):
                store(p)
            sp.wait_ge(done["stored"], 16 * PAIRS)

        @block.tensor
        def _(pe):
            mm = nc.tensor.matmul

            def three(o, w_hi, w_lo, m_hi, m_lo, start, stop):
                mm(o, w_hi, m_hi, start=start, stop=False)
                mm(o, w_hi, m_lo, start=False, stop=False)
                return mm(o, w_lo, m_hi, start=False, stop=stop)

            pe.wait_ge(loaded, 16 * len(weights))
            mm(pC[0][:, 0:2], w3_raw[:], a3_c[:], start=True, stop=True)
            pe.wait_ge(prep_g, 1)
            mm(pC[0][:, 2:3], b3rep[:], a12_c[:], start=True, stop=True).then_inc(prep_t, 1)
            pe.wait_ge(prep_v, 1)
            pe.wait_ge(prep_s, 1)

            def adj_transposes(p):
                pe.wait_ge(done["adj_loaded"], (p + 1) * 16)
                for g in range(2):
                    if g == 0:
                        before(pe, "sT", p, C0)
                    else:
                        before(pe, "x1", p)
                    for mt in range(TILES):
                        for nt in range(TILES):
                            o = mt * NODES + nt * P
                            i = nc.tensor.transpose(pA[g][:, o:o + P], adj_s[:, g * TILES + nt, mt * P:mt * P + P], ident)
                i.then_inc(done["adj_transposed"], 1)

            def aggregate(p):
                pe.wait_ge(done["adjT"], 2 * (p + 1))
                pe.wait_ge(done["adjE"], p + 1)
                pe.wait_ge(done["h1"], p + 1)
                for g in range(2):
                    for nt in range(TILES):
                        o = pA[0][:, g * NODES + nt * P:g * NODES + nt * P + P]
                        for mt in range(TILES):
                            q = g * TILES + mt
                            rhs = adjE[:, q, :] if mt == nt else adjT(p, g, mt * NODES + nt * P, P)
                            i = mm(o, h1[:, q * P:q * P + P], rhs, start=(mt == 0), stop=(mt == TILES - 1))
                i.then_inc(done["agg_mm"], 1)

            def hidden0(p):
                pe.wait_ge(done["agg_hi"], p + 1)
                pe.wait_ge(done["agg_lo"], p + 1)
                for q in range(Q):
                    if q >= 2:
                        pe.wait_ge(done["hb"], Q * p + q - 1)
                    t = slice(q * P, q * P + P)
                    three(pA[1 - q % 2][:], ag_hi[:, t], ag_lo[:, t], w1_hi[:], w1_lo[:], True, True
                          ).then_inc(done["w1_mm"], 1)

            def hidden0_transposes(p):
                pe.wait_ge(done["hb"], Q * (p + 1))
                pe.wait_ge(done["u0"], p + 1)
                for c in range(C0):
                    if c >= 2:
                        pe.wait_ge(done["sT"], C0 * p + c - 1)
                    for q in range(Q):
                        i = nc.tensor.transpose(pA[1 - c % 2][:, q * P:q * P + P], hb[:, q, c * P:c * P + P], ident)
                    i.then_inc(done["u_tr"], 1)

            def output0(p):
                pe.wait_ge(done["sT"], C0 * (p + 1))
                for q in range(Q):
                    for c in range(C0):
                        i = mm(pA[1][:, q * D:q * D + D], sT[:, c, q * P:q * P + P], w2_s[:, c, :],
                               start=(c == 0), stop=(c == C0 - 1))
                i.then_inc(done["w2_mm"], 1)

            def h2_transposes(p):
                pe.wait_ge(done["xn2"], p + 1)
                before(pe, "x2", p)
                for q in range(Q):
                    i = nc.tensor.transpose(pB[1][:, q * P:q * P + P], xn2[:, q * P:q * P + P], ident)
                i.then_inc(done["h2_tr"], 1)

            def project(p):
                pe.wait_ge(done["h2_hi"], p + 1)
                pe.wait_ge(done["h2_lo"], p + 1)
                before(pe, "gm", p)
                three(pB[2][:], c1_hi[:], c1_lo[:], h2_hi[:], h2_lo[:], True, True).then_inc(done["conv1_mm"], 1)
                three(pB[1][:], se_hi[:], se_lo[:], h2_hi[:], h2_lo[:], True, True).then_inc(done["se_mm"], 1)
                pe.wait_ge(done["y1_hi"], p + 1)
                pe.wait_ge(done["y1_full"], p + 1)
                for q in range(Q):
                    t = slice(q * P, q * P + P)
                    i = three(pB[2][:, q * D:q * D + D], h2_hi[:, t], h2_lo[:, t], msg_hi[:], msg_lo[:], True, True)
                i.then_inc(done["msg_mm"], 1)

            def distances(p):
                pe.wait_ge(done["dl"], p + 1)
                pe.wait_ge(done["dr"], p + 1)
                pe.wait_ge(done["msg_t"], p + 1)
                for g in range(2):
                    for mt in range(TILES):
                        m = g * NODES + mt * P
                        i = mm(pB[1 + g][:, mt * NODES:(mt + 1) * NODES], dl[0:K_DIST, m:m + P],
                               dr[0:K_DIST, g * NODES:(g + 1) * NODES], start=True, stop=True)
                    i.then_inc(done["dist_mm"], 1)

            def conv2(p, part):
                if part == 0:
                    pe.wait_ge(done["y1_hi"], p + 1)
                    pe.wait_ge(done["y1_lo"], p + 1)
                    before(pe, "tz", p)
                for k in range(CONV_CUTS[part], CONV_CUTS[part + 1]):
                    w = slice(k * D, k * D + D)
                    three(pB[0][:], c2_hi[:, w], c2_lo[:, w], y1_hi[:, :, k:k + NODES], y1_lo[:, :, k:k + NODES],
                          k == 0, False)
                if part == len(CONV_CUTS) - 2:
                    mm(pB[0][:], identr[:], h2_hi[:], start=False, stop=False)
                    mm(pB[0][:], identr[:], h2_lo[:], start=False, stop=True).then_inc(done["conv2_mm"], 1)

            def messages(p):
                pe.wait_ge(done["msg"], p + 1)
                pe.wait_ge(done["amask1"], 2 * (p + 1))
                for g in range(2):
                    for mt in range(TILES):
                        q = g * TILES + mt
                        i = mm(pB[1][:, g * NODES:(g + 1) * NODES], msg[:, q * D:q * D + D],
                               ex1[:, g, mt * NODES:(mt + 1) * NODES], start=(mt == 0), stop=(mt == TILES - 1))
                i.then_inc(done["nmp_mm"], 1)

            def gate(o, j, from_x, from_h, name):
                w = slice(j * D, j * D + D)
                if from_h:
                    i = three(o, hh_hi[:, w], hh_lo[:, w], h2_hi[:], h2_lo[:], True, not from_x)
                if from_x:
                    three(o, ih_hi[:, 1, w], ih_lo[:, 1, w], nm_hi[:], nm_lo[:], not from_h, False)
                    i = three(o, ih_hi[:, 0, w], ih_lo[:, 0, w], xc_hi[:], xc_lo[:], False, True)
                i.then_inc(done[name], 1)

            def gate_hn(p):
                pe.wait_ge(done["nm_hi"], p + 1)
                pe.wait_ge(done["nm_lo"], p + 1)
                gate(pB[1][:], 2, False, True, "ghn_mm")

            def gate_r(p):
                pe.wait_ge(done["ex1"], 2 * (p + 1))
                pe.wait_ge(done["xc_hi"], p + 1)
                pe.wait_ge(done["xc_lo"], p + 1)
                gate(pB[2][:], 0, True, True, "r_mm")

            def gate_in(p):
                pe.wait_ge(done["tr"], p + 1)
                gate(pB[2][:], 2, True, False, "gin_mm")

            def gate_z(p):
                pe.wait_ge(done["xc_full"], p + 1)
                gate(pB[0][:], 1, True, True, "z_mm")

            def back_transposes(p):
                pe.wait_ge(done["go"], p + 1)
                pe.wait_ge(done["gh"], p + 1)
                for q in range(Q):
                    i = nc.tensor.transpose(pB[1][:, q * P:q * P + P], go[:, q * P:q * P + P], ident)
                i.then_inc(done["go_tr"], 1)

            def joints_left(p):
                pe.wait_ge(done["jadj_loaded"], (p + 1) * 32)
                before(pe, "rec", p)
                before(pe, "x4", p)
                mm(pC[0][:, 0:NS], jadj[0:JP, :], sel, start=True, stop=True).then_inc(done["jq_mm"], 1)

            def joints_right(p):
                pe.wait_ge(done["jq"], p + 1)
                before(pe, "ex3", p, Q)
                mm(pC[1][0:NS, 0:NS], jq[0:JP, :], sel, start=True, stop=True).then_inc(done["n0_mm"], 1)
                pe.wait_ge(done["xj"], p + 1)
                before(pe, "x4", p)
                mm(pC[2][0:NS, 0:D], sel, xj[0:JP, :], start=True, stop=True).then_inc(done["xs_mm"], 1)

            def norm_transpose(p):
                pe.wait_ge(done["nsc"], p + 1)
                nc.tensor.transpose(pC[0][0:NS, 0:NS], nsc[0:NS, :], ident[0:NS, 0:NS]).then_inc(done["n_tr"], 1)

            def spread1(p):
                pe.wait_ge(done["nT"], p + 1)
                pe.wait_ge(done["xs"], p + 1)
                pe.wait_ge(done["nmask"], p + 1)
                mm(pC[1][:, 0:NS], xs[0:NS, :], nT[0:NS, :], start=True, stop=True).then_inc(done["t1_mm"], 1)

            def hidden2(p):
                pe.wait_ge(done["t1"], p + 1)
                for c in range(C2):
                    for g in range(NG):
                        a, n = G_START[g], G_SIZE[g]
                        i = mm(pC[2][:, c * NS + a:c * NS + a + n], v1_s[:, g, c * P:c * P + P], t1[:, a:a + n],
                               start=True, stop=True)
                i.then_inc(done["hid_mm"], 1)

            def output2(p):
                pe.wait_ge(done["hidr"], p + 1)
                for g in range(NG):
                    a, n = G_START[g], G_SIZE[g]
                    for c in range(C2):
                        i = mm(pC[0][:, a:a + n], v2_s[:, g, c, :], hidr[:, c, a:a + n], start=(c == 0), stop=(c == C2 - 1))
                i.then_inc(done["y_mm"], 1)

            def y_transpose(p):
                pe.wait_ge(done["yT"], p + 1)
                nc.tensor.transpose(pC[1][0:NS, 0:P], yT[:, :], ident).then_inc(done["y_tr"], 1)

            def spread2(p):
                pe.wait_ge(done["ys"], p + 1)
                mm(pC[2][0:NS, 0:D], nT[0:NS, :], ys[0:NS, :], start=True, stop=True).then_inc(done["z2_mm"], 1)

            def fuse(p):
                pe.wait_ge(done["zr"], p + 1)
                for a in range(2):
                    back = kst[0:NS, K_BACK + 32 * a:K_BACK + 32 * a + 32]
                    i = mm(pC[0][0:32, a * D:a * D + D], back, zr[0:NS, :], start=True, stop=True)
                i.then_inc(done["fus_mm"], 1)

            def h4_transposes(p):
                pe.wait_ge(done["xn4"], p + 1)
                for q in range(Q):
                    i = nc.tensor.transpose(pC[1][:, q * P:q * P + P], xn4[:, q * P:q * P + P], ident)
                i.then_inc(done["h4_tr"], 1)

            def project3(p):
                pe.wait_ge(done["h4T"], p + 1)
                for g in range(2):
                    for mt in range(TILES):
                        m = g * NODES + mt * P
                        i = mm(pC[2 * g][:, mt * (D + 1):(mt + 1) * (D + 1)], h4T[:, m:m + P], w3x[:],
                               start=True, stop=True)
                i.then_inc(done["l3_mm"], 1)
                mm(pC[1][:], e_rep[:], h4T[:], start=True, stop=True).then_inc(done["e_mm"], 1)

            def attend(p):
                pe.wait_ge(done["fcol"], p + 1)
                pe.wait_ge(done["u3"], 2 * (p + 1))
                for g in range(2):
                    for nt in range(TILES):
                        for mt in range(TILES):
                            m = mt * NODES + nt * P
                            i = mm(pC[2 * g][:, nt * (D + 1):(nt + 1) * (D + 1)], ex3[:, g, m:m + P],
                                   hx[:, g * TILES + mt, :], start=(mt == 0), stop=(mt == TILES - 1))
                i.then_inc(done["u3_mm"], 1)

            def turn(t, a, b, c):
                def A(step, *args):
                    if a is not None:
                        step(a, *args)

                def B(step, *args):
                    if b is not None:
                        step(b, *args)

                def C(step, *args):
                    if c is not None:
                        step(c, *args)

                A(adj_transposes)
                B(h2_transposes)
                C(joints_left)
                A(aggregate)
                B(project)
                C(joints_right)
                B(conv2, 0)
                A(hidden0)
                B(distances)
                C(norm_transpose)
                B(conv2, 1)
                C(spread1)
                B(conv2, 2)
                C(hidden2)
                A(hidden0_transposes)
                B(messages)
                C(output2)
                B(conv2, 3)
                C(y_transpose)
                B(conv2, 4)
                C(spread2)
                B(gate_hn)
                C(fuse)
                B(conv2, 5)
                A(output0)
                B(gate_r)
                C(h4_transposes)
                B(gate_in)
                C(project3)
                B(gate_z)
                C(attend)
                B(back_transposes)

            turns(pe, turn)

        @block.vector
        def _(dve):
            v = nc.vector
            link_at = [0]
            chain = link_sem

            def link(ins):
                link_at[0] += 1
                ins.then_inc(chain, 1)
                dve.wait_ge(chain, link_at[0])

            dve.wait_ge(split_in, 16 * len(splits))
            for (src, hi, lo, n), at in zip(splits, ST_AT):
                h2 = hi[:] if n != 6 * D else hi[:].rearrange("p k n -> p (k n)")
                l2 = lo[:] if n != 6 * D else lo[:].rearrange("p k n -> p (k n)")
                link(v.tensor_copy(h2, stage[:, at:at + n]))
                last = v.tensor_tensor(l2, stage[:, at:at + n], h2.bitcast(F32), ALU.subtract)
            last.then_inc(stage_free, 1)
            dve.wait_ge(loaded, 16 * len(weights))
            dve.wait_ge(pool_ready, 2)
            v.tensor_copy(identr[:], ident)
            v.tensor_scalar(epsI[:], ident, eps_c[:, 0:1], None, ALU.mult)
            for k, (bn, s, o) in enumerate(((bn1_c, s1_c, o1_c), (bn2_c, s2_c, o2_c))):
                link(v.tensor_tensor(s[:], bn[:, 0:1], bnw[:, k:k + 1], ALU.mult))
                link(v.tensor_tensor(bnw[:, k + 2:k + 3], bn[:, 2:3], s[:], ALU.mult))
                link(v.tensor_tensor(o[:], bn[:, 1:2], bnw[:, k + 2:k + 3], ALU.subtract))
            link(v.tensor_tensor(bnt[:, 0, :], bn2_r[:, 0, :], bnt[:, 1, :], ALU.mult))
            ROOT2 = 2.0 ** 0.5
            link(v.tensor_scalar(wse_raw[:], wse_raw[:], ROOT2, None, ALU.mult))
            link(v.tensor_scalar(bse_c[:], bse_c[:], ROOT2, None, ALU.mult))
            link(v.tensor_copy(se_hi[:], wse_raw[:]))
            v.tensor_tensor(se_lo[:], wse_raw[:], se_hi[:].bitcast(F32), ALU.subtract)
            link(v.tensor_tensor(brz_c[:], bih_c[:, 0:2], bhh_c[:, 0:2], ALU.add))
            v.tensor_scalar(brz_c[:], brz_c[:], 0.5, None, ALU.mult)
            v.tensor_scalar(bhn_c[:], bhh_c[:, 2:3], 0.5, None, ALU.mult)
            for g in range(NG):
                for c in range(C2):
                    a, n = G_START[g], G_SIZE[g]
                    v.tensor_scalar(hb_m[:, c, a:a + n], ones[:, 0:n], vb1_c[:, g, c:c + 1], None, ALU.mult)
            link(v.tensor_reduce(fwm[:], fw[:], AX.X, ALU.max))
            link(v.tensor_scalar(fw[:], fw[:], fwm[:, 0:1], None, ALU.subtract))
            v.tensor_copy(fwe[:], fw[:]).then_inc(fw_ready, 1)
            dve.wait_ge(fw_exp, 1)
            link(v.tensor_reduce(fws[:], fw[:], AX.X, ALU.add))
            link(v.reciprocal(fws[:], fws[:]))
            link(v.tensor_scalar(fwe[:], fw[:], fws[:, 0:1], None, ALU.mult))
            link(v.tensor_tensor(fwe[0:NS, :], fwe[0:NS, :], grp, ALU.mult))
            v.tensor_reduce(nw_row[0:NS, :], fwe[0:NS, :], AX.X, ALU.add)
            dve.wait_ge(prep_t, 1)
            v.tensor_copy(w3x[:, D:D + 1], pC[0][:, 1:2])
            link(v.tensor_copy(v1col[:], pC[0][:, 0:1]))
            v.tensor_scalar(e_rep[:], ones[:], v1col[:, 0:1], None, ALU.mult)
            v.tensor_tensor(fconst[:], pC[0][:, 2:3], ab_c[:], ALU.add)
            dve.wait_ge(conv2_in, 16)
            s2_row = bnt[:, 0, :].rearrange("p (a d) -> p a d", a=1).broadcast_to([P, TAPS, D])
            link(v.tensor_tensor(stage[:].rearrange("p (k d) -> p k d", d=D), stage[:].rearrange("p (k d) -> p k d", d=D),
                                 s2_row, ALU.mult))
            link(v.tensor_copy(c2_hi[:], stage[:]))
            link(v.tensor_tensor(c2_lo[:], stage[:], c2_hi[:].bitcast(F32), ALU.subtract))
            v.tensor_copy(bnw[:, 0:1], bnw[:, 1:2]).then_inc(prep_v, 1)

            def carry_wait(n):
                v.memset(tick[:, n:n + 1], 0.0)

            def norm_stats(k, tiles, n=P):
                carry_wait(2 * int(k) - 2)
                for q, tile in tiles:
                    i = v.bn_stats(ln_st[k][0:n, q, :], tile)
                i.then_inc(done["stats" + k], 1)

            def norm_mean(k, p, qs, n=P):
                dve.wait_ge(done["stats" + k], p + 1)
                carry_wait(2 * int(k) - 1)
                for q in qs:
                    i = v.bn_aggr(ln_mv[k][0:n, q, :], ln_st[k][0:n, q, :])
                i.then_inc(done["mean" + k], 1)

            def norm_apply(k, p, tiles, name, n=P):
                dve.wait_ge(done["rstd" + k], p + 1)
                for q, tile, dst in tiles:
                    i = v.tensor_scalar(dst, tile, ln_mv[k][0:n, q, 0:1], ln_rs[k][0:n, q:q + 1],
                                        ALU.subtract, ALU.mult)
                i.then_inc(done[name], 1)

            def norm1(p):
                dve.wait_ge(done["x_loaded"], (p + 1) * 16)
                norm_stats("1", [(q, x_tile(p, q)) for q in range(Q)])
                norm_mean("1", p, range(Q))

            def norm1_apply(p):
                norm_apply("1", p, [(q, x_tile(p, q), h1n[:, q * P:q * P + P]) for q in range(Q)], "xn1")
                dve.wait_ge(done["xn1"], p + 1)
                before(dve, "agg_mm", p)
                v.tensor_scalar(h1[:], h1n[:], 0.0, None, ALU.max).then_inc(done["h1"], 1)

            def adjT_out(p):
                dve.wait_ge(done["adj_transposed"], p + 1)
                v.tensor_copy(adjT(p, 1), pA[1][:]).then_inc(done["adjT"], 1)

            def agg_low(p):
                dve.wait_ge(done["agg_hi"], p + 1)
                before(dve, "w1_mm", p, Q)
                v.tensor_tensor(ag_lo[:], pA[0][:], ag_hi[:].bitcast(F32), ALU.subtract).then_inc(done["agg_lo"], 1)

            def hidden0_bias(p):
                before(dve, "u_tr", p, C0)
                for q in range(Q):
                    dve.wait_ge(done["w1_mm"], Q * p + q + 1)
                    v.tensor_tensor(hb[:, q, :], pA[1 - q % 2][:], b1_r[:], ALU.add).then_inc(done["hb"], 1)

            def hidden0_scale(p):
                dve.wait_ge(done["srs"], p + 1)
                for q in range(Q):
                    i = v.tensor_scalar(hb[:, q, :], hb[:, q, :], srs[:, q:q + 1], HID0 ** 0.5, ALU.mult, ALU.mult)
                i.then_inc(done["u0"], 1)

            def residual0(p):
                dve.wait_ge(done["w2_mm"], p + 1)
                dve.wait_ge(done["x_b2"], p + 1)
                v.tensor_tensor(x_pair(p), pA[1][:], x_pair(p), ALU.add).then_inc(done["x1"], 1)

            def norm2(p):
                dve.wait_ge(done["x1"], p + 1)
                norm_stats("2", [(q, x_tile(p, q)) for q in range(Q)])
                norm_mean("2", p, range(Q))

            def norm2_apply(p):
                before(dve, "h2_tr", p)
                norm_apply("2", p, [(q, x_tile(p, q), xn2[:, q * P:q * P + P]) for q in range(Q)], "xn2")

            def h2_low(p):
                dve.wait_ge(done["h2_hi"], p + 1)
                v.scalar_tensor_tensor(out=h2_lo[:], in0=pB[1][:], scalar=0.0, in1=h2_hi[:].bitcast(F32),
                                       op0=ALU.max, op1=ALU.subtract).then_inc(done["h2_lo"], 1)

            def dist_right(p):
                dve.wait_ge(done["se_mm"], p + 1)
                before(dve, "dist_mm", p, 2)
                v.tensor_scalar(dr[0:3, :], pB[1][0:3, :], bse_c[0:3, 0:1], None, ALU.add)
                v.tensor_scalar(dl[0:3, :], pB[1][0:3, :], bse_c[0:3, 0:1], None, ALU.add).then_inc(done["dr"], 1)

            def msg_bias(p):
                dve.wait_ge(done["msg_mm"], p + 1)
                before(dve, "nmp_mm", p)
                row = bmsg_r[:].rearrange("p (a d) -> p a d", a=1).broadcast_to([P, Q, D])
                v.tensor_tensor(msg_t[:].rearrange("p (q d) -> p q d", d=D), pB[2][:].rearrange("p (q d) -> p q d", d=D),
                                row, ALU.add).then_inc(done["msg_t"], 1)
                dve.wait_ge(done["msg_t"], p + 1)
                v.tensor_scalar(msg[:], msg_t[:], 0.0, None, ALU.max).then_inc(done["msg"], 1)

            def mask1(p):
                for g in range(2):
                    dve.wait_ge(done["ex1"], 2 * p + g + 1)
                    v.tensor_tensor(ex1[:, g, :], ex1[:, g, :], adjT(p, g), ALU.mult).then_inc(done["amask1"], 1)

            def nmp_low(p):
                dve.wait_ge(done["nm_hi"], p + 1)
                v.tensor_tensor(nm_lo[:], pB[1][:], nm_hi[:].bitcast(F32), ALU.subtract).then_inc(done["nm_lo"], 1)

            def conv_full(p):
                dve.wait_ge(done["xc_hi"], p + 1)
                before(dve, "xc_lo", p)
                v.tensor_scalar(xc_full[:], pB[0][:], o2_c[:, 0:1], 0.0, ALU.add, ALU.max).then_inc(done["xc_full"], 1)

            def gate_mix(p):
                dve.wait_ge(done["tr"], p + 1)
                dve.wait_ge(done["gh"], p + 1)
                before(dve, "gn", p)
                v.scalar_tensor_tensor(out=gm[:], in0=tr[:], scalar=1.0, in1=gh[:], op0=ALU.add,
                                       op1=ALU.mult).then_inc(done["gm1"], 1)
                dve.wait_ge(done["gm1"], p + 1)
                dve.wait_ge(done["gin_mm"], p + 1)
                v.tensor_tensor(gm[:], pB[2][:], gm[:], ALU.add).then_inc(done["gm"], 1)

            def gate_out(p):
                dve.wait_ge(done["gd"], p + 1)
                dve.wait_ge(done["tz"], p + 1)
                v.scalar_tensor_tensor(out=gd[:], in0=tz[:], scalar=1.0, in1=gd[:], op0=ALU.add,
                                       op1=ALU.mult).then_inc(done["ge"], 1)
                dve.wait_ge(done["ge"], p + 1)
                before(dve, "go_tr", p)
                v.scalar_tensor_tensor(out=go[:], in0=gd[:], scalar=0.5, in1=gn[:], op0=ALU.mult,
                                       op1=ALU.add).then_inc(done["go"], 1)

            def residual1(p):
                dve.wait_ge(done["go_tr"], p + 1)
                v.tensor_tensor(x_pair(p), pB[1][:], x_pair(p), ALU.add).then_inc(done["x2"], 1)

            def joint_tiles(p):
                return [(0, x_tile(p, 0)[0:JOINTS, :]), (2, x_tile(p, 2)[0:JOINTS, :])]

            def joints_copy(p):
                dve.wait_ge(done["jq_mm"], p + 1)
                before(dve, "n0_mm", p)
                v.tensor_copy(jq[0:JP, :], pC[0][0:JP, 0:NS]).then_inc(done["jq"], 1)

            def norm3(p):
                dve.wait_ge(done["x2"], p + 1)
                norm_stats("3", joint_tiles(p), JOINTS)
                norm_mean("3", p, (0, 2), JOINTS)

            def norm3_apply(p):
                before(dve, "xs_mm", p)
                norm_apply("3", p, [(q, x, xj[32 * (q // 2):32 * (q // 2) + JOINTS, :]) for q, x in joint_tiles(p)],
                           "xn3", JOINTS)
                dve.wait_ge(done["xn3"], p + 1)
                v.tensor_scalar(xj[0:JP, :], xj[0:JP, :], 0.0, None, ALU.max).then_inc(done["xj"], 1)

            def degrees(p):
                dve.wait_ge(done["n0_mm"], p + 1)
                v.tensor_tensor(nsc[0:NS, :], pC[1][0:NS, 0:NS], same, ALU.mult).then_inc(done["nmask"], 1)
                dve.wait_ge(done["nmask"], p + 1)
                v.tensor_tensor(nmat[0:NS, :], nsc[0:NS, :], ident[0:NS, 0:NS], ALU.add).then_inc(done["nmat"], 1)
                dve.wait_ge(done["nmat"], p + 1)
                v.tensor_reduce(deg[0:NS, :], nmat[0:NS, :], AX.X, ALU.add).then_inc(done["dgz"], 1)
                dve.wait_ge(done["dgz"], 3 * p + 1)
                v.tensor_scalar(isz[0:NS, :], deg[0:NS, :], 0.0, None, ALU.is_equal).then_inc(done["dgz"], 1)
                dve.wait_ge(done["dgz"], 3 * p + 2)
                v.tensor_tensor(dsafe[0:NS, :], deg[0:NS, :], isz[0:NS, :], ALU.add).then_inc(done["dgz"], 1)

            def norm_rows(p):
                dve.wait_ge(done["dpw"], p + 1)
                v.tensor_tensor(dinv[0:NS, :], dpow[0:NS, :], isz[0:NS, :], ALU.mult).then_inc(done["dsf"], 1)
                dve.wait_ge(done["dsf"], p + 1)
                v.tensor_tensor(dinv[0:NS, :], dpow[0:NS, :], dinv[0:NS, :], ALU.subtract).then_inc(done["dinv"], 1)
                dve.wait_ge(done["dinv"], p + 1)
                v.tensor_scalar(nsc[0:NS, :], nmat[0:NS, :], dinv[0:NS, 0:1], None, ALU.mult).then_inc(done["nsc"], 1)

            def norm_cols(p):
                dve.wait_ge(done["n_tr"], p + 1)
                before(dve, "z2_mm", p)
                v.tensor_scalar(nT[0:NS, :], pC[0][0:NS, 0:NS], dinv[0:NS, 0:1], None, ALU.mult).then_inc(done["nT"], 1)

            def stack_copy(p):
                dve.wait_ge(done["xs_mm"], p + 1)
                before(dve, "t1_mm", p)
                v.tensor_copy(xs[0:NS, :], pC[2][0:NS, 0:D]).then_inc(done["xs"], 1)

            def hid_bias(p):
                dve.wait_ge(done["hid_mm"], p + 1)
                v.tensor_tensor(hid[:], pC[2][:, 0:C2 * NS].rearrange("p (c n) -> p c n", c=C2), hb_m[:], ALU.add
                                ).then_inc(done["hid"], 1)
                dve.wait_ge(done["hid"], p + 1)
                before(dve, "y_mm", p)
                v.tensor_scalar(hidr[:], hid[:], 0.0, None, ALU.max).then_inc(done["hidr"], 1)

            def z_bias(p):
                dve.wait_ge(done["z2_mm"], p + 1)
                v.tensor_tensor(zb[0:NS, :], pC[2][0:NS, 0:D], zb_m[:], ALU.add).then_inc(done["zb"], 1)
                dve.wait_ge(done["zb"], p + 1)
                before(dve, "fus_mm", p)
                v.tensor_scalar(zr[0:NS, :], zb[0:NS, :], 0.0, nw_row[0:NS, 0:1], ALU.max, ALU.mult
                                ).then_inc(done["zr"], 1)

            def residual2(p):
                dve.wait_ge(done["fus_mm"], p + 1)
                for a, (_, x) in enumerate(joint_tiles(p)):
                    i = v.tensor_tensor(x, pC[0][0:JOINTS, a * D:a * D + D], x, ALU.add)
                i.then_inc(done["x3"], 1)

            def norm4(p):
                dve.wait_ge(done["x3"], p + 1)
                norm_stats("4", [(q, x_tile(p, q)) for q in range(Q)])
                norm_mean("4", p, range(Q))

            def norm4_apply(p):
                before(dve, "h4_tr", p)
                norm_apply("4", p, [(q, x_tile(p, q), xn4[:, q * P:q * P + P]) for q in range(Q)], "xn4")

            def h3_bias(p):
                dve.wait_ge(done["l3_mm"], p + 1)
                before(dve, "u3_mm", p)
                row = b3_r[:].rearrange("p (a d) -> p a d", a=1).broadcast_to([P, TILES, D])
                for g in range(2):
                    src = pC[2 * g][:, 0:TILES * (D + 1)].rearrange("p (q d) -> p q d", d=D + 1)
                    v.tensor_scalar(fcol[:, g * TILES:(g + 1) * TILES], src[:, :, D], fconst[:, 0:1], None, ALU.add)
                    i = v.tensor_tensor(hx[:, g * TILES:(g + 1) * TILES, 0:D], src[:, :, 0:D], row, ALU.add)
                i.then_inc(done["fcol"], 1)

            def mask3(p):
                for g in range(2):
                    dve.wait_ge(done["ex3"], Q * p + TILES * (g + 1))
                    v.tensor_tensor(ex3[:, g, :], ex3[:, g, :], adjT(p, g), ALU.mult).then_inc(done["u3"], 1)

            def attend_out(p):
                dve.wait_ge(done["u3_mm"], p + 1)
                for g in range(2):
                    src = pC[2 * g][:, 0:TILES * (D + 1)].rearrange("p (q d) -> p q d", d=D + 1)
                    i = v.reciprocal(rec[:, g * TILES:(g + 1) * TILES], src[:, :, D])
                i.then_inc(done["rec"], 1)
                dve.wait_ge(done["rec"], p + 1)
                for q in range(Q):
                    g, nt = q // TILES, q % TILES
                    i = v.scalar_tensor_tensor(out=x_tile(p, q), in0=pC[2 * g][:, nt * (D + 1):nt * (D + 1) + D],
                                               scalar=rec[:, q:q + 1], in1=x_tile(p, q), op0=ALU.mult, op1=ALU.add)
                i.then_inc(done["x4"], 1)

            def turn(t, a, b, c):
                def A(step):
                    if a is not None:
                        step(a)

                def B(step):
                    if b is not None:
                        step(b)

                def C(step):
                    if c is not None:
                        step(c)

                B(norm2)
                A(norm1)
                C(norm3)
                B(norm2_apply)
                A(norm1_apply)
                A(adjT_out)
                C(norm3_apply)
                B(h2_low)
                C(joints_copy)
                A(agg_low)
                B(dist_right)
                C(degrees)
                C(stack_copy)
                B(msg_bias)
                C(norm_rows)
                A(hidden0_bias)
                B(mask1)
                C(norm_cols)
                A(hidden0_scale)
                C(hid_bias)
                B(nmp_low)
                C(z_bias)
                C(residual2)
                C(norm4)
                B(conv_full)
                C(norm4_apply)
                A(residual0)
                B(gate_mix)
                C(h3_bias)
                C(mask3)
                B(gate_out)
                C(attend_out)
                B(residual1)

            turns(dve, turn)

        @block.scalar
        def _(act):
            s = nc.scalar.activation
            act.wait_ge(fw_ready, 1)
            s(fw[:], fwe[:], ACT.Exp).then_inc(fw_exp, 1)
            act.wait_ge(prep_v, 1)
            act.wait_ge(pool_ready, 2)
            s(ssq[:, 0:1], ones[:, 0:1], ACT.Copy).then_inc(prep_s, 1)

            def adjT_out(p):
                act.wait_ge(done["adj_transposed"], p + 1)
                s(adjT(p, 0), pA[0][:], ACT.Copy).then_inc(done["adjT"], 1)

            def agg_high(p):
                act.wait_ge(done["agg_mm"], p + 1)
                before(act, "w1_mm", p, Q)
                s(ag_hi[:], pA[0][:], ACT.Copy).then_inc(done["agg_hi"], 1)

            def squares(p):
                before(act, "sve", p)
                for q in range(Q):
                    act.wait_ge(done["hb"], Q * p + q + 1)
                    if q:
                        act.wait_ge(done["hsq"], Q * p + q)
                    s(hsq[:], hb[:, q, :], ACT.Square, accum_out=ssq[:, q:q + 1]).then_inc(done["hsq"], 1)

            def silu(p):
                before(act, "w2_mm", p)
                for c in range(C0):
                    act.wait_ge(done["u_tr"], C0 * p + c + 1)
                    s(sT[:, c, :], pA[1 - c % 2][:], ACT.Silu, scale=rmsw_c[:, c:c + 1]).then_inc(done["sT"], 1)

            def h2_high(p):
                act.wait_ge(done["h2_tr"], p + 1)
                before(act, "z_mm", p)
                before(act, "gd", p)
                s(h2_hi[:], pB[1][:], ACT.Relu).then_inc(done["h2_hi"], 1)

            def conv1_out(p):
                act.wait_ge(done["conv1_mm"], p + 1)
                before(act, "conv2_mm", p)
                before(act, "y1_lo", p)
                s(y1_hi[:, :, PAD:PAD + NODES], pB[2][:].rearrange("p (g n) -> p g n", g=2), ACT.Relu,
                  scale=s1_c[:, 0:1], bias=o1_c[:, 0:1]).then_inc(done["y1_hi"], 1)
                s(y1_full[:], pB[2][:], ACT.Relu, scale=s1_c[:, 0:1], bias=o1_c[:, 0:1]).then_inc(done["y1_full"], 1)

            def dist_squares(p):
                act.wait_ge(done["se_mm"], p + 1)
                before(act, "dist_mm", p, 2)
                s(dl[32:35, :], pB[1][32:35, :], ACT.Square, bias=bse_c[32:35, 0:1])
                s(dr[64:67, :], pB[1][64:67, :], ACT.Square, bias=bse_c[64:67, 0:1]).then_inc(done["dl"], 1)

            def exp1(p):
                before(act, "nmp_mm", p)
                for g in range(2):
                    act.wait_ge(done["dist_mm"], 2 * p + g + 1)
                    s(ex1[:, g, :], pB[1 + g][:], ACT.Exp).then_inc(done["ex1"], 1)

            def nmp_high(p):
                act.wait_ge(done["nmp_mm"], p + 1)
                before(act, "z_mm", p)
                s(nm_hi[:], pB[1][:], ACT.Copy).then_inc(done["nm_hi"], 1)

            def conv_high(p):
                act.wait_ge(done["conv2_mm"], p + 1)
                before(act, "z_mm", p)
                before(act, "xc_lo", p)
                s(xc_hi[:], pB[0][:], ACT.Relu, bias=o2_c[:, 0:1]).then_inc(done["xc_hi"], 1)

            def gate_h(p):
                act.wait_ge(done["ghn_mm"], p + 1)
                before(act, "gm1", p)
                s(gh[:], pB[1][:], ACT.Identity, scale=0.5, bias=bhn_c[:, 0:1]).then_inc(done["gh"], 1)

            def gate_r(p):
                act.wait_ge(done["r_mm"], p + 1)
                before(act, "gm1", p)
                s(tr[:], pB[2][:], ACT.Tanh, scale=0.5, bias=brz_c[:, 0:1]).then_inc(done["tr"], 1)

            def gate_n(p):
                act.wait_ge(done["gm"], p + 1)
                before(act, "go", p)
                s(gn[:], gm[:], ACT.Tanh, bias=bih_c[:, 2:3]).then_inc(done["gn"], 1)

            def gate_z(p):
                act.wait_ge(done["z_mm"], p + 1)
                before(act, "ge", p)
                s(tz[:], pB[0][:], ACT.Tanh, scale=0.5, bias=brz_c[:, 1:2]).then_inc(done["tz"], 1)

            def t1_copy(p):
                act.wait_ge(done["t1_mm"], p + 1)
                before(act, "hid_mm", p)
                s(t1[:], pC[1][:, 0:NS], ACT.Copy).then_inc(done["t1"], 1)

            def y_copy(p):
                act.wait_ge(done["y_mm"], p + 1)
                before(act, "y_tr", p)
                s(yT[:], pC[0][:, 0:NS], ACT.Copy).then_inc(done["yT"], 1)

            def ys_copy(p):
                act.wait_ge(done["y_tr"], p + 1)
                before(act, "z2_mm", p)
                s(ys[0:NS, :], pC[1][0:NS, 0:P], ACT.Copy).then_inc(done["ys"], 1)

            def h4_out(p):
                act.wait_ge(done["h4_tr"], p + 1)
                before(act, "e_mm", p)
                s(h4T[:], pC[1][:], ACT.Relu).then_inc(done["h4T"], 1)

            def exp3(p):
                act.wait_ge(done["e_mm"], p + 1)
                act.wait_ge(done["fcol"], p + 1)
                before(act, "u3_mm", p)
                for g in range(2):
                    for mt in range(TILES):
                        s(ex3[:, g, mt * NODES:(mt + 1) * NODES], pC[1][:, g * NODES:(g + 1) * NODES], ACT.Exp,
                          bias=fcol[:, g * TILES + mt:g * TILES + mt + 1]).then_inc(done["ex3"], 1)

            def turn(t, a, b, c):
                def A(step):
                    if a is not None:
                        step(a)

                def B(step):
                    if b is not None:
                        step(b)

                def C(step):
                    if c is not None:
                        step(c)

                A(adjT_out)
                B(h2_high)
                A(agg_high)
                B(conv1_out)
                B(dist_squares)
                A(squares)
                B(exp1)
                C(t1_copy)
                A(silu)
                B(nmp_high)
                C(y_copy)
                C(ys_copy)
                B(gate_h)
                B(conv_high)
                B(gate_r)
                C(h4_out)
                B(gate_n)
                C(exp3)
                B(gate_z)

            turns(act, turn)

        @block.gpsimd
        def _(pool):
            g_ = nc.gpsimd
            g_.memset(jadj[:], 0.0)
            g_.memset(xj[:], 0.0)
            g_.memset(ones[:], 1.0).then_inc(pool_mem, 1)
            pool.wait_ge(pool_mem, 1)
            g_.memset(epsln[:], LN_EPS)
            g_.memset(epsrms[:], RMS_EPS * HID0)
            g_.memset(mhalf[:], -0.5).then_inc(pool_ready, 1)
            g_.memset(y1_hi[:].bitcast(F32), 0.0)
            g_.memset(y1_lo[:].bitcast(F32), 0.0)
            g_.memset(dl[:], 0.0)
            g_.memset(dr[:], 0.0)
            g_.memset(hx[:], 1.0).then_inc(pool_mem, 1)
            pool.wait_ge(pool_mem, 2)
            g_.memset(dl[64:67, :], -0.5).then_inc(pool_mem, 1)
            pool.wait_ge(pool_mem, 3)
            g_.memset(dr[32:35, :], -0.5).then_inc(pool_mem, 1)
            pool.wait_ge(pool_mem, 4)
            pool.wait_ge(loaded, 16 * len(weights))
            g_.tensor_scalar(bnw[:, 0:1], bn1_c[:, 3:4], BN_EPS, None, ALU.add)
            g_.tensor_scalar(bnw[:, 1:2], bn2_c[:, 3:4], BN_EPS, None, ALU.add)
            g_.tensor_scalar(bnt[:, 0, :], bn2_r[:, 1, :], BN_EPS, None, ALU.add).then_inc(pool_mem, 1)
            pool.wait_ge(pool_mem, 5)
            g_.tensor_tensor(bnt[:, 1, :], bnt[:, 0, :], mhalf[:, 0:D], ALU.pow)
            g_.tensor_tensor(bnw[:, 0:2], bnw[:, 0:2], mhalf[:, 0:2], ALU.pow).then_inc(pool_ready, 1)
            g_.tensor_scalar(b3rep[:], ones[:], b3_c[:, 0:1], None, ALU.mult)
            g_.tensor_tensor(a12_c[:], a3_c[:, 0:1], a3_c[:, 1:2], ALU.add).then_inc(prep_g, 1)
            pool.wait_ge(prep_v, 1)

            def rstd(p, k):
                n = JOINTS if k == "3" else P
                qs = slice(0, Q, 2) if k == "3" else slice(0, Q)
                pool.wait_ge(done["mean" + k], p + 1)
                g_.tensor_tensor(ln_ve[k][0:n, qs], ln_mv[k][0:n, qs, 1], epsln[0:n, qs], ALU.add).then_inc(done["ve" + k], 1)
                pool.wait_ge(done["ve" + k], p + 1)
                g_.tensor_tensor(ln_rs[k][0:n, qs], ln_ve[k][0:n, qs], mhalf[0:n, qs], ALU.pow).then_inc(done["rstd" + k], 1)

            def adj_eps(p):
                pool.wait_ge(done["adjT"], 2 * (p + 1))
                before(pool, "agg_mm", p)
                for g in range(2):
                    for t in range(TILES):
                        i = g_.tensor_tensor(adjE[:, g * TILES + t, :], adjT(p, g, t * NODES + t * P, P), epsI[:], ALU.add)
                i.then_inc(done["adjE"], 1)

            def x_bias(p):
                pool.wait_ge(done["h1"], p + 1)
                row = b2_r[:].rearrange("p (a d) -> p a d", a=1).broadcast_to([P, Q, D])
                xp = x_pair(p).rearrange("p (q d) -> p q d", d=D)
                g_.tensor_tensor(xp, xp, row, ALU.add).then_inc(done["x_b2"], 1)

            def rms(p):
                pool.wait_ge(done["hsq"], Q * (p + 1))
                g_.tensor_tensor(sve[:], ssq[:], epsrms[:], ALU.add).then_inc(done["sve"], 1)
                pool.wait_ge(done["sve"], p + 1)
                g_.tensor_tensor(srs[:], sve[:], mhalf[:, 0:Q], ALU.pow).then_inc(done["srs"], 1)

            def y1_low(p):
                pool.wait_ge(done["y1_full"], p + 1)
                g_.tensor_tensor(y1_lo[:, :, PAD:PAD + NODES], y1_full[:].rearrange("p (g n) -> p g n", g=2),
                                 y1_hi[:, :, PAD:PAD + NODES].bitcast(F32), ALU.subtract).then_inc(done["y1_lo"], 1)

            def degree_root(p):
                pool.wait_ge(done["dgz"], 3 * (p + 1))
                g_.tensor_tensor(dpow[0:NS, :], dsafe[0:NS, :], mhalf[0:NS, 0:1], ALU.pow).then_inc(done["dpw"], 1)

            def conv_low(p):
                pool.wait_ge(done["xc_hi"], p + 1)
                pool.wait_ge(done["xc_full"], p + 1)
                g_.tensor_tensor(xc_lo[:], xc_full[:], xc_hi[:].bitcast(F32), ALU.subtract).then_inc(done["xc_lo"], 1)

            def gate_diff(p):
                pool.wait_ge(done["gn"], p + 1)
                before(pool, "go", p)
                g_.tensor_tensor(gd[:], h2_hi[:].bitcast(F32), gn[:], ALU.subtract).then_inc(done["gd1"], 1)
                pool.wait_ge(done["gd1"], p + 1)
                g_.tensor_tensor(gd[:], gd[:], h2_lo[:].bitcast(F32), ALU.add).then_inc(done["gd"], 1)

            def turn(t, a, b, c):
                def A(step, *args):
                    if a is not None:
                        step(a, *args)

                def B(step, *args):
                    if b is not None:
                        step(b, *args)

                def C(step, *args):
                    if c is not None:
                        step(c, *args)

                B(rstd, "2")
                A(rstd, "1")
                C(rstd, "3")
                A(adj_eps)
                A(x_bias)
                B(y1_low)
                C(degree_root)
                A(rms)
                C(rstd, "4")
                B(conv_low)
                B(gate_diff)

            turns(pool, turn)


def kernel(**inputs):
    import numpy as np
    import concourse.bacc as bacc
    from concourse.bass_utils import run_bass_kernel_spmd

    f = {k: np.asarray(v) for k, v in inputs.items()}
    consts = np.zeros((P, K_COLS), np.float32)
    consts[:, K_IDENT:K_IDENT + P] = np.eye(P)
    for i, (g, a, n) in enumerate(STACK):
        consts[32 * a + n, K_SEL + i] = 1
        consts[i, K_BACK + 32 * a + n] = 1
        consts[i, K_GRP + g] = 1
        for j, (g2, a2, _) in enumerate(STACK):
            consts[i, K_SAME + j] = g == g2 and a == a2
    L0, L1, L2, L3 = "L0_gnn_", "L1_gnn_", "L2_gnn_", "L3_gnn_"
    bn1, bn2 = (np.stack([f[L1 + bn + k] for k in "gbmv"]) for bn in ("bn1_", "bn2_"))
    w_se, b_se = np.zeros((D, P), np.float32), np.zeros((P, 1), np.float32)
    for k in range(3):
        w_se[:, 32 * k:32 * k + 3] = f[L1 + "w_se"].T
        b_se[32 * k:32 * k + 3, 0] = f[L1 + "b_se"]
    vectors = {"rms_w": f[L0 + "rms_weight"].reshape(C0, P).T, "bn1": bn1.T, "bn2": bn2.T,
               "b_ih": f[L1 + "b_ih"].reshape(3, P).T, "b_hh": f[L1 + "b_hh"].reshape(3, P).T,
               "l2_b1": f[L2 + "b1"].reshape(NG * C2, P).T, "b3": f[L3 + "W_b"].reshape(P, 1),
               "a3": f[L3 + "a_w"].reshape(2, P).T, "b_se": b_se}
    laid = [
        f["x"], f["adj"], f[L0 + "epsilon"].reshape(1), f[L0 + "W1"], f[L0 + "b1"], f[L0 + "W2"],
        f[L0 + "b2"], w_se, f[L1 + "conv1_w"][:, :, 0].T,
        f[L1 + "conv2_w"].transpose(1, 2, 0).reshape(D, TAPS * D), bn2[[0, 3]], f[L1 + "w_msg"].T, f[L1 + "b_msg"],
        f[L1 + "w_ih"].T, f[L1 + "w_hh"].T, f[L2 + "W1"], f[L2 + "W2"], f[L2 + "b2"],
        f[L2 + "fusion_w"], f[L3 + "W_w"], f[L3 + "W_w"].T, f[L3 + "W_b"], f[L3 + "a_b"], consts,
        np.concatenate([vectors[k] for k in VECTORS], 1),
    ]
    nc = bacc.Bacc("TRN2", target_bir_lowering=False, num_devices=1)
    arrays, args = {}, []
    for i, a in enumerate(laid):
        a = np.ascontiguousarray(a)
        arrays[f"in_{i}_dram"] = a
        args.append(nc.dram_tensor(f"in_{i}_dram", a.shape, mybir.dt.from_np(a.dtype), kind="ExternalInput").ap())
    args.append(nc.dram_tensor("out_dram", (GRAPHS, NODES, D), F32, kind="ExternalOutput").ap())
    build(nc, *args)
    r = run_bass_kernel_spmd(nc, [arrays], core_ids=[0])
    return r.results[0]["out_dram"]
```

```python
from contextlib import ExitStack

import concourse.bass as bass
from concourse import mybir

F32 = mybir.dt.float32
F32R = mybir.dt.float32r
ACT = mybir.ActivationFunctionType
ALU = mybir.AluOpType
AX = mybir.AxisListType

GRAPHS, NODES, D = 32, 256, 128
P = 128
TILES = NODES // P
PAIRS = GRAPHS // 2
X_RING = 8
RING = 5
Q = 2 * TILES
W = 2 * NODES
HID0 = 512
C0 = HID0 // P
TAPS, PAD = 17, 8
PADW = NODES + 2 * PAD
GROUPS = [list(range(25)), [0, 1, 2, 3, 4, 5, 6, 7, 8], [0, 9, 10, 11, 12, 13, 14], [6, 7, 8, 12, 13, 14],
          [3, 4, 5, 9, 10, 11]]
NG = len(GROUPS)
JOINTS = 25
HID2 = 256
C2 = HID2 // P
STACK = [(g, a, n) for g, nodes in enumerate(GROUPS) for a in range(2) for n in nodes]
NS = len(STACK)
G_START = [min(i for i, s in enumerate(STACK) if s[0] == g) for g in range(NG)]
G_SIZE = [2 * len(nodes) for nodes in GROUPS]
JP = 32 + JOINTS
K_DIST = 67
K_IDENT, K_SEL, K_SAME, K_BACK, K_GRP = 0, P, P + NS, P + 2 * NS, P + 2 * NS + 64
K_COLS = K_GRP + NG
VECTORS = {"rms_w": C0, "bn1": 4, "bn2": 4, "b_ih": 3, "b_hh": 3, "l2_b1": NG * C2, "b3": 1, "a3": 2, "b_se": 1}
V_AT = {k: sum(list(VECTORS.values())[:i]) for i, k in enumerate(VECTORS)}
V_COLS = sum(VECTORS.values())
LN_EPS, RMS_EPS, BN_EPS = 1e-5, 1e-6, 1e-5
CONV_CUTS = [0, 3, 6, 9, 12, 15, 17]


def build(nc, x, adj, eps0, w1, b1, w2, b2, w_seT, conv1T, conv2T, w_msgT, b_msg, w_ihT, w_hhT,
          l2_w1, l2_w2, l2_b2, fusion, w3, w3T, b3, ab3, consts, vectors, out):
    with ExitStack() as ctx:
        def sb(name, shape, dt=F32):
            return ctx.enter_context(nc.sbuf_tensor(name, shape, dt))

        def sem(name):
            return ctx.enter_context(nc.semaphore(name))

        def pair_of(name, shape):
            return sb(name + "_hi", shape, F32R), sb(name + "_lo", shape, F32R)

        x_all = sb("x_all", [P, X_RING * W])
        adjT_all = sb("adjT_all", [P, RING * 2 * W])

        kst = sb("kst", [P, K_COLS])
        ident, sel = kst[:, K_IDENT:K_IDENT + P], kst[0:JP, K_SEL:K_SEL + NS]
        same = kst[0:NS, K_SAME:K_SAME + NS]
        grp = kst[0:NS, K_GRP:K_GRP + NG]
        identr = sb("identr", [P, P], F32R)
        eps_c = sb("eps_c", [P, 1])
        epsI = sb("epsI", [P, P])
        w1_hi, w1_lo = pair_of("w1", [P, HID0])
        w2_s = sb("w2_s", [P, C0, D])
        b1_r = sb("b1_r", [P, HID0])
        b2_r = sb("b2_r", [P, D])
        vec = sb("vec", [P, V_COLS])

        def vector(name):
            return vec[:, V_AT[name]:V_AT[name] + VECTORS[name]]

        rmsw_c, bn1_c, bn2_c, bih_c, bhh_c = (vector(n) for n in ("rms_w", "bn1", "bn2", "b_ih", "b_hh"))
        vb1_c = vector("l2_b1").rearrange("p (g c) -> p g c", g=NG)
        b3_c, a3_c, bse_c = vector("b3"), vector("a3"), vector("b_se")
        c1_hi, c1_lo = pair_of("c1", [P, D])
        c2_hi, c2_lo = pair_of("c2", [P, TAPS * D])
        s2rep, s2_row = sb("s2rep", [P, P]), sb("s2_row", [P, D])
        s1_c, o1_c, s2_c, o2_c = (sb(n, [P, 1]) for n in ("s1_c", "o1_c", "s2_c", "o2_c"))
        bnw = sb("bnw", [P, 4])
        wse_raw = sb("wse_raw", [P, P])
        se_hi, se_lo = pair_of("se", [P, P])
        wmsg_s = sb("wmsg_s", [P, D])
        bmsg_r = sb("bmsg_r", [P, D])
        ih_hi, ih_lo = pair_of("ih", [P, 2, 3 * D])
        hh_hi, hh_lo = pair_of("hh", [P, 3 * D])
        brz_c, bhn_c = sb("brz_c", [P, 2]), sb("bhn_c", [P, 1])
        v1_s = sb("v1_s", [P, NG, HID2])
        v2_s = sb("v2_s", [P, NG, C2, D])
        hb_m = sb("hb_m", [P, C2, NS])
        zb_m = sb("zb_m", [NS, D])
        fw = sb("fw", [P, NG])
        fwm, fws, nw_row = sb("fwm", [P, 1]), sb("fws", [P, 1]), sb("nw_row", [P, 1])
        fwe = sb("fwe", [P, NG])
        w3_raw = sb("w3_raw", [P, D])
        w3x = sb("w3x", [P, D + 1])
        b3_r, b3rep = sb("b3_r", [P, D]), sb("b3rep", [P, P])
        a12_c, ab_c, v1col = sb("a12_c", [P, 1]), sb("ab_c", [P, 1]), sb("v1col", [P, 1])
        e_rep = sb("e_rep", [P, P])
        fconst = sb("fconst", [P, 1])
        mhalf = sb("mhalf", [P, Q])
        ones = sb("ones", [P, P])
        epsln, epsrms = sb("epsln", [P, Q]), sb("epsrms", [P, Q])
        table_tick = sb("table_tick", [P, 2])
        tick = sb("tick", [P, 8])

        adj_s = sb("adj_s", [P, Q, NODES])
        adjE = sb("adjE", [P, Q, P])
        ln_st = {k: sb("st" + k, [P, Q, 6]) for k in "1234"}
        ln_mv = {k: sb("mv" + k, [P, Q, 2]) for k in "1234"}
        ln_ve = {k: sb("ve" + k, [P, Q]) for k in "1234"}
        ln_rs = {k: sb("rs" + k, [P, Q]) for k in "1234"}
        h1, nb1 = sb("h1", [P, W]), sb("nb1", [P, Q])
        ag_hi, ag_lo = pair_of("ag", [P, W])
        hb = sb("hb", [P, Q, HID0])
        hsq = sb("hsq", [P, HID0])
        ssq, sve, srs = sb("ssq", [P, Q]), sb("sve", [P, Q]), sb("srs", [P, Q])
        sT = sb("sT", [P, C0, W])
        xn2 = sb("xn2", [P, W])
        h2_hi, h2_lo = pair_of("h2", [P, W])
        h2_full = sb("h2_full", [P, W])
        y1_hi, y1_lo = pair_of("y1", [P, 2, PADW])
        y1_full = sb("y1_full", [P, W])
        dl, dr = sb("dl", [P, W]), sb("dr", [P, W])
        ex1 = sb("ex1", [P, 2, W])
        msg_t, msg = sb("msg_t", [P, W]), sb("msg", [P, W])
        nm_hi, nm_lo = pair_of("nm", [P, W])
        xc_hi, xc_lo = pair_of("xc", [P, W])
        xc_full = sb("xc_full", [P, W])
        tr, tz, gh, gm, gn = (sb(n, [P, W]) for n in ("tr", "tz", "gh", "gm", "gn"))
        gd, go = sb("gd", [P, W]), sb("go", [P, W])
        jadj = sb("jadj", [P, P])
        jq = sb("jq", [P, NS])
        nmat, nsc, nT = sb("nmat", [P, NS]), sb("nsc", [P, NS]), sb("nT", [P, NS])
        deg, isz, dsafe, dpow, dinv = (sb(n, [P, 1]) for n in ("deg", "isz", "dsafe", "dpow", "dinv"))
        xj = sb("xj", [P, D])
        xs, t1, hid = sb("xs", [P, D]), sb("t1", [P, NS]), sb("hid", [P, C2, NS])
        hidr = sb("hidr", [P, C2, NS])
        yT, ys, zb, zr = sb("yT", [P, NS]), sb("ys", [P, D]), sb("zb", [P, D]), sb("zr", [P, D])
        xn4, h4T = sb("xn4", [P, W]), sb("h4T", [P, W])
        hx = sb("hx", [P, Q, D + 1])
        fcol = sb("fcol", [P, Q])
        ex3 = sb("ex3", [P, 2, W])
        rec = sb("rec", [P, Q])

        pA = [ctx.enter_context(nc.psum_tensor(f"pA{k}", [P, W], F32)) for k in range(2)]
        pB = [ctx.enter_context(nc.psum_tensor(f"pB{k}", [P, W], F32)) for k in range(3)]
        pC = ctx.enter_context(nc.psum_tensor("pC", [P, W], F32))
        pD = [ctx.enter_context(nc.psum_tensor(f"pD{k}", [P, W], F32)) for k in range(2)]

        names = """adj_loaded jadj_loaded x_loaded stored adj_transposed adjT adjE
            stats1 mean1 ve1 rstd1 h1 agg_mm agg_hi agg_lo w1_mm hb hsq sve srs u0 u_tr sT w2_mm x_b2 x1
            stats2 mean2 ve2 rstd2 xn2 h2_tr h2_hi h2_lo h2_full nb1 conv1_mm y1_hi y1_full y1_lo se_mm dl dr0 dr dist_mm ex1 amask1
            msg_mm msg_t msg nmp_mm nm_hi nm_lo conv2_mm xc_hi xc_full xc_lo r_mm tr ghn_mm gh gm1 gin_mm gm gn
            z_mm tz gd ge go go_tr x2
            jq_mm jq n0_mm nmask nmat dgz dsf dpw dinv nsc n_tr nT stats3 mean3 ve3 rstd3 xn3 xj xs_mm xs t1_mm t1
            hid_mm hid hidr y_mm yT y_tr ys z2_mm zb zr fus_mm x3
            stats4 mean4 ve4 rstd4 xn4 h4_tr h4T hx fcol e_mm ex3 u3 u3_mm rec x4""".split()
        done = {n: sem(n) for n in names}
        first_loaded, loaded = sem("first_weights_loaded"), sem("weights_loaded")
        prep0, bn_roots, prep1, prep_gates = sem("prep0"), sem("bn_roots"), sem("prep1"), sem("prep_gates")
        s2_spread, s2_mm, s2_out = sem("s2_spread"), sem("s2_mm"), sem("s2_out")
        conv2_scaled, conv2_hi, conv2_lo = sem("conv2_scaled"), sem("conv2_hi"), sem("conv2_lo")
        prep_g, consts3_mm, prep3 = sem("prep_g"), sem("consts3_mm"), sem("prep3")
        pool_ready = sem("pool_ready")
        weights = []

        def bc(src, n=P):
            return src.rearrange("(a c) -> a c", a=1).broadcast_to([n, src.shape[0]])

        first_weights = [(kst[:], consts), (eps_c[:], bc(eps0)), (vec[:], vectors), (b1_r[:], bc(b1)), (b2_r[:], bc(b2)),
                         (w2_s[:], w2.rearrange("(c p) d -> p c d", p=P))]
        weights += [(wse_raw[:], w_seT), (wmsg_s[:], w_msgT), (bmsg_r[:], bc(b_msg)),
                    (v1_s[:], l2_w1.rearrange("g d h -> d g h")), (v2_s[:], l2_w2.rearrange("g (c p) d -> p g c d", p=P)),
                    (fw[:], bc(fusion)), (w3_raw[:], w3), (w3x[:, 0:D], w3T), (b3_r[:], bc(b3)), (ab_c[:], bc(ab3))]
        weights += [(zb_m[G_START[g]:G_START[g] + G_SIZE[g], :], bc(l2_b2[g], G_SIZE[g])) for g in range(NG)]
        x_free, adjT_free = 5 * W, 2 * (2 * W)
        raw_w1, raw_ih = x_all[:, x_free:x_free + HID0], x_all[:, x_free + HID0:x_free + HID0 + 6 * D]
        raw_c2 = adjT_all[:, adjT_free:adjT_free + TAPS * D]
        raw_c1 = adjT_all[:, adjT_free + TAPS * D:adjT_free + (TAPS + 1) * D]
        raw_hh = adjT_all[:, adjT_free + (TAPS + 1) * D:adjT_free + (TAPS + 4) * D]
        assert HID0 + 6 * D <= 3 * W and (TAPS + 4) * D <= 3 * 2 * W
        w1_in, split_in, conv2_in = sem("w1_in"), sem("split_in"), sem("conv2_in")
        link_sem, fw_exp, pool_mem = sem("link"), sem("fw_exp"), sem("pool_mem")

        def x_tile(p, q):
            s = (p % X_RING) * W + q * P
            return x_all[:, bass.ds(s, P)] if not isinstance(p, int) else x_all[:, s:s + P]

        def x_pair(p):
            s = (p % X_RING) * W
            return x_all[:, bass.ds(s, W)] if not isinstance(p, int) else x_all[:, s:s + W]

        def adjT(p, g, at=0, n=W):
            s = (p % RING) * (2 * W) + (g * W + at)
            return adjT_all[:, bass.ds(s, n)] if not isinstance(p, int) else adjT_all[:, s:s + n]

        def turns(eng, turn, after={}):
            for t in range(5):
                turn(t, *(t - k if t >= k else None for k in range(1, 5)))
                if t in after:
                    after[t]()
            with eng.Fori(5, PAIRS) as t:
                turn(t, t - 1, t - 2, t - 3, t - 4)
            for t in range(PAIRS, PAIRS + 4):
                turn(None, *(t - k if t - k < PAIRS else None for k in range(1, 5)))

        def before(eng, name, p, per=1):
            if not (isinstance(p, int) and p == 0):
                eng.wait_ge(done[name], p * per)

        def at_first(eng, p, signal, n=1):
            if isinstance(p, int) and p == 0:
                eng.wait_ge(signal, n)

        block = ctx.enter_context(nc.Block())

        @block.sync
        def _(sp):
            sp.dma_start(adj_s[:], adj[0:2].rearrange("b (t p) m -> p (b t) m", p=P)).then_inc(done["adj_loaded"], 16)
            sp.dma_start(x_all[:, 0:W].rearrange("p (q d) -> p q d", d=D),
                         x[0:2].rearrange("b (t p) d -> p (b t) d", p=P)).then_inc(done["x_loaded"], 16)
            for dst, src in first_weights[:3]:
                sp.dma_start(dst, src).then_inc(first_loaded, 16)
            sp.dma_start(raw_w1, w1).then_inc(w1_in, 16)
            for dst, src in first_weights[3:]:
                sp.dma_start(dst, src).then_inc(first_loaded, 16)
            sp.dma_start(raw_c1, conv1T).then_inc(split_in, 16)
            sp.dma_start(raw_hh, w_hhT).then_inc(split_in, 16)
            sp.dma_start(raw_ih.rearrange("p (k n) -> p k n", k=2),
                         w_ihT.rearrange("(k p) n -> p k n", p=P)).then_inc(split_in, 16)
            sp.dma_start(raw_c2, conv2T).then_inc(conv2_in, 16)
            for dst, src in weights:
                sp.dma_start(dst, src).then_inc(loaded, 16)

            def load_x(p):
                before(sp, "stats1", p)
                sp.dma_start(x_pair(p).rearrange("p (q d) -> p q d", d=D),
                             x[bass.ds(p * 2, 2)].rearrange("b (t p) d -> p (b t) d", p=P)
                             ).then_inc(done["x_loaded"], 16)

            def load_adj(p):
                before(sp, "adj_transposed", p, 2)
                sp.dma_start(adj_s[:], adj[bass.ds(p * 2, 2)].rearrange("b (t p) m -> p (b t) m", p=P)
                             ).then_inc(done["adj_loaded"], 16)

            def load_joints(p):
                before(sp, "jq_mm", p)
                for a in range(2):
                    sp.dma_start(jadj[32 * a:32 * a + JOINTS, 32 * a:32 * a + JOINTS],
                                 adj[bass.ds(p * 2 + a, 1), 0:JOINTS, 0:JOINTS].rearrange("b n m -> (b n) m")
                                 ).then_inc(done["jadj_loaded"], 16)

            def store(p):
                at = (p % X_RING) * W
                at = at if isinstance(p, int) else sp.snap(at)
                sp.wait_ge(done["x4"], p + 1)
                before(sp, "stored", p, 16)
                sp.dma_start(out[bass.ds(p * 2, 2)].rearrange("b (t p) d -> p (b t) d", p=P),
                             x_all[:, bass.ds(at, W)].rearrange("p (q d) -> p q d", d=D)).then_inc(done["stored"], 16)

            sp.wait_ge(pool_ready, 1)
            load_joints(0)
            for t in range(1, 5):
                load_x(t)
                load_adj(t)
            load_joints(1)
            load_joints(2)
            with sp.Fori(5, PAIRS) as t:
                load_x(t)
                load_adj(t)
                store(t - 5)
                load_joints(t - 2)
            store(PAIRS - 5)
            load_joints(PAIRS - 2)
            store(PAIRS - 4)
            load_joints(PAIRS - 1)
            for p in range(PAIRS - 3, PAIRS):
                store(p)
            sp.wait_ge(done["stored"], 16 * PAIRS)

        @block.tensor
        def _(pe):
            mm = nc.tensor.matmul

            def three(o, w_hi, w_lo, m_hi, m_lo, start, stop):
                mm(o, w_hi, m_hi, start=start, stop=False)
                mm(o, w_hi, m_lo, start=False, stop=False)
                return mm(o, w_lo, m_hi, start=False, stop=stop)

            def start_constants():
                pe.wait_ge(s2_spread, 1)
                mm(pC[:, 0:D], s2rep[:], ident, start=True, stop=True).then_inc(s2_mm, 1)

            def constants3():
                pe.wait_ge(s2_out, 1)
                pe.wait_ge(loaded, 16 * len(weights))
                mm(pC[:, 0:2], w3_raw[:], a3_c[:], start=True, stop=True)
                pe.wait_ge(prep_g, 1)
                mm(pC[:, 2:3], b3rep[:], a12_c[:], start=True, stop=True).then_inc(consts3_mm, 1)

            pe.wait_ge(first_loaded, 16 * len(first_weights))

            def adj_transposes(p, g):
                if g == 0:
                    pe.wait_ge(done["adj_loaded"], (p + 1) * 16)
                    before(pe, "sT", p, C0)
                else:
                    pe.wait_ge(done["adjT"], 2 * p + 1)
                for mt in range(TILES):
                    for nt in range(TILES):
                        o = mt * NODES + nt * P
                        i = nc.tensor.transpose(pA[0][:, o:o + P], adj_s[:, g * TILES + nt, mt * P:mt * P + P], ident)
                i.then_inc(done["adj_transposed"], 1)

            def aggregate(p):
                pe.wait_ge(done["adjT"], 2 * (p + 1))
                pe.wait_ge(done["adjE"], p + 1)
                pe.wait_ge(done["h1"], p + 1)
                for g in range(2):
                    for nt in range(TILES):
                        o = pA[0][:, g * NODES + nt * P:g * NODES + nt * P + P]
                        for mt in range(TILES):
                            q = g * TILES + mt
                            rhs = adjE[:, q, :] if mt == nt else adjT(p, g, mt * NODES + nt * P, P)
                            i = mm(o, h1[:, q * P:q * P + P], rhs, start=(mt == 0), stop=(mt == TILES - 1))
                i.then_inc(done["agg_mm"], 1)

            def hidden0(p, first):
                if first == 0:
                    at_first(pe, p, prep0)
                    pe.wait_ge(done["agg_hi"], p + 1)
                    pe.wait_ge(done["agg_lo"], p + 1)
                    before(pe, "x1", p)
                for q in range(first, first + 2):
                    if q >= 2:
                        pe.wait_ge(done["hb"], Q * p + q - 1)
                    t = slice(q * P, q * P + P)
                    three(pA[1 - q % 2][:], ag_hi[:, t], ag_lo[:, t], w1_hi[:], w1_lo[:], True, True
                          ).then_inc(done["w1_mm"], 1)

            def hidden0_transposes(p, first):
                if first == 0:
                    pe.wait_ge(done["hb"], Q * (p + 1))
                    pe.wait_ge(done["u0"], p + 1)
                for c in range(first, first + 2):
                    if c >= 2:
                        pe.wait_ge(done["sT"], C0 * p + c - 1)
                    for q in range(Q):
                        i = nc.tensor.transpose(pA[1 - c % 2][:, q * P:q * P + P], hb[:, q, c * P:c * P + P], ident)
                    i.then_inc(done["u_tr"], 1)

            def output0(p, first):
                if first == 0:
                    pe.wait_ge(done["sT"], C0 * (p + 1))
                for q in range(first, first + 2):
                    for c in range(C0):
                        i = mm(pA[1][:, q * D:q * D + D], sT[:, c, q * P:q * P + P], w2_s[:, c, :],
                               start=(c == 0), stop=(c == C0 - 1))
                if first:
                    i.then_inc(done["w2_mm"], 1)

            def h2_transposes(p):
                pe.wait_ge(done["xn2"], p + 1)
                before(pe, "gm", p)
                for q in range(Q):
                    i = nc.tensor.transpose(pB[1][:, q * P:q * P + P], xn2[:, q * P:q * P + P], ident)
                i.then_inc(done["h2_tr"], 1)

            def project_dist(p):
                at_first(pe, p, prep1)
                pe.wait_ge(done["h2_hi"], p + 1)
                pe.wait_ge(done["h2_lo"], p + 1)
                three(pB[1][:], se_hi[:], se_lo[:], h2_hi[:], h2_lo[:], True, True).then_inc(done["se_mm"], 1)

            def project_conv(p):
                before(pe, "x2", p)
                three(pB[2][:], c1_hi[:], c1_lo[:], h2_hi[:], h2_lo[:], True, True).then_inc(done["conv1_mm"], 1)

            def project_msg(p):
                pe.wait_ge(done["h2_full"], p + 1)
                pe.wait_ge(done["y1_full"], p + 1)
                for q in range(Q):
                    i = mm(pB[2][:, q * D:q * D + D], h2_full[:, q * P:q * P + P], wmsg_s[:], start=True, stop=True)
                i.then_inc(done["msg_mm"], 1)

            def distances(p, g):
                if g == 0:
                    pe.wait_ge(done["dl"], p + 1)
                    pe.wait_ge(done["dr"], p + 1)
                else:
                    pe.wait_ge(done["msg_t"], p + 1)
                for mt in range(TILES):
                    m = g * NODES + mt * P
                    i = mm(pB[1 + g][:, mt * NODES:(mt + 1) * NODES], dl[0:K_DIST, m:m + P],
                           dr[0:K_DIST, g * NODES:(g + 1) * NODES], start=True, stop=True)
                i.then_inc(done["dist_mm"], 1)

            def conv2(p, part):
                if part == 0:
                    at_first(pe, p, conv2_lo)
                    pe.wait_ge(done["y1_hi"], p + 1)
                    pe.wait_ge(done["y1_lo"], p + 1)
                    before(pe, "tz", p)
                for k in range(CONV_CUTS[part], CONV_CUTS[part + 1]):
                    w = slice(k * D, k * D + D)
                    three(pB[0][:], c2_hi[:, w], c2_lo[:, w], y1_hi[:, :, k:k + NODES], y1_lo[:, :, k:k + NODES],
                          k == 0, False)
                if part == len(CONV_CUTS) - 2:
                    mm(pB[0][:], identr[:], h2_hi[:], start=False, stop=False)
                    mm(pB[0][:], identr[:], h2_lo[:], start=False, stop=True).then_inc(done["conv2_mm"], 1)

            def messages(p):
                pe.wait_ge(done["msg"], p + 1)
                pe.wait_ge(done["amask1"], 2 * (p + 1))
                for g in range(2):
                    for mt in range(TILES):
                        q = g * TILES + mt
                        i = mm(pB[1][:, g * NODES:(g + 1) * NODES], msg[:, q * D:q * D + D],
                               ex1[:, g, mt * NODES:(mt + 1) * NODES], start=(mt == 0), stop=(mt == TILES - 1))
                i.then_inc(done["nmp_mm"], 1)

            def of_h2(o, j, start, stop):
                w = slice(j * D, j * D + D)
                return three(o, hh_hi[:, w], hh_lo[:, w], h2_hi[:], h2_lo[:], start, stop)

            def of_nmp(o, j, start, stop):
                w = slice(j * D, j * D + D)
                return three(o, ih_hi[:, 1, w], ih_lo[:, 1, w], nm_hi[:], nm_lo[:], start, stop)

            def of_conv(o, j, start, stop):
                w = slice(j * D, j * D + D)
                return three(o, ih_hi[:, 0, w], ih_lo[:, 0, w], xc_hi[:], xc_lo[:], start, stop)

            def gate_hn(p):
                at_first(pe, p, prep_gates)
                pe.wait_ge(done["nm_hi"], p + 1)
                pe.wait_ge(done["nm_lo"], p + 1)
                of_h2(pB[1][:], 2, True, True).then_inc(done["ghn_mm"], 1)

            def gates_early(p):
                pe.wait_ge(done["ex1"], 2 * (p + 1))
                of_h2(pB[2][:], 0, True, False)
                of_nmp(pB[2][:], 0, False, False)
                pe.wait_ge(done["gh"], p + 1)
                of_nmp(pB[1][:], 2, True, False)

            def gates_late(p):
                pe.wait_ge(done["xc_hi"], p + 1)
                pe.wait_ge(done["xc_lo"], p + 1)
                of_conv(pB[2][:], 0, False, True).then_inc(done["r_mm"], 1)
                of_conv(pB[1][:], 2, False, True).then_inc(done["gin_mm"], 1)

            def gate_z(p):
                pe.wait_ge(done["xc_full"], p + 1)
                of_h2(pB[0][:], 1, True, False)
                of_nmp(pB[0][:], 1, False, False)
                of_conv(pB[0][:], 1, False, True).then_inc(done["z_mm"], 1)

            def back_transposes(p):
                pe.wait_ge(done["go"], p + 1)
                pe.wait_ge(done["tr"], p + 1)
                for q in range(Q):
                    i = nc.tensor.transpose(pB[2][:, q * P:q * P + P], go[:, q * P:q * P + P], ident)
                i.then_inc(done["go_tr"], 1)

            def joints_left(p):
                pe.wait_ge(done["jadj_loaded"], (p + 1) * 32)
                before(pe, "x3", p)
                mm(pC[:, 0:NS], jadj[0:JP, :], sel, start=True, stop=True).then_inc(done["jq_mm"], 1)

            def joints_right(p):
                pe.wait_ge(done["jq"], p + 1)
                mm(pC[0:NS, 0:NS], jq[0:JP, :], sel, start=True, stop=True).then_inc(done["n0_mm"], 1)

            def stack_rows(p):
                pe.wait_ge(done["xj"], p + 1)
                pe.wait_ge(done["nmask"], p + 1)
                mm(pC[0:NS, 0:D], sel, xj[0:JP, :], start=True, stop=True).then_inc(done["xs_mm"], 1)

            def norm_transpose(p):
                pe.wait_ge(done["nsc"], p + 1)
                pe.wait_ge(done["xs"], p + 1)
                nc.tensor.transpose(pC[0:NS, 0:NS], nsc[0:NS, :], ident[0:NS, 0:NS]).then_inc(done["n_tr"], 1)

            def spread1(p):
                pe.wait_ge(done["nT"], p + 1)
                mm(pC[:, 0:NS], xs[0:NS, :], nT[0:NS, :], start=True, stop=True).then_inc(done["t1_mm"], 1)

            def hidden2(p):
                pe.wait_ge(done["t1"], p + 1)
                for c in range(C2):
                    for g in range(NG):
                        a, n = G_START[g], G_SIZE[g]
                        i = mm(pC[:, c * NS + a:c * NS + a + n], v1_s[:, g, c * P:c * P + P], t1[:, a:a + n],
                               start=True, stop=True)
                i.then_inc(done["hid_mm"], 1)

            def output2(p):
                pe.wait_ge(done["hidr"], p + 1)
                for g in range(NG):
                    a, n = G_START[g], G_SIZE[g]
                    for c in range(C2):
                        i = mm(pC[:, a:a + n], v2_s[:, g, c, :], hidr[:, c, a:a + n], start=(c == 0), stop=(c == C2 - 1))
                i.then_inc(done["y_mm"], 1)

            def y_transpose(p):
                pe.wait_ge(done["yT"], p + 1)
                nc.tensor.transpose(pC[0:NS, 0:P], yT[:, :], ident).then_inc(done["y_tr"], 1)

            def spread2(p):
                pe.wait_ge(done["ys"], p + 1)
                mm(pC[0:NS, 0:D], nT[0:NS, :], ys[0:NS, :], start=True, stop=True).then_inc(done["z2_mm"], 1)

            def fuse(p):
                pe.wait_ge(done["zr"], p + 1)
                for a in range(2):
                    back = kst[0:NS, K_BACK + 32 * a:K_BACK + 32 * a + 32]
                    i = mm(pC[0:32, a * D:a * D + D], back, zr[0:NS, :], start=True, stop=True)
                i.then_inc(done["fus_mm"], 1)

            def h4_transposes(p):
                pe.wait_ge(done["xn4"], p + 1)
                before(pe, "x4", p)
                for q in range(Q):
                    i = nc.tensor.transpose(pD[0][:, q * P:q * P + P], xn4[:, q * P:q * P + P], ident)
                i.then_inc(done["h4_tr"], 1)

            def project3(p, g):
                if g == 0:
                    at_first(pe, p, prep3)
                    pe.wait_ge(done["h4T"], p + 1)
                    for q in range(Q):
                        o = pD[1][:, q * (D + 1):(q + 1) * (D + 1)] if q < Q - 1 else pD[0][:, NODES:NODES + D + 1]
                        mm(o, h4T[:, q * P:q * P + P], w3x[:], start=True, stop=True)
                else:
                    pe.wait_ge(done["hx"], p + 1)
                mm(pD[g][:, 0:NODES], e_rep[:], h4T[:, g * NODES:(g + 1) * NODES], start=True, stop=True
                   ).then_inc(done["e_mm"], 1)

            def attend(p):
                pe.wait_ge(done["hx"], p + 1)
                pe.wait_ge(done["u3"], 2 * (p + 1))
                for g in range(2):
                    for nt in range(TILES):
                        for mt in range(TILES):
                            m = mt * NODES + nt * P
                            i = mm(pD[g][:, nt * (D + 1):(nt + 1) * (D + 1)], ex3[:, g, m:m + P],
                                   hx[:, g * TILES + mt, :], start=(mt == 0), stop=(mt == TILES - 1))
                i.then_inc(done["u3_mm"], 1)

            def turn(l, a, b, c, d):
                def L(step, *args):
                    if l is not None:
                        step(l, *args)

                def A(step, *args):
                    if a is not None:
                        step(a, *args)

                def B(step, *args):
                    if b is not None:
                        step(b, *args)

                def C(step, *args):
                    if c is not None:
                        step(c, *args)

                def D(step, *args):
                    if d is not None:
                        step(d, *args)

                D(h4_transposes)
                A(aggregate)
                B(h2_transposes)
                C(joints_left)
                D(project3, 0)
                C(back_transposes)
                B(project_dist)
                A(hidden0, 0)
                B(project_conv)
                A(hidden0, 2)
                D(project3, 1)
                B(distances, 0)
                B(project_msg)
                C(joints_right)
                B(conv2, 0)
                B(distances, 1)
                C(stack_rows)
                D(attend)
                C(norm_transpose)
                B(conv2, 1)
                C(spread1)
                A(hidden0_transposes, 0)
                B(conv2, 2)
                C(hidden2)
                A(hidden0_transposes, 2)
                B(messages)
                C(output2)
                B(conv2, 3)
                C(y_transpose)
                B(gate_hn)
                A(output0, 0)
                C(spread2)
                B(conv2, 4)
                L(adj_transposes, 0)
                C(fuse)
                B(conv2, 5)
                A(output0, 2)
                L(adj_transposes, 1)
                B(gates_early)
                B(gates_late)
                B(gate_z)

            turns(pe, turn, {0: start_constants, 1: constants3})

        @block.vector
        def _(dve):
            v = nc.vector
            link_at = [0]
            chain = link_sem

            def link(ins):
                link_at[0] += 1
                ins.then_inc(chain, 1)
                dve.wait_ge(chain, link_at[0])

            def split(hi, lo, raw):
                link(v.tensor_copy(hi, raw))
                return v.tensor_tensor(lo, raw, hi.bitcast(F32), ALU.subtract)

            def start0():
                dve.wait_ge(first_loaded, 16 * len(first_weights))
                v.tensor_scalar(epsI[:], ident, eps_c[:, 0:1], None, ALU.mult)
                dve.wait_ge(w1_in, 16)
                split(w1_hi[:], w1_lo[:], raw_w1).then_inc(prep0, 1)

            def start1():
                dve.wait_ge(bn_roots, 1)
                for k, (bn, s, o) in enumerate(((bn1_c, s1_c, o1_c), (bn2_c, s2_c, o2_c))):
                    link(v.tensor_tensor(s[:], bn[:, 0:1], bnw[:, k:k + 1], ALU.mult))
                    link(v.tensor_tensor(bnw[:, k + 2:k + 3], bn[:, 2:3], s[:], ALU.mult))
                    link(v.tensor_tensor(o[:], bn[:, 1:2], bnw[:, k + 2:k + 3], ALU.subtract))
                v.tensor_scalar(s2rep[:], ones[:], s2_c[:, 0:1], None, ALU.mult).then_inc(s2_spread, 1)
                dve.wait_ge(split_in, 48)
                split(c1_hi[:], c1_lo[:], raw_c1)
                v.tensor_copy(identr[:], ident)
                dve.wait_ge(s2_mm, 1)
                v.tensor_copy(s2_row[:], pC[:, 0:D]).then_inc(s2_out, 1)
                dve.wait_ge(loaded, 16 * len(weights))
                ROOT2 = 2.0 ** 0.5
                link(v.tensor_scalar(wse_raw[:], wse_raw[:], ROOT2, None, ALU.mult))
                link(v.tensor_scalar(bse_c[:], bse_c[:], ROOT2, None, ALU.mult))
                split(se_hi[:], se_lo[:], wse_raw[:])
                link(v.tensor_tensor(brz_c[:], bih_c[:, 0:2], bhh_c[:, 0:2], ALU.add))
                v.tensor_scalar(brz_c[:], brz_c[:], 0.5, None, ALU.mult)
                v.tensor_scalar(bhn_c[:], bhh_c[:, 2:3], 0.5, None, ALU.mult)
                link(v.tensor_reduce(fwm[:], fw[:], AX.X, ALU.max))
                link(v.tensor_scalar(fw[:], fw[:], fwm[:, 0:1], None, ALU.subtract))
                v.tensor_copy(fwe[:], fw[:]).then_inc(prep1, 1)

            def gate_weights(p):
                if isinstance(p, int) and p == 0:
                    split(hh_hi[:], hh_lo[:], raw_hh)
                    split(ih_hi[:].rearrange("p k n -> p (k n)"), ih_lo[:].rearrange("p k n -> p (k n)"), raw_ih
                          ).then_inc(prep_gates, 1)
                    dve.wait_ge(conv2_hi, 1)
                    v.tensor_tensor(c2_lo[:], raw_c2, c2_hi[:].bitcast(F32), ALU.subtract).then_inc(conv2_lo, 1)

            def start3():
                for g in range(NG):
                    for c in range(C2):
                        a, n = G_START[g], G_SIZE[g]
                        v.tensor_scalar(hb_m[:, c, a:a + n], ones[:, 0:n], vb1_c[:, g, c:c + 1], None, ALU.mult)
                dve.wait_ge(fw_exp, 1)
                link(v.tensor_reduce(fws[:], fw[:], AX.X, ALU.add))
                link(v.reciprocal(fws[:], fws[:]))
                link(v.tensor_scalar(fwe[:], fw[:], fws[:, 0:1], None, ALU.mult))
                link(v.tensor_tensor(fwe[0:NS, :], fwe[0:NS, :], grp, ALU.mult))
                v.tensor_reduce(nw_row[0:NS, :], fwe[0:NS, :], AX.X, ALU.add)
                dve.wait_ge(consts3_mm, 1)
                v.tensor_copy(w3x[:, D:D + 1], pC[:, 1:2])
                link(v.tensor_copy(v1col[:], pC[:, 0:1]))
                v.tensor_tensor(fconst[:], pC[:, 2:3], ab_c[:], ALU.add)
                v.tensor_scalar(e_rep[:], ones[:], v1col[:, 0:1], None, ALU.mult).then_inc(prep3, 1)

            start0()

            def carry_wait(n):
                v.memset(tick[:, n:n + 1], 0.0)

            def norm_stats(k, tiles, n=P):
                carry_wait(2 * int(k) - 2)
                for q, tile in tiles:
                    i = v.bn_stats(ln_st[k][0:n, q, :], tile)
                i.then_inc(done["stats" + k], 1)

            def norm_mean(k, p, qs, n=P):
                dve.wait_ge(done["stats" + k], p + 1)
                carry_wait(2 * int(k) - 1)
                for q in qs:
                    i = v.bn_aggr(ln_mv[k][0:n, q, :], ln_st[k][0:n, q, :])
                i.then_inc(done["mean" + k], 1)

            def norm_apply(k, p, tiles, name, n=P):
                dve.wait_ge(done["rstd" + k], p + 1)
                for q, tile, dst in tiles:
                    i = v.tensor_scalar(dst, tile, ln_mv[k][0:n, q, 0:1], ln_rs[k][0:n, q:q + 1],
                                        ALU.subtract, ALU.mult)
                i.then_inc(done[name], 1)

            def norm1(p):
                dve.wait_ge(done["x_loaded"], (p + 1) * 16)
                norm_stats("1", [(q, x_tile(p, q)) for q in range(Q)])
                norm_mean("1", p, range(Q))
                dve.wait_ge(done["rstd1"], p + 1)
                before(dve, "h1", p)
                v.scalar_tensor_tensor(out=nb1[:], in0=ln_mv["1"][:, :, 0], scalar=-1.0, in1=ln_rs["1"][:],
                                       op0=ALU.mult, op1=ALU.mult).then_inc(done["nb1"], 1)

            def adjT_out(p):
                dve.wait_ge(done["adj_transposed"], 2 * (p + 1))
                v.tensor_copy(adjT(p, 1), pA[0][:]).then_inc(done["adjT"], 1)

            def agg_low(p):
                dve.wait_ge(done["agg_hi"], p + 1)
                before(dve, "w1_mm", p, Q)
                v.tensor_tensor(ag_lo[:], pA[0][:], ag_hi[:].bitcast(F32), ALU.subtract).then_inc(done["agg_lo"], 1)

            def hidden0_bias(p, first):
                if first == 0:
                    before(dve, "u_tr", p, C0)
                for q in range(first, first + 2):
                    dve.wait_ge(done["w1_mm"], Q * p + q + 1)
                    v.tensor_tensor(hb[:, q, :], pA[1 - q % 2][:], b1_r[:], ALU.add).then_inc(done["hb"], 1)

            def hidden0_scale(p):
                dve.wait_ge(done["srs"], p + 1)
                for q in range(Q):
                    i = v.tensor_scalar(hb[:, q, :], hb[:, q, :], srs[:, q:q + 1], HID0 ** 0.5, ALU.mult, ALU.mult)
                i.then_inc(done["u0"], 1)

            def residual0(p):
                dve.wait_ge(done["w2_mm"], p + 1)
                dve.wait_ge(done["x_b2"], p + 1)
                v.tensor_tensor(x_pair(p), pA[1][:], x_pair(p), ALU.add).then_inc(done["x1"], 1)

            def norm2(p):
                dve.wait_ge(done["x1"], p + 1)
                norm_stats("2", [(q, x_tile(p, q)) for q in range(Q)])
                norm_mean("2", p, range(Q))

            def norm2_apply(p):
                before(dve, "h2_tr", p)
                norm_apply("2", p, [(q, x_tile(p, q), xn2[:, q * P:q * P + P]) for q in range(Q)], "xn2")

            def h2_low(p):
                dve.wait_ge(done["h2_hi"], p + 1)
                dve.wait_ge(done["h2_full"], p + 1)
                v.scalar_tensor_tensor(out=h2_lo[:], in0=pB[1][:], scalar=0.0, in1=h2_hi[:].bitcast(F32),
                                       op0=ALU.max, op1=ALU.subtract).then_inc(done["h2_lo"], 1)

            def dist_right(p):
                dve.wait_ge(done["se_mm"], p + 1)
                before(dve, "dist_mm", p, 2)
                v.tensor_scalar(dr[0:3, :], pB[1][0:3, :], bse_c[0:3, 0:1], None, ALU.add).then_inc(done["dr0"], 1)
                dve.wait_ge(done["dr0"], p + 1)
                v.tensor_copy(dl[0:3, :], dr[0:3, :]).then_inc(done["dr"], 1)

            def msg_bias(p):
                dve.wait_ge(done["msg_mm"], p + 1)
                before(dve, "nmp_mm", p)
                row = bmsg_r[:].rearrange("p (a d) -> p a d", a=1).broadcast_to([P, Q, D])
                v.tensor_tensor(msg_t[:].rearrange("p (q d) -> p q d", d=D), pB[2][:].rearrange("p (q d) -> p q d", d=D),
                                row, ALU.add).then_inc(done["msg_t"], 1)
                dve.wait_ge(done["msg_t"], p + 1)
                v.tensor_scalar(msg[:], msg_t[:], 0.0, None, ALU.max).then_inc(done["msg"], 1)

            def mask1(p):
                for g in range(2):
                    dve.wait_ge(done["ex1"], 2 * p + g + 1)
                    v.tensor_tensor(ex1[:, g, :], ex1[:, g, :], adjT(p, g), ALU.mult).then_inc(done["amask1"], 1)

            def nmp_low(p):
                dve.wait_ge(done["nm_hi"], p + 1)
                v.tensor_tensor(nm_lo[:], pB[1][:], nm_hi[:].bitcast(F32), ALU.subtract).then_inc(done["nm_lo"], 1)

            def y1_low(p):
                dve.wait_ge(done["y1_full"], p + 1)
                v.tensor_tensor(y1_lo[:, :, PAD:PAD + NODES], y1_full[:].rearrange("p (g n) -> p g n", g=2),
                                y1_hi[:, :, PAD:PAD + NODES].bitcast(F32), ALU.subtract).then_inc(done["y1_lo"], 1)

            def conv_low(p):
                dve.wait_ge(done["xc_full"], p + 1)
                v.tensor_tensor(xc_lo[:], xc_full[:], xc_hi[:].bitcast(F32), ALU.subtract).then_inc(done["xc_lo"], 1)

            def gate_mix(p):
                dve.wait_ge(done["tr"], p + 1)
                dve.wait_ge(done["gh"], p + 1)
                before(dve, "gn", p)
                v.scalar_tensor_tensor(out=gm[:], in0=tr[:], scalar=1.0, in1=gh[:], op0=ALU.add,
                                       op1=ALU.mult).then_inc(done["gm1"], 1)
                dve.wait_ge(done["gm1"], p + 1)
                dve.wait_ge(done["gin_mm"], p + 1)
                v.tensor_tensor(gm[:], pB[1][:], gm[:], ALU.add).then_inc(done["gm"], 1)

            def gate_out(p):
                dve.wait_ge(done["gn"], p + 1)
                v.tensor_tensor(gd[:], h2_full[:], gn[:], ALU.subtract).then_inc(done["gd"], 1)
                dve.wait_ge(done["gd"], p + 1)
                dve.wait_ge(done["tz"], p + 1)
                v.scalar_tensor_tensor(out=gd[:], in0=tz[:], scalar=1.0, in1=gd[:], op0=ALU.add,
                                       op1=ALU.mult).then_inc(done["ge"], 1)
                dve.wait_ge(done["ge"], p + 1)
                before(dve, "go_tr", p)
                v.scalar_tensor_tensor(out=go[:], in0=gd[:], scalar=0.5, in1=gn[:], op0=ALU.mult,
                                       op1=ALU.add).then_inc(done["go"], 1)

            def residual1(p):
                dve.wait_ge(done["go_tr"], p + 1)
                v.tensor_tensor(x_pair(p), pB[2][:], x_pair(p), ALU.add).then_inc(done["x2"], 1)

            def joint_tiles(p):
                return [(0, x_tile(p, 0)[0:JOINTS, :]), (2, x_tile(p, 2)[0:JOINTS, :])]

            def joints_copy(p):
                dve.wait_ge(done["jq_mm"], p + 1)
                before(dve, "n0_mm", p)
                v.tensor_copy(jq[0:JP, :], pC[0:JP, 0:NS]).then_inc(done["jq"], 1)

            def norm3(p):
                dve.wait_ge(done["x2"], p + 1)
                norm_stats("3", joint_tiles(p), JOINTS)
                norm_mean("3", p, (0, 2), JOINTS)

            def norm3_apply(p):
                before(dve, "xs_mm", p)
                norm_apply("3", p, [(q, x, xj[32 * (q // 2):32 * (q // 2) + JOINTS, :]) for q, x in joint_tiles(p)],
                           "xn3", JOINTS)
                dve.wait_ge(done["xn3"], p + 1)
                v.tensor_scalar(xj[0:JP, :], xj[0:JP, :], 0.0, None, ALU.max).then_inc(done["xj"], 1)

            def degrees(p):
                dve.wait_ge(done["n0_mm"], p + 1)
                v.tensor_tensor(nsc[0:NS, :], pC[0:NS, 0:NS], same, ALU.mult).then_inc(done["nmask"], 1)
                dve.wait_ge(done["nmask"], p + 1)
                v.tensor_tensor(nmat[0:NS, :], nsc[0:NS, :], ident[0:NS, 0:NS], ALU.add).then_inc(done["nmat"], 1)
                dve.wait_ge(done["nmat"], p + 1)
                v.tensor_reduce(deg[0:NS, :], nmat[0:NS, :], AX.X, ALU.add).then_inc(done["dgz"], 1)
                dve.wait_ge(done["dgz"], 3 * p + 1)
                v.tensor_scalar(isz[0:NS, :], deg[0:NS, :], 0.0, None, ALU.is_equal).then_inc(done["dgz"], 1)
                dve.wait_ge(done["dgz"], 3 * p + 2)
                v.tensor_tensor(dsafe[0:NS, :], deg[0:NS, :], isz[0:NS, :], ALU.add).then_inc(done["dgz"], 1)

            def norm_rows(p):
                dve.wait_ge(done["dpw"], p + 1)
                v.tensor_tensor(dinv[0:NS, :], dpow[0:NS, :], isz[0:NS, :], ALU.mult).then_inc(done["dsf"], 1)
                dve.wait_ge(done["dsf"], p + 1)
                v.tensor_tensor(dinv[0:NS, :], dpow[0:NS, :], dinv[0:NS, :], ALU.subtract).then_inc(done["dinv"], 1)
                dve.wait_ge(done["dinv"], p + 1)
                v.tensor_scalar(nsc[0:NS, :], nmat[0:NS, :], dinv[0:NS, 0:1], None, ALU.mult).then_inc(done["nsc"], 1)

            def norm_cols(p):
                dve.wait_ge(done["n_tr"], p + 1)
                before(dve, "z2_mm", p)
                v.tensor_scalar(nT[0:NS, :], pC[0:NS, 0:NS], dinv[0:NS, 0:1], None, ALU.mult).then_inc(done["nT"], 1)

            def stack_copy(p):
                dve.wait_ge(done["xs_mm"], p + 1)
                before(dve, "t1_mm", p)
                v.tensor_copy(xs[0:NS, :], pC[0:NS, 0:D]).then_inc(done["xs"], 1)

            def hid_bias(p):
                dve.wait_ge(done["hid_mm"], p + 1)
                v.tensor_tensor(hid[:], pC[:, 0:C2 * NS].rearrange("p (c n) -> p c n", c=C2), hb_m[:], ALU.add
                                ).then_inc(done["hid"], 1)
                dve.wait_ge(done["hid"], p + 1)
                before(dve, "y_mm", p)
                v.tensor_scalar(hidr[:], hid[:], 0.0, None, ALU.max).then_inc(done["hidr"], 1)

            def z_bias(p):
                dve.wait_ge(done["z2_mm"], p + 1)
                v.tensor_tensor(zb[0:NS, :], pC[0:NS, 0:D], zb_m[:], ALU.add).then_inc(done["zb"], 1)
                dve.wait_ge(done["zb"], p + 1)
                before(dve, "fus_mm", p)
                v.tensor_scalar(zr[0:NS, :], zb[0:NS, :], 0.0, nw_row[0:NS, 0:1], ALU.max, ALU.mult
                                ).then_inc(done["zr"], 1)

            def residual2(p):
                dve.wait_ge(done["fus_mm"], p + 1)
                for a, (_, x) in enumerate(joint_tiles(p)):
                    i = v.tensor_tensor(x, pC[0:JOINTS, a * D:a * D + D], x, ALU.add)
                i.then_inc(done["x3"], 1)

            def norm4(p):
                dve.wait_ge(done["x3"], p + 1)
                norm_stats("4", [(q, x_tile(p, q)) for q in range(Q)])
                norm_mean("4", p, range(Q))

            def norm4_apply(p):
                before(dve, "h4_tr", p)
                norm_apply("4", p, [(q, x_tile(p, q), xn4[:, q * P:q * P + P]) for q in range(Q)], "xn4")

            def h3_bias(p):
                dve.wait_ge(done["e_mm"], 2 * p + 1)
                before(dve, "u3_mm", p)
                most = pD[1][:, 0:(Q - 1) * (D + 1)].rearrange("p (q d) -> p q d", d=D + 1)
                v.tensor_scalar(fcol[:, 0:Q - 1], most[:, :, D], fconst[:, 0:1], None, ALU.add)
                v.tensor_scalar(fcol[:, Q - 1:Q], pD[0][:, NODES + D:NODES + D + 1], fconst[:, 0:1], None, ALU.add)
                v.tensor_tensor(hx[:, Q - 1, 0:D], pD[0][:, NODES:NODES + D], b3_r[:], ALU.add).then_inc(done["fcol"], 1)
                row = b3_r[:].rearrange("p (a d) -> p a d", a=1).broadcast_to([P, Q - 1, D])
                v.tensor_tensor(hx[:, 0:Q - 1, 0:D], most[:, :, 0:D], row, ALU.add).then_inc(done["hx"], 1)

            def mask3(p):
                for g in range(2):
                    dve.wait_ge(done["ex3"], Q * p + TILES * (g + 1))
                    v.tensor_tensor(ex3[:, g, :], ex3[:, g, :], adjT(p, g), ALU.mult).then_inc(done["u3"], 1)

            def attend_out(p):
                dve.wait_ge(done["u3_mm"], p + 1)
                for g in range(2):
                    src = pD[g][:, 0:TILES * (D + 1)].rearrange("p (q d) -> p q d", d=D + 1)
                    i = v.reciprocal(rec[:, g * TILES:(g + 1) * TILES], src[:, :, D])
                i.then_inc(done["rec"], 1)
                dve.wait_ge(done["rec"], p + 1)
                for q in range(Q):
                    g, nt = q // TILES, q % TILES
                    i = v.scalar_tensor_tensor(out=x_tile(p, q), in0=pD[g][:, nt * (D + 1):nt * (D + 1) + D],
                                               scalar=rec[:, q:q + 1], in1=x_tile(p, q), op0=ALU.mult, op1=ALU.add)
                i.then_inc(done["x4"], 1)

            def turn(l, a, b, c, d):
                def L(step, *args):
                    if l is not None:
                        step(l, *args)

                def A(step, *args):
                    if a is not None:
                        step(a, *args)

                def B(step, *args):
                    if b is not None:
                        step(b, *args)

                def C(step, *args):
                    if c is not None:
                        step(c, *args)

                def D(step, *args):
                    if d is not None:
                        step(d, *args)

                A(agg_low)
                B(h2_low)
                C(residual1)
                B(dist_right)
                A(hidden0_bias, 0)
                C(norm3)
                A(hidden0_bias, 2)
                D(h3_bias)
                B(y1_low)
                C(norm3_apply)
                C(joints_copy)
                B(msg_bias)
                D(mask3)
                C(degrees)
                C(norm_rows)
                C(stack_copy)
                B(mask1)
                A(gate_weights)
                A(hidden0_scale)
                C(norm_cols)
                D(attend_out)
                C(hid_bias)
                B(nmp_low)
                L(norm1)
                C(z_bias)
                C(residual2)
                C(norm4)
                B(conv_low)
                A(residual0)
                A(norm2)
                C(norm4_apply)
                L(adjT_out)
                A(norm2_apply)
                B(gate_mix)
                B(gate_out)

            turns(dve, turn, {0: start1, 1: start3})

        @block.scalar
        def _(act):
            s = nc.scalar.activation
            def start1():
                act.wait_ge(prep1, 1)
                s(fw[:], fwe[:], ACT.Exp).then_inc(fw_exp, 1)
                act.wait_ge(conv2_scaled, 1)
                s(c2_hi[:], raw_c2, ACT.Copy).then_inc(conv2_hi, 1)

            act.wait_ge(first_loaded, 16 * len(first_weights))

            def adjT_out(p):
                act.wait_ge(done["adj_transposed"], 2 * p + 1)
                s(adjT(p, 0), pA[0][:], ACT.Copy).then_inc(done["adjT"], 1)

            def norm1_apply(p):
                act.wait_ge(done["nb1"], p + 1)
                before(act, "agg_mm", p)
                for q in range(Q):
                    i = s(h1[:, q * P:q * P + P], x_tile(p, q), ACT.Relu, scale=ln_rs["1"][:, q:q + 1], bias=nb1[:, q:q + 1])
                i.then_inc(done["h1"], 1)

            def agg_high(p):
                act.wait_ge(done["agg_mm"], p + 1)
                before(act, "w1_mm", p, Q)
                s(ag_hi[:], pA[0][:], ACT.Copy).then_inc(done["agg_hi"], 1)

            def squares(p):
                before(act, "sve", p)
                for q in range(Q):
                    act.wait_ge(done["hb"], Q * p + q + 1)
                    if q:
                        act.wait_ge(done["hsq"], Q * p + q)
                    s(hsq[:], hb[:, q, :], ACT.Square, accum_out=ssq[:, q:q + 1]).then_inc(done["hsq"], 1)

            def silu(p):
                before(act, "w2_mm", p)
                for c in range(C0):
                    act.wait_ge(done["u_tr"], C0 * p + c + 1)
                    s(sT[:, c, :], pA[1 - c % 2][:], ACT.Silu, scale=rmsw_c[:, c:c + 1]).then_inc(done["sT"], 1)

            def h2_high(p):
                act.wait_ge(done["h2_tr"], p + 1)
                before(act, "z_mm", p)
                before(act, "gd", p)
                s(h2_hi[:], pB[1][:], ACT.Relu).then_inc(done["h2_hi"], 1)
                s(h2_full[:], pB[1][:], ACT.Relu).then_inc(done["h2_full"], 1)

            def conv1_out(p):
                act.wait_ge(done["conv1_mm"], p + 1)
                before(act, "conv2_mm", p)
                before(act, "y1_lo", p)
                s(y1_hi[:, :, PAD:PAD + NODES], pB[2][:].rearrange("p (g n) -> p g n", g=2), ACT.Relu,
                  scale=s1_c[:, 0:1], bias=o1_c[:, 0:1]).then_inc(done["y1_hi"], 1)
                s(y1_full[:], pB[2][:], ACT.Relu, scale=s1_c[:, 0:1], bias=o1_c[:, 0:1]).then_inc(done["y1_full"], 1)

            def dist_squares(p):
                act.wait_ge(done["se_mm"], p + 1)
                before(act, "dist_mm", p, 2)
                s(dl[32:35, :], pB[1][32:35, :], ACT.Square, bias=bse_c[32:35, 0:1])
                s(dr[64:67, :], pB[1][64:67, :], ACT.Square, bias=bse_c[64:67, 0:1]).then_inc(done["dl"], 1)

            def exp1(p):
                before(act, "nmp_mm", p)
                for g in range(2):
                    act.wait_ge(done["dist_mm"], 2 * p + g + 1)
                    s(ex1[:, g, :], pB[1 + g][:], ACT.Exp).then_inc(done["ex1"], 1)

            def exp_table(p):
                s(table_tick[:, 1:2], ones[:, 0:1], ACT.Exp)

            def silu_table(p):
                s(table_tick[:, 0:1], ones[:, 0:1], ACT.Silu)

            def nmp_high(p):
                act.wait_ge(done["nmp_mm"], p + 1)
                before(act, "z_mm", p)
                s(nm_hi[:], pB[1][:], ACT.Copy).then_inc(done["nm_hi"], 1)

            def conv_high(p):
                act.wait_ge(done["conv2_mm"], p + 1)
                before(act, "z_mm", p)
                before(act, "xc_lo", p)
                s(xc_hi[:], pB[0][:], ACT.Relu, bias=o2_c[:, 0:1]).then_inc(done["xc_hi"], 1)
                s(xc_full[:], pB[0][:], ACT.Relu, bias=o2_c[:, 0:1]).then_inc(done["xc_full"], 1)

            def gate_h(p):
                act.wait_ge(done["ghn_mm"], p + 1)
                before(act, "gm1", p)
                s(gh[:], pB[1][:], ACT.Identity, scale=0.5, bias=bhn_c[:, 0:1]).then_inc(done["gh"], 1)

            def gate_r(p):
                act.wait_ge(done["r_mm"], p + 1)
                before(act, "gm1", p)
                s(tr[:], pB[2][:], ACT.Tanh, scale=0.5, bias=brz_c[:, 0:1]).then_inc(done["tr"], 1)

            def gate_n(p):
                act.wait_ge(done["gm"], p + 1)
                before(act, "go", p)
                s(gn[:], gm[:], ACT.Tanh, bias=bih_c[:, 2:3]).then_inc(done["gn"], 1)

            def gate_z(p):
                act.wait_ge(done["z_mm"], p + 1)
                before(act, "ge", p)
                s(tz[:], pB[0][:], ACT.Tanh, scale=0.5, bias=brz_c[:, 1:2]).then_inc(done["tz"], 1)

            def t1_copy(p):
                act.wait_ge(done["t1_mm"], p + 1)
                before(act, "hid_mm", p)
                s(t1[:], pC[:, 0:NS], ACT.Copy).then_inc(done["t1"], 1)

            def y_copy(p):
                act.wait_ge(done["y_mm"], p + 1)
                before(act, "y_tr", p)
                s(yT[:], pC[:, 0:NS], ACT.Copy).then_inc(done["yT"], 1)

            def ys_copy(p):
                act.wait_ge(done["y_tr"], p + 1)
                before(act, "z2_mm", p)
                s(ys[0:NS, :], pC[0:NS, 0:P], ACT.Copy).then_inc(done["ys"], 1)

            def h4_out(p):
                act.wait_ge(done["h4_tr"], p + 1)
                before(act, "e_mm", p, 2)
                s(h4T[:], pD[0][:], ACT.Relu).then_inc(done["h4T"], 1)

            def exp3(p):
                act.wait_ge(done["fcol"], p + 1)
                before(act, "u3_mm", p)
                for g in range(2):
                    act.wait_ge(done["e_mm"], 2 * p + g + 1)
                    for mt in range(TILES):
                        s(ex3[:, g, mt * NODES:(mt + 1) * NODES], pD[g][:, 0:NODES], ACT.Exp,
                          bias=fcol[:, g * TILES + mt:g * TILES + mt + 1]).then_inc(done["ex3"], 1)

            def turn(l, a, b, c, d):
                def L(step, *args):
                    if l is not None:
                        step(l, *args)

                def A(step, *args):
                    if a is not None:
                        step(a, *args)

                def B(step, *args):
                    if b is not None:
                        step(b, *args)

                def C(step, *args):
                    if c is not None:
                        step(c, *args)

                def D(step, *args):
                    if d is not None:
                        step(d, *args)

                D(h4_out)
                A(agg_high)
                D(exp_table)
                B(h2_high)
                B(dist_squares)
                B(conv1_out)
                D(exp3)
                A(squares)
                B(exp1)
                A(silu_table)
                C(t1_copy)
                A(silu)
                B(nmp_high)
                C(y_copy)
                C(ys_copy)
                B(gate_h)
                L(norm1_apply)
                L(adjT_out)
                B(conv_high)
                B(gate_r)
                B(gate_n)
                B(gate_z)

            turns(act, turn, {0: start1})

        @block.gpsimd
        def _(pool):
            g_ = nc.gpsimd
            g_.memset(jadj[:], 0.0)
            g_.memset(xj[:], 0.0)
            g_.memset(ones[:], 1.0).then_inc(pool_mem, 1)
            pool.wait_ge(pool_mem, 1)
            g_.memset(epsln[:], LN_EPS)
            g_.memset(epsrms[:], RMS_EPS * HID0)
            g_.memset(mhalf[:], -0.5).then_inc(pool_ready, 1)
            g_.memset(y1_hi[:].bitcast(F32), 0.0)
            g_.memset(y1_lo[:].bitcast(F32), 0.0)
            g_.memset(dl[:], 0.0)
            g_.memset(dr[:], 0.0)
            g_.memset(hx[:], 1.0).then_inc(pool_mem, 1)
            pool.wait_ge(pool_mem, 2)
            g_.memset(dl[64:67, :], -0.5).then_inc(pool_mem, 1)
            pool.wait_ge(pool_mem, 3)
            g_.memset(dr[32:35, :], -0.5).then_inc(pool_mem, 1)
            pool.wait_ge(pool_mem, 4)

            def start1():
                g_.tensor_scalar(bnw[:, 0:1], bn1_c[:, 3:4], BN_EPS, None, ALU.add)
                g_.tensor_scalar(bnw[:, 1:2], bn2_c[:, 3:4], BN_EPS, None, ALU.add).then_inc(pool_mem, 1)
                pool.wait_ge(pool_mem, 5)
                g_.tensor_tensor(bnw[:, 0:2], bnw[:, 0:2], mhalf[:, 0:2], ALU.pow).then_inc(bn_roots, 1)
                g_.tensor_scalar(b3rep[:], ones[:], b3_c[:, 0:1], None, ALU.mult)
                g_.tensor_tensor(a12_c[:], a3_c[:, 0:1], a3_c[:, 1:2], ALU.add).then_inc(prep_g, 1)
                pool.wait_ge(conv2_in, 16)
                pool.wait_ge(s2_out, 1)
                taps = raw_c2.rearrange("p (k d) -> p k d", d=D)
                row = s2_row[:].rearrange("p (a d) -> p a d", a=1).broadcast_to([P, TAPS, D])
                g_.tensor_tensor(taps, taps, row, ALU.mult).then_inc(conv2_scaled, 1)

            pool.wait_ge(first_loaded, 16 * len(first_weights))

            def rstd(p, k):
                n = JOINTS if k == "3" else P
                qs = slice(0, Q, 2) if k == "3" else slice(0, Q)
                pool.wait_ge(done["mean" + k], p + 1)
                g_.tensor_tensor(ln_ve[k][0:n, qs], ln_mv[k][0:n, qs, 1], epsln[0:n, qs], ALU.add).then_inc(done["ve" + k], 1)
                pool.wait_ge(done["ve" + k], p + 1)
                g_.tensor_tensor(ln_rs[k][0:n, qs], ln_ve[k][0:n, qs], mhalf[0:n, qs], ALU.pow).then_inc(done["rstd" + k], 1)

            def adj_eps(p):
                at_first(pool, p, prep0)
                pool.wait_ge(done["adjT"], 2 * (p + 1))
                before(pool, "agg_mm", p)
                for g in range(2):
                    for t in range(TILES):
                        i = g_.tensor_tensor(adjE[:, g * TILES + t, :], adjT(p, g, t * NODES + t * P, P), epsI[:], ALU.add)
                i.then_inc(done["adjE"], 1)

            def x_bias(p):
                pool.wait_ge(done["h1"], p + 1)
                row = b2_r[:].rearrange("p (a d) -> p a d", a=1).broadcast_to([P, Q, D])
                xp = x_pair(p).rearrange("p (q d) -> p q d", d=D)
                g_.tensor_tensor(xp, xp, row, ALU.add).then_inc(done["x_b2"], 1)

            def rms(p):
                pool.wait_ge(done["hsq"], Q * (p + 1))
                g_.tensor_tensor(sve[:], ssq[:], epsrms[:], ALU.add).then_inc(done["sve"], 1)
                pool.wait_ge(done["sve"], p + 1)
                g_.tensor_tensor(srs[:], sve[:], mhalf[:, 0:Q], ALU.pow).then_inc(done["srs"], 1)

            def degree_root(p):
                pool.wait_ge(done["dgz"], 3 * (p + 1))
                g_.tensor_tensor(dpow[0:NS, :], dsafe[0:NS, :], mhalf[0:NS, 0:1], ALU.pow).then_inc(done["dpw"], 1)

            def turn(l, a, b, c, d):
                def L(step, *args):
                    if l is not None:
                        step(l, *args)

                def A(step, *args):
                    if a is not None:
                        step(a, *args)

                def B(step, *args):
                    if b is not None:
                        step(b, *args)

                def C(step, *args):
                    if c is not None:
                        step(c, *args)

                def D(step, *args):
                    if d is not None:
                        step(d, *args)

                A(x_bias)
                C(rstd, "3")
                C(degree_root)
                A(rms)
                L(rstd, "1")
                C(rstd, "4")
                A(rstd, "2")
                L(adj_eps)

            turns(pool, turn, {0: start1})


def kernel(**inputs):
    import numpy as np
    import concourse.bacc as bacc
    from concourse.bass_utils import run_bass_kernel_spmd

    f = {k: np.asarray(v) for k, v in inputs.items()}
    consts = np.zeros((P, K_COLS), np.float32)
    consts[:, K_IDENT:K_IDENT + P] = np.eye(P)
    for i, (g, a, n) in enumerate(STACK):
        consts[32 * a + n, K_SEL + i] = 1
        consts[i, K_BACK + 32 * a + n] = 1
        consts[i, K_GRP + g] = 1
        for j, (g2, a2, _) in enumerate(STACK):
            consts[i, K_SAME + j] = g == g2 and a == a2
    L0, L1, L2, L3 = "L0_gnn_", "L1_gnn_", "L2_gnn_", "L3_gnn_"
    bn1, bn2 = (np.stack([f[L1 + bn + k] for k in "gbmv"]) for bn in ("bn1_", "bn2_"))
    w_se, b_se = np.zeros((D, P), np.float32), np.zeros((P, 1), np.float32)
    for k in range(3):
        w_se[:, 32 * k:32 * k + 3] = f[L1 + "w_se"].T
        b_se[32 * k:32 * k + 3, 0] = f[L1 + "b_se"]
    vectors = {"rms_w": f[L0 + "rms_weight"].reshape(C0, P).T, "bn1": bn1.T, "bn2": bn2.T,
               "b_ih": f[L1 + "b_ih"].reshape(3, P).T, "b_hh": f[L1 + "b_hh"].reshape(3, P).T,
               "l2_b1": f[L2 + "b1"].reshape(NG * C2, P).T, "b3": f[L3 + "W_b"].reshape(P, 1),
               "a3": f[L3 + "a_w"].reshape(2, P).T, "b_se": b_se}
    laid = [
        f["x"], f["adj"], f[L0 + "epsilon"].reshape(1), f[L0 + "W1"], f[L0 + "b1"], f[L0 + "W2"],
        f[L0 + "b2"], w_se, f[L1 + "conv1_w"][:, :, 0].T,
        f[L1 + "conv2_w"].transpose(1, 2, 0).reshape(D, TAPS * D), f[L1 + "w_msg"].T, f[L1 + "b_msg"],
        f[L1 + "w_ih"].T, f[L1 + "w_hh"].T, f[L2 + "W1"], f[L2 + "W2"], f[L2 + "b2"],
        f[L2 + "fusion_w"], f[L3 + "W_w"], f[L3 + "W_w"].T, f[L3 + "W_b"], f[L3 + "a_b"], consts,
        np.concatenate([vectors[k] for k in VECTORS], 1),
    ]
    nc = bacc.Bacc("TRN2", target_bir_lowering=False, num_devices=1)
    arrays, args = {}, []
    for i, a in enumerate(laid):
        a = np.ascontiguousarray(a)
        arrays[f"in_{i}_dram"] = a
        args.append(nc.dram_tensor(f"in_{i}_dram", a.shape, mybir.dt.from_np(a.dtype), kind="ExternalInput").ap())
    args.append(nc.dram_tensor("out_dram", (GRAPHS, NODES, D), F32, kind="ExternalOutput").ap())
    build(nc, *args)
    r = run_bass_kernel_spmd(nc, [arrays], core_ids=[0])
    return r.results[0]["out_dram"]
```

```python
from contextlib import ExitStack

import concourse.bass as bass
from concourse import mybir

F32 = mybir.dt.float32
F32R = mybir.dt.float32r
ACT = mybir.ActivationFunctionType
ALU = mybir.AluOpType
AX = mybir.AxisListType

GRAPHS, NODES, D = 32, 256, 128
P = 128
TILES = NODES // P
PAIRS = GRAPHS // 2
X_RING = 8
RING = 5
Q = 2 * TILES
W = 2 * NODES
HID0 = 512
C0 = HID0 // P
TAPS, PAD = 17, 8
HALF, HALO = NODES // 2, PAD // 2
ODD_N = HALF + 2
PADH = HALF + 2 * HALO + 2
E_TAPS = TAPS // 2 + 1
GROUPS = [list(range(25)), [0, 1, 2, 3, 4, 5, 6, 7, 8], [0, 9, 10, 11, 12, 13, 14], [6, 7, 8, 12, 13, 14],
          [3, 4, 5, 9, 10, 11]]
NG = len(GROUPS)
JOINTS = 25
HID2 = 256
C2 = HID2 // P
STACK = [(g, a, n) for g, nodes in enumerate(GROUPS) for a in range(2) for n in nodes]
NS = len(STACK)
G_START = [min(i for i, s in enumerate(STACK) if s[0] == g) for g in range(NG)]
G_SIZE = [2 * len(nodes) for nodes in GROUPS]
JP = 32 + JOINTS
SQ_P, CROSS, SQ_Q = 0, 64, 96
DIMS = 3
K_DIST = SQ_Q + 2 * DIMS
K_IDENT, K_SEL, K_SAME, K_BACK, K_GRP = 0, P, P + NS, P + 2 * NS, P + 2 * NS + 64
K_COLS = K_GRP + NG
VECTORS = {"rms_w": C0, "bn1": 4, "bn2": 4, "b_ih": 3, "b_hh": 3, "l2_b1": NG * C2, "b3": 1, "a3": 2, "b_se": 1, "minus_lo": 2}
V_AT = {k: sum(list(VECTORS.values())[:i]) for i, k in enumerate(VECTORS)}
V_COLS = sum(VECTORS.values())
LN_EPS, RMS_EPS, BN_EPS = 1e-5, 1e-6, 1e-5


def build(nc, x, adj, eps0, w1, b1, w2, b2, w_seT, conv1T, conv2T, w_msgT, b_msg, w_ihT, w_hhT,
          l2_w1, l2_w2, l2_b2, fusion, w3, w3T, b3, ab3, consts, vectors, out):
    with ExitStack() as ctx:
        def sb(name, shape, dt=F32):
            return ctx.enter_context(nc.sbuf_tensor(name, shape, dt))

        def sem(name):
            return ctx.enter_context(nc.semaphore(name))

        def pair_of(name, shape):
            return sb(name + "_hi", shape, F32R), sb(name + "_lo", shape, F32R)

        x_all = sb("x_all", [P, X_RING * W])
        adjT_all = sb("adjT_all", [P, RING * 2 * W])

        kst = sb("kst", [P, K_COLS])
        ident, sel = kst[:, K_IDENT:K_IDENT + P], kst[0:JP, K_SEL:K_SEL + NS]
        same = kst[0:NS, K_SAME:K_SAME + NS]
        grp = kst[0:NS, K_GRP:K_GRP + NG]
        eps_c = sb("eps_c", [P, 1])
        epsI = sb("epsI", [P, P])
        w1_hi, w1_lo = pair_of("w1", [P, HID0])
        w2_s = sb("w2_s", [P, C0, D])
        b1_r = sb("b1_r", [P, HID0])
        b2_r = sb("b2_r", [P, D])
        vec = sb("vec", [P, V_COLS])

        def vector(name):
            return vec[:, V_AT[name]:V_AT[name] + VECTORS[name]]

        rmsw_c, bn1_c, bn2_c, bih_c, bhh_c = (vector(n) for n in ("rms_w", "bn1", "bn2", "b_ih", "b_hh"))
        vb1_c = vector("l2_b1").rearrange("p (g c) -> p g c", g=NG)
        b3_c, a3_c, bse_c = vector("b3"), vector("a3"), vector("b_se")
        minus_lo = vector("minus_lo")
        c1_hi, c1_lo = pair_of("c1", [P, D])
        c2_hi, c2_lo = pair_of("c2", [P, TAPS * D])
        cs_hi, cs_lo = pair_of("cs", [P, (E_TAPS - 1) * D])
        s2rep, s2_row = sb("s2rep", [P, P]), sb("s2_row", [P, D])
        s1_c, o1_c, s2_c, o2_c = (sb(n, [P, 1]) for n in ("s1_c", "o1_c", "s2_c", "o2_c"))
        bnw = sb("bnw", [P, 4])
        wse_raw = sb("wse_raw", [P, P])
        se_hi, se_lo = pair_of("se", [P, P])
        wmsg_s = sb("wmsg_s", [P, D])
        bmsg_r = sb("bmsg_r", [P, D])
        ih_hi, ih_lo = pair_of("ih", [P, 2, 3 * D])
        hh_hi, hh_lo = pair_of("hh", [P, 3 * D])
        brz_c, bhn_c = sb("brz_c", [P, 2]), sb("bhn_c", [P, 1])
        v1_s = sb("v1_s", [P, NG, HID2])
        v2_s = sb("v2_s", [P, NG, C2, D])
        hb_m = sb("hb_m", [P, C2, NS])
        zb_m = sb("zb_m", [NS, D])
        fw = sb("fw", [P, NG])
        fwm, fws, nw_row = sb("fwm", [P, 1]), sb("fws", [P, 1]), sb("nw_row", [P, 1])
        fwe = sb("fwe", [P, NG])
        w3_raw = sb("w3_raw", [P, D])
        w3x = sb("w3x", [P, D + 1])
        b3_r, b3rep = sb("b3_r", [P, D]), sb("b3rep", [P, P])
        a12_c, ab_c, v1col = sb("a12_c", [P, 1]), sb("ab_c", [P, 1]), sb("v1col", [P, 1])
        e_rep = sb("e_rep", [P, P])
        fconst = sb("fconst", [P, 1])
        mhalf = sb("mhalf", [P, Q])
        ones = sb("ones", [P, P])
        epsln, epsrms = sb("epsln", [P, Q]), sb("epsrms", [P, Q])
        table_tick = sb("table_tick", [P, 2])
        tick = sb("tick", [P, 8])

        adj_s = sb("adj_s", [P, Q, NODES])
        adjE = sb("adjE", [P, Q, P])
        ln_st = {k: sb("st" + k, [P, Q, 6]) for k in "1234"}
        ln_mv = {k: sb("mv" + k, [P, Q, 2]) for k in "1234"}
        ln_ve = {k: sb("ve" + k, [P, Q]) for k in "1234"}
        ln_rs = {k: sb("rs" + k, [P, Q]) for k in "1234"}
        h1, nb1 = sb("h1", [P, W]), sb("nb1", [P, Q])
        ag_hi, ag_lo = pair_of("ag", [P, W])
        hb = sb("hb", [P, Q, HID0])
        hsq = sb("hsq", [P, HID0], mybir.dt.bfloat16)
        ssq, sve, srs = sb("ssq", [P, Q]), sb("sve", [P, Q]), sb("srs", [P, Q])
        xn2 = sb("xn2", [P, W])
        h2_hi, h2_lo = pair_of("h2", [P, W])
        h2_full = sb("h2_full", [P, W])
        y1_hi, y1_lo = pair_of("y1", [P, 2, 2, PADH])
        y1_full = sb("y1_full", [P, 2, 2, PADH])
        xs_hi, xs_lo = pair_of("xs", [P, 2, PADH])
        xs_full = sb("xs_full", [P, 2, PADH])
        odd_s = sb("odd_s", [P, 2, ODD_N])
        ds_x, ds_hi = sb("ds_x", [P, W]), sb("ds_hi", [P, W], F32R)
        dl, dr = sb("dl", [P, W], F32R), sb("dr", [P, W], F32R)
        ex1 = sb("ex1", [P, 2, W])
        msg = sb("msg", [P, W])
        nm_hi, nm_lo = pair_of("nm", [P, W])
        xc_hi, xc_lo = pair_of("xc", [P, W])
        xc_sum = sb("xc_sum", [P, W])
        tr, tz, gh, gm, gn, go = (sb(n, [P, W]) for n in ("tr", "tz", "gh", "gm", "gn", "go"))
        gd = gm
        msg_t = go
        jadj = sb("jadj", [P, P])
        jq = sb("jq", [P, NS])
        nmat, nsc, nT = sb("nmat", [P, NS]), sb("nsc", [P, NS]), sb("nT", [P, NS])
        deg, isz, dsafe, dpow, dinv = (sb(n, [P, 1]) for n in ("deg", "isz", "dsafe", "dpow", "dinv"))
        xj = sb("xj", [P, D])
        xs, t1, hid = sb("xs", [P, D]), sb("t1", [P, NS]), sb("hid", [P, C2, NS])
        hidr = sb("hidr", [P, C2, NS])
        yT, ys, zb, zr = sb("yT", [P, NS]), sb("ys", [P, D]), sb("zb", [P, D]), sb("zr", [P, D])
        xn4, h4T = sb("xn4", [P, W]), sb("h4T", [P, W])
        hx = sb("hx", [P, Q, D + 1])
        fcol = sb("fcol", [P, Q])
        ex3 = sb("ex3", [P, 2, W])
        rec = sb("rec", [P, Q])

        pA = [ctx.enter_context(nc.psum_tensor(f"pA{k}", [P, W], F32)) for k in range(2)]
        pB = [ctx.enter_context(nc.psum_tensor(f"pB{k}", [P, W], F32)) for k in range(3)]
        pC = ctx.enter_context(nc.psum_tensor("pC", [P, W], F32))
        pD = [ctx.enter_context(nc.psum_tensor(f"pD{k}", [P, W], F32)) for k in range(2)]

        names = """adj_loaded jadj_loaded x_loaded stored adj_transposed adjT adjE
            stats1 mean1 ve1 rstd1 h1 agg_mm agg_hi agg_lo w1_mm hb hsq sve srs u0 u_tr sT w2_mm x_b2 x1
            stats2 mean2 ve2 rstd2 xn2 h2_tr h2_hi h2_lo h2_full nb1 conv1_mm y1_hi y1_full y1_lo xs_full xs_hi xs_lo se_mm ds_cross ds_sq ds_hi dr dist_mm ex1 amask1
            msg_mm msg_t msg nmp_mm nm_hi nm_lo odd_mm odd_s xc_base xc_even conv2_mm xc_sum xc_hi xc_lo r_mm tr ghn_mm gh gm1 gin_mm gm gn
            z_mm tz gd ge go go_tr x2
            jq_mm jq n0_mm nmask nmat dgz dsf dpw dinv nsc n_tr nT stats3 mean3 ve3 rstd3 xn3 xj xs_mm xs t1_mm t1
            hid_mm hid hidr y_mm yT y_tr ys z2_mm zb zr fus_mm x3
            stats4 mean4 ve4 rstd4 xn4 h4_tr h4T hx fcol e_mm ex3 u3 u3_mm rec x4""".split()
        done = {n: sem(n) for n in names}
        first_loaded, loaded = sem("first_weights_loaded"), sem("weights_loaded")
        prep0, bn_roots, prep1, prep_gates = sem("prep0"), sem("bn_roots"), sem("prep1"), sem("prep_gates")
        s2_spread, s2_mm, s2_out = sem("s2_spread"), sem("s2_mm"), sem("s2_out")
        conv2_scaled, conv2_hi, conv2_lo = sem("conv2_scaled"), sem("conv2_hi"), sem("conv2_lo")
        prep_g, consts3_mm, prep3 = sem("prep_g"), sem("consts3_mm"), sem("prep3")
        pool_ready = sem("pool_ready")
        weights = []

        def bc(src, n=P):
            return src.rearrange("(a c) -> a c", a=1).broadcast_to([n, src.shape[0]])

        first_weights = [(kst[:], consts), (eps_c[:], bc(eps0)), (vec[:], vectors), (b1_r[:], bc(b1)), (b2_r[:], bc(b2)),
                         (w2_s[:], w2.rearrange("(c p) d -> p c d", p=P))]
        weights += [(wse_raw[:], w_seT), (wmsg_s[:], w_msgT), (bmsg_r[:], bc(b_msg)),
                    (v1_s[:], l2_w1.rearrange("g d h -> d g h")), (v2_s[:], l2_w2.rearrange("g (c p) d -> p g c d", p=P)),
                    (fw[:], bc(fusion)), (w3_raw[:], w3), (w3x[:, 0:D], w3T), (b3_r[:], bc(b3)), (ab_c[:], bc(ab3))]
        weights += [(zb_m[G_START[g]:G_START[g] + G_SIZE[g], :], bc(l2_b2[g], G_SIZE[g])) for g in range(NG)]
        x_free, adjT_free = 5 * W, 2 * (2 * W)
        raw_w1, raw_ih = x_all[:, x_free:x_free + HID0], x_all[:, x_free + HID0:x_free + HID0 + 6 * D]
        raw_c2 = adjT_all[:, adjT_free:adjT_free + TAPS * D]
        raw_c1 = adjT_all[:, adjT_free + TAPS * D:adjT_free + (TAPS + 1) * D]
        raw_hh = adjT_all[:, adjT_free + (TAPS + 1) * D:adjT_free + (TAPS + 4) * D]
        raw_cs = x_all[:, x_free - (E_TAPS - 1) * D:x_free]
        assert HID0 + 6 * D <= 3 * W and (TAPS + 4) * D <= 3 * 2 * W
        w1_in, split_in, conv2_in = sem("w1_in"), sem("split_in"), sem("conv2_in")
        link_sem, fw_exp, pool_mem = sem("link"), sem("fw_exp"), sem("pool_mem")

        def is_first(p):
            return isinstance(p, int) and p == 0

        def by_parity(t):
            return t[:].rearrange("p (g i r) -> p r g i", g=2, r=2)

        def x_tile(p, q):
            s = (p % X_RING) * W + q * P
            return x_all[:, bass.ds(s, P)] if not isinstance(p, int) else x_all[:, s:s + P]

        def x_pair(p):
            s = (p % X_RING) * W
            return x_all[:, bass.ds(s, W)] if not isinstance(p, int) else x_all[:, s:s + W]

        def adjT(p, g, at=0, n=W):
            s = (p % RING) * (2 * W) + (g * W + at)
            return adjT_all[:, bass.ds(s, n)] if not isinstance(p, int) else adjT_all[:, s:s + n]

        def turns(eng, turn, after={}):
            for t in range(5):
                turn(t, *(t - k if t >= k else None for k in range(1, 5)))
                if t in after:
                    after[t]()
            with eng.Fori(5, PAIRS) as t:
                turn(t, t - 1, t - 2, t - 3, t - 4)
            for t in range(PAIRS, PAIRS + 4):
                turn(None, *(t - k if t - k < PAIRS else None for k in range(1, 5)))

        def before(eng, name, p, per=1):
            if not is_first(p):
                eng.wait_ge(done[name], p * per)

        def at_first(eng, p, signal, n=1):
            if is_first(p):
                eng.wait_ge(signal, n)

        block = ctx.enter_context(nc.Block())

        @block.sync
        def _(sp):
            sp.dma_start(adj_s[:], adj[0:2].rearrange("b (t p) m -> p (b t) m", p=P)).then_inc(done["adj_loaded"], 16)
            sp.dma_start(x_all[:, 0:W].rearrange("p (q d) -> p q d", d=D),
                         x[0:2].rearrange("b (t p) d -> p (b t) d", p=P)).then_inc(done["x_loaded"], 16)
            for dst, src in first_weights[:3]:
                sp.dma_start(dst, src).then_inc(first_loaded, 16)
            sp.dma_start(raw_w1, w1).then_inc(w1_in, 16)
            for dst, src in first_weights[3:]:
                sp.dma_start(dst, src).then_inc(first_loaded, 16)
            sp.dma_start(raw_c1, conv1T).then_inc(split_in, 16)
            sp.dma_start(raw_hh, w_hhT).then_inc(split_in, 16)
            sp.dma_start(raw_ih.rearrange("p (k n) -> p k n", k=2),
                         w_ihT.rearrange("(k p) n -> p k n", p=P)).then_inc(split_in, 16)
            sp.dma_start(raw_c2, conv2T).then_inc(conv2_in, 16)
            for dst, src in weights:
                sp.dma_start(dst, src).then_inc(loaded, 16)

            def load_x(p):
                before(sp, "stats1", p)
                sp.dma_start(x_pair(p).rearrange("p (q d) -> p q d", d=D),
                             x[bass.ds(p * 2, 2)].rearrange("b (t p) d -> p (b t) d", p=P)
                             ).then_inc(done["x_loaded"], 16)

            def load_adj(p):
                before(sp, "adj_transposed", p, 2)
                sp.dma_start(adj_s[:], adj[bass.ds(p * 2, 2)].rearrange("b (t p) m -> p (b t) m", p=P)
                             ).then_inc(done["adj_loaded"], 16)

            def load_joints(p):
                before(sp, "jq_mm", p)
                for a in range(2):
                    sp.dma_start(jadj[32 * a:32 * a + JOINTS, 32 * a:32 * a + JOINTS],
                                 adj[bass.ds(p * 2 + a, 1), 0:JOINTS, 0:JOINTS].rearrange("b n m -> (b n) m")
                                 ).then_inc(done["jadj_loaded"], 16)

            def store(p):
                at = (p % X_RING) * W
                at = at if isinstance(p, int) else sp.snap(at)
                sp.wait_ge(done["x4"], p + 1)
                before(sp, "stored", p, 16)
                sp.dma_start(out[bass.ds(p * 2, 2)].rearrange("b (t p) d -> p (b t) d", p=P),
                             x_all[:, bass.ds(at, W)].rearrange("p (q d) -> p q d", d=D)).then_inc(done["stored"], 16)

            sp.wait_ge(pool_ready, 1)
            load_joints(0)
            for t in range(1, 5):
                load_x(t)
                load_adj(t)
            load_joints(1)
            load_joints(2)
            with sp.Fori(5, PAIRS) as t:
                load_x(t)
                load_adj(t)
                store(t - 5)
                load_joints(t - 2)
            store(PAIRS - 5)
            load_joints(PAIRS - 2)
            store(PAIRS - 4)
            load_joints(PAIRS - 1)
            for p in range(PAIRS - 3, PAIRS):
                store(p)
            sp.wait_ge(done["stored"], 16 * PAIRS)

        @block.tensor
        def _(pe):
            mm = nc.tensor.matmul

            def three(o, w_hi, w_lo, m_hi, m_lo, start, stop):
                mm(o, w_hi, m_hi, start=start, stop=False)
                mm(o, w_hi, m_lo, start=False, stop=False)
                return mm(o, w_lo, m_hi, start=False, stop=stop)

            def bn2_row(p):
                if is_first(p):
                    pe.wait_ge(s2_spread, 1)
                    mm(pC[:, 0:D], s2rep[:], ident, start=True, stop=True).then_inc(s2_mm, 1)

            def constants3():
                pe.wait_ge(s2_out, 1)
                pe.wait_ge(loaded, 16 * len(weights))
                mm(pC[:, 0:2], w3_raw[:], a3_c[:], start=True, stop=True)
                pe.wait_ge(prep_g, 1)
                mm(pC[:, 2:3], b3rep[:], a12_c[:], start=True, stop=True).then_inc(consts3_mm, 1)

            pe.wait_ge(first_loaded, 16 * len(first_weights))

            def adj_transposes(p, g):
                if g == 0:
                    pe.wait_ge(done["adj_loaded"], (p + 1) * 16)
                    before(pe, "sT", p, C0)
                else:
                    pe.wait_ge(done["adjT"], 2 * p + 1)
                for mt in range(TILES):
                    for nt in range(TILES):
                        o = mt * NODES + nt * P
                        i = nc.tensor.transpose(pA[0][:, o:o + P], adj_s[:, g * TILES + nt, mt * P:mt * P + P], ident)
                i.then_inc(done["adj_transposed"], 1)

            def aggregate(p):
                pe.wait_ge(done["adjT"], 2 * (p + 1))
                pe.wait_ge(done["adjE"], p + 1)
                pe.wait_ge(done["h1"], p + 1)
                for g in range(2):
                    for nt in range(TILES):
                        o = pA[0][:, g * NODES + nt * P:g * NODES + nt * P + P]
                        for mt in range(TILES):
                            q = g * TILES + mt
                            rhs = adjE[:, q, :] if mt == nt else adjT(p, g, mt * NODES + nt * P, P)
                            i = mm(o, h1[:, q * P:q * P + P], rhs, start=(mt == 0), stop=(mt == TILES - 1))
                i.then_inc(done["agg_mm"], 1)

            def hidden0(p, *tiles):
                for q in tiles:
                    if q == 0:
                        at_first(pe, p, prep0)
                        pe.wait_ge(done["agg_hi"], p + 1)
                        pe.wait_ge(done["agg_lo"], p + 1)
                        before(pe, "x1", p)
                    if q >= 2:
                        pe.wait_ge(done["hb"], Q * p + q - 1)
                    t = slice(q * P, q * P + P)
                    three(pA[1 - q % 2][:], ag_hi[:, t], ag_lo[:, t], w1_hi[:], w1_lo[:], True, True
                          ).then_inc(done["w1_mm"], 1)

            def hidden0_transposes(p, *chunks):
                for c in chunks:
                    if c == 0:
                        pe.wait_ge(done["hb"], Q * (p + 1))
                        pe.wait_ge(done["u0"], p + 1)
                    if c >= 2:
                        pe.wait_ge(done["sT"], C0 * p + c - 1)
                    for q in range(Q):
                        i = nc.tensor.transpose(pA[1 - c % 2][:, q * P:q * P + P], hb[:, q, c * P:c * P + P], ident)
                    i.then_inc(done["u_tr"], 1)

            def output0(p, *tiles):
                for q in tiles:
                    if q == 0:
                        pe.wait_ge(done["sT"], C0 * (p + 1))
                    for c in range(C0):
                        i = mm(pA[1][:, q * D:q * D + D], hb[:, q, c * P:c * P + P], w2_s[:, c, :],
                               start=(c == 0), stop=(c == C0 - 1))
                if q == Q - 1:
                    i.then_inc(done["w2_mm"], 1)

            def h2_transposes(p):
                pe.wait_ge(done["xn2"], p + 1)
                before(pe, "gm", p)
                for q in range(Q):
                    i = nc.tensor.transpose(pB[1][:, q * P:q * P + P], xn2[:, q * P:q * P + P], ident)
                i.then_inc(done["h2_tr"], 1)

            def project_dist(p):
                at_first(pe, p, prep1)
                pe.wait_ge(done["h2_hi"], p + 1)
                pe.wait_ge(done["h2_lo"], p + 1)
                three(pB[1][:], se_hi[:], se_lo[:], h2_hi[:], h2_lo[:], True, True).then_inc(done["se_mm"], 1)

            def project_conv(p):
                before(pe, "x2", p)
                three(pB[2][:], c1_hi[:], c1_lo[:], h2_hi[:], h2_lo[:], True, True).then_inc(done["conv1_mm"], 1)

            def project_msg(p):
                pe.wait_ge(done["h2_full"], p + 1)
                pe.wait_ge(done["y1_full"], p + 1)
                for q in range(Q):
                    i = mm(pB[2][:, q * D:q * D + D], h2_full[:, q * P:q * P + P], wmsg_s[:], start=True, stop=True)
                i.then_inc(done["msg_mm"], 1)

            def distances(p, g):
                if g == 0:
                    pe.wait_ge(done["dr"], p + 1)
                else:
                    pe.wait_ge(done["msg_t"], p + 1)
                for mt in range(TILES):
                    m = g * NODES + mt * P
                    i = mm(pB[1 + g][:, mt * NODES:(mt + 1) * NODES], dl[0:K_DIST, m:m + P],
                           dr[0:K_DIST, g * NODES:(g + 1) * NODES], start=True, stop=True)
                i.then_inc(done["dist_mm"], 1)

            def conv2_taps(o, w_hi, w_lo, at, m_hi, m_lo, j, start, stop):
                n = ODD_N if o is odd_o else HALF
                w = slice(at * D, at * D + D)
                return three(o, w_hi[:, w], w_lo[:, w], m_hi[:, :, j:j + n], m_lo[:, :, j:j + n], start, stop)

            odd_o, even_o, sum_o = pB[0][:, 0:2 * ODD_N], pB[0][:, 0:NODES], pB[0][:, NODES:W]

            def conv2_odd(p, *taps):
                for j in taps:
                    if j == 1:
                        at_first(pe, p, conv2_lo)
                        pe.wait_ge(done["y1_lo"], p + 1)
                        before(pe, "tz", p)
                    i = conv2_taps(odd_o, c2_hi, c2_lo, 2 * j - 1, y1_hi[:, 1], y1_lo[:, 1], j - 1, j == 1, j == E_TAPS - 1)
                if j == E_TAPS - 1:
                    i.then_inc(done["odd_mm"], 1)

            def conv2_even(p, *taps):
                for j in taps:
                    if j == 0:
                        pe.wait_ge(done["odd_s"], p + 1)
                    conv2_taps(even_o, c2_hi, c2_lo, 2 * j, y1_hi[:, 0], y1_lo[:, 0], j, j == 0, j == E_TAPS - 1)

            def conv2_sum(p, *taps):
                for j in taps:
                    if j == 0:
                        pe.wait_ge(done["xs_lo"], p + 1)
                    w_hi, w_lo, at = (cs_hi, cs_lo, j - 1) if j else (c2_hi, c2_lo, 0)
                    i = conv2_taps(sum_o, w_hi, w_lo, at, xs_hi, xs_lo, j, j == 0, j == E_TAPS - 1)
                if j == E_TAPS - 1:
                    i.then_inc(done["conv2_mm"], 1)

            def messages(p, *graphs):
                for g in graphs:
                    if g == 0:
                        pe.wait_ge(done["msg"], p + 1)
                        pe.wait_ge(done["ex1"], 2 * (p + 1))
                    pe.wait_ge(done["amask1"], 2 * p + g + 1)
                    for mt in range(TILES):
                        q = g * TILES + mt
                        i = mm(pB[1][:, g * NODES:(g + 1) * NODES], msg[:, q * D:q * D + D],
                               ex1[:, g, mt * NODES:(mt + 1) * NODES], start=(mt == 0), stop=(mt == TILES - 1))
                if g:
                    i.then_inc(done["nmp_mm"], 1)

            def of_h2(o, j, start, stop):
                w = slice(j * D, j * D + D)
                return three(o, hh_hi[:, w], hh_lo[:, w], h2_hi[:], h2_lo[:], start, stop)

            def of_nmp(o, j, start, stop):
                w = slice(j * D, j * D + D)
                return three(o, ih_hi[:, 1, w], ih_lo[:, 1, w], nm_hi[:], nm_lo[:], start, stop)

            def of_conv(o, j, start, stop):
                w = slice(j * D, j * D + D)
                return three(o, ih_hi[:, 0, w], ih_lo[:, 0, w], xc_hi[:], xc_lo[:], start, stop)

            def gate_hn(p):
                at_first(pe, p, prep_gates)
                pe.wait_ge(done["nm_hi"], p + 1)
                pe.wait_ge(done["nm_lo"], p + 1)
                of_h2(pB[1][:], 2, True, True).then_inc(done["ghn_mm"], 1)

            def gates_early(p):
                pe.wait_ge(done["ex1"], 2 * (p + 1))
                of_h2(pB[2][:], 0, True, False)
                of_nmp(pB[2][:], 0, False, False)
                pe.wait_ge(done["gh"], p + 1)
                of_nmp(pB[1][:], 2, True, False)

            def gates_late(p):
                pe.wait_ge(done["xc_hi"], p + 1)
                pe.wait_ge(done["xc_lo"], p + 1)
                of_conv(pB[2][:], 0, False, True).then_inc(done["r_mm"], 1)
                of_conv(pB[1][:], 2, False, True).then_inc(done["gin_mm"], 1)

            def gate_z(p):
                pe.wait_ge(done["xc_sum"], p + 1)
                of_h2(pB[0][:], 1, True, False)
                of_nmp(pB[0][:], 1, False, False)
                of_conv(pB[0][:], 1, False, True).then_inc(done["z_mm"], 1)

            def back_transposes(p):
                pe.wait_ge(done["go"], p + 1)
                pe.wait_ge(done["tr"], p + 1)
                for q in range(Q):
                    i = nc.tensor.transpose(pB[2][:, q * P:q * P + P], go[:, q * P:q * P + P], ident)
                i.then_inc(done["go_tr"], 1)

            def joints_left(p):
                pe.wait_ge(done["jadj_loaded"], (p + 1) * 32)
                before(pe, "x3", p)
                mm(pC[:, 0:NS], jadj[0:JP, :], sel, start=True, stop=True).then_inc(done["jq_mm"], 1)

            def joints_right(p):
                pe.wait_ge(done["jq"], p + 1)
                mm(pC[0:NS, 0:NS], jq[0:JP, :], sel, start=True, stop=True).then_inc(done["n0_mm"], 1)

            def stack_rows(p):
                pe.wait_ge(done["xj"], p + 1)
                pe.wait_ge(done["nmask"], p + 1)
                mm(pC[0:NS, 0:D], sel, xj[0:JP, :], start=True, stop=True).then_inc(done["xs_mm"], 1)

            def norm_transpose(p):
                pe.wait_ge(done["nsc"], p + 1)
                pe.wait_ge(done["xs"], p + 1)
                nc.tensor.transpose(pC[0:NS, 0:NS], nsc[0:NS, :], ident[0:NS, 0:NS]).then_inc(done["n_tr"], 1)

            def spread1(p):
                pe.wait_ge(done["nT"], p + 1)
                mm(pC[:, 0:NS], xs[0:NS, :], nT[0:NS, :], start=True, stop=True).then_inc(done["t1_mm"], 1)

            def hidden2(p, *chunks):
                if chunks[0] == 0:
                    pe.wait_ge(done["t1"], p + 1)
                for c in chunks:
                    for g in range(NG):
                        a, n = G_START[g], G_SIZE[g]
                        i = mm(pC[:, c * NS + a:c * NS + a + n], v1_s[:, g, c * P:c * P + P], t1[:, a:a + n],
                               start=True, stop=True)
                if c == C2 - 1:
                    i.then_inc(done["hid_mm"], 1)

            def output2(p, *groups):
                if groups[0] == 0:
                    pe.wait_ge(done["hidr"], p + 1)
                for g in groups:
                    a, n = G_START[g], G_SIZE[g]
                    for c in range(C2):
                        i = mm(pC[:, a:a + n], v2_s[:, g, c, :], hidr[:, c, a:a + n], start=(c == 0), stop=(c == C2 - 1))
                if g == NG - 1:
                    i.then_inc(done["y_mm"], 1)

            def y_transpose(p):
                pe.wait_ge(done["yT"], p + 1)
                nc.tensor.transpose(pC[0:NS, 0:P], yT[:, :], ident).then_inc(done["y_tr"], 1)

            def spread2(p):
                pe.wait_ge(done["ys"], p + 1)
                mm(pC[0:NS, 0:D], nT[0:NS, :], ys[0:NS, :], start=True, stop=True).then_inc(done["z2_mm"], 1)

            def fuse(p):
                pe.wait_ge(done["zr"], p + 1)
                for a in range(2):
                    back = kst[0:NS, K_BACK + 32 * a:K_BACK + 32 * a + 32]
                    i = mm(pC[0:32, a * D:a * D + D], back, zr[0:NS, :], start=True, stop=True)
                i.then_inc(done["fus_mm"], 1)

            def h4_transposes(p):
                pe.wait_ge(done["xn4"], p + 1)
                before(pe, "x4", p)
                for q in range(Q):
                    i = nc.tensor.transpose(pD[0][:, q * P:q * P + P], xn4[:, q * P:q * P + P], ident)
                i.then_inc(done["h4_tr"], 1)

            def project3(p, g):
                if g == 0:
                    at_first(pe, p, prep3)
                    pe.wait_ge(done["h4T"], p + 1)
                    for q in range(Q):
                        o = pD[1][:, q * (D + 1):(q + 1) * (D + 1)] if q < Q - 1 else pD[0][:, NODES:NODES + D + 1]
                        mm(o, h4T[:, q * P:q * P + P], w3x[:], start=True, stop=True)
                else:
                    pe.wait_ge(done["hx"], p + 1)
                mm(pD[g][:, 0:NODES], e_rep[:], h4T[:, g * NODES:(g + 1) * NODES], start=True, stop=True
                   ).then_inc(done["e_mm"], 1)

            def attend(p, *graphs):
                for g in graphs:
                    if g == 0:
                        pe.wait_ge(done["hx"], p + 1)
                    pe.wait_ge(done["u3"], 2 * p + g + 1)
                    for nt in range(TILES):
                        for mt in range(TILES):
                            m = mt * NODES + nt * P
                            i = mm(pD[g][:, nt * (D + 1):(nt + 1) * (D + 1)], ex3[:, g, m:m + P],
                                   hx[:, g * TILES + mt, :], start=(mt == 0), stop=(mt == TILES - 1))
                if g:
                    i.then_inc(done["u3_mm"], 1)

            def turn(l, a, b, c, d):
                def L(step, *args):
                    if l is not None:
                        step(l, *args)

                def A(step, *args):
                    if a is not None:
                        step(a, *args)

                def B(step, *args):
                    if b is not None:
                        step(b, *args)

                def C(step, *args):
                    if c is not None:
                        step(c, *args)

                def D(step, *args):
                    if d is not None:
                        step(d, *args)

                A(bn2_row)
                B(h2_transposes)
                C(joints_left)
                A(aggregate)
                D(h4_transposes)
                C(back_transposes)
                B(project_dist)
                A(hidden0, 0, 1)
                B(project_conv)
                A(hidden0, 2, 3)
                D(project3, 0)
                B(distances, 0)
                B(project_msg)
                B(conv2_odd, 1, 2, 3, 4, 5, 6, 7, 8)
                C(joints_right)
                D(project3, 1)
                B(distances, 1)
                B(conv2_even, 0)
                C(stack_rows)
                B(conv2_even, 1, 2, 3, 4, 5, 6, 7, 8)
                B(conv2_sum, 0)
                C(norm_transpose)
                B(conv2_sum, 1, 2)
                C(spread1)
                B(conv2_sum, 3)
                C(hidden2, 0, 1)
                A(hidden0_transposes, 0)
                B(conv2_sum, 4, 5)
                A(hidden0_transposes, 1)
                B(conv2_sum, 6)
                C(output2, 0, 1, 2, 3, 4)
                B(conv2_sum, 7)
                A(hidden0_transposes, 2, 3)
                B(conv2_sum, 8)
                C(y_transpose)
                B(messages, 0, 1)
                A(output0, 0)
                L(adj_transposes, 0)
                C(spread2)
                A(output0, 1, 2, 3)
                D(attend, 0)
                C(fuse)
                L(adj_transposes, 1)
                D(attend, 1)
                B(gate_hn)
                B(gates_early)
                B(gates_late)
                B(gate_z)

            turns(pe, turn, {1: constants3})

        @block.vector
        def _(dve):
            v = nc.vector
            link_at = [0]
            chain = link_sem

            def link(ins):
                link_at[0] += 1
                ins.then_inc(chain, 1)
                dve.wait_ge(chain, link_at[0])

            def split(hi, lo, raw):
                link(v.tensor_copy(hi, raw))
                return v.tensor_tensor(lo, raw, hi.bitcast(F32), ALU.subtract)

            def start0():
                dve.wait_ge(first_loaded, 16 * len(first_weights))
                v.tensor_scalar(epsI[:], ident, eps_c[:, 0:1], None, ALU.mult)
                dve.wait_ge(w1_in, 16)
                split(w1_hi[:], w1_lo[:], raw_w1).then_inc(prep0, 1)

            def start1():
                dve.wait_ge(bn_roots, 1)
                for k, (bn, s, o) in enumerate(((bn1_c, s1_c, o1_c), (bn2_c, s2_c, o2_c))):
                    link(v.tensor_tensor(s[:], bn[:, 0:1], bnw[:, k:k + 1], ALU.mult))
                    link(v.tensor_tensor(bnw[:, k + 2:k + 3], bn[:, 2:3], s[:], ALU.mult))
                    link(v.tensor_tensor(o[:], bn[:, 1:2], bnw[:, k + 2:k + 3], ALU.subtract))
                v.tensor_scalar(s2rep[:], ones[:], s2_c[:, 0:1], None, ALU.mult).then_inc(s2_spread, 1)

            def small_weights(p):
                if is_first(p):
                    dve.wait_ge(split_in, 48)
                    split(c1_hi[:], c1_lo[:], raw_c1)
                    dve.wait_ge(s2_mm, 1)
                    v.tensor_copy(s2_row[:], pC[:, 0:D]).then_inc(s2_out, 1)
                    dve.wait_ge(loaded, 16 * len(weights))
                    ROOT2 = 2.0 ** 0.5
                    link(v.tensor_scalar(wse_raw[:], wse_raw[:], ROOT2, None, ALU.mult))
                    link(v.tensor_scalar(bse_c[:], bse_c[:], ROOT2, None, ALU.mult))
                    split(se_hi[:], se_lo[:], wse_raw[:])
                    link(v.tensor_tensor(brz_c[:], bih_c[:, 0:2], bhh_c[:, 0:2], ALU.add))
                    v.tensor_scalar(brz_c[:], brz_c[:], 0.5, None, ALU.mult)
                    v.tensor_scalar(bhn_c[:], bhh_c[:, 2:3], 0.5, None, ALU.mult)
                    link(v.tensor_reduce(fwm[:], fw[:], AX.X, ALU.max))
                    link(v.tensor_scalar(fw[:], fw[:], fwm[:, 0:1], None, ALU.subtract))
                    v.tensor_copy(fwe[:], fw[:]).then_inc(prep1, 1)

            def gate_weights(p):
                if is_first(p):
                    split(hh_hi[:], hh_lo[:], raw_hh)
                    split(ih_hi[:].rearrange("p k n -> p (k n)"), ih_lo[:].rearrange("p k n -> p (k n)"), raw_ih
                          ).then_inc(prep_gates, 1)

            def conv2_low(p):
                if is_first(p):
                    dve.wait_ge(conv2_hi, 1)
                    v.tensor_tensor(c2_lo[:], raw_c2, c2_hi[:].bitcast(F32), ALU.subtract)
                    v.tensor_tensor(cs_lo[:], raw_cs, cs_hi[:].bitcast(F32), ALU.subtract).then_inc(conv2_lo, 1)

            def start3():
                for g in range(NG):
                    for c in range(C2):
                        a, n = G_START[g], G_SIZE[g]
                        v.tensor_scalar(hb_m[:, c, a:a + n], ones[:, 0:n], vb1_c[:, g, c:c + 1], None, ALU.mult)
                dve.wait_ge(fw_exp, 1)
                link(v.tensor_reduce(fws[:], fw[:], AX.X, ALU.add))
                link(v.reciprocal(fws[:], fws[:]))
                link(v.tensor_scalar(fwe[:], fw[:], fws[:, 0:1], None, ALU.mult))
                link(v.tensor_tensor(fwe[0:NS, :], fwe[0:NS, :], grp, ALU.mult))
                v.tensor_reduce(nw_row[0:NS, :], fwe[0:NS, :], AX.X, ALU.add)
                dve.wait_ge(consts3_mm, 1)
                v.tensor_copy(w3x[:, D:D + 1], pC[:, 1:2])
                link(v.tensor_copy(v1col[:], pC[:, 0:1]))
                v.tensor_tensor(fconst[:], pC[:, 2:3], ab_c[:], ALU.add)
                v.tensor_scalar(e_rep[:], ones[:], v1col[:, 0:1], None, ALU.mult).then_inc(prep3, 1)

            start0()

            def carry_wait(n):
                v.memset(tick[:, n:n + 1], 0.0)

            def norm_stats(k, tiles, n=P):
                carry_wait(2 * int(k) - 2)
                for q, tile in tiles:
                    i = v.bn_stats(ln_st[k][0:n, q, :], tile)
                i.then_inc(done["stats" + k], 1)

            def norm_mean(k, p, qs, n=P):
                dve.wait_ge(done["stats" + k], p + 1)
                carry_wait(2 * int(k) - 1)
                for q in qs:
                    i = v.bn_aggr(ln_mv[k][0:n, q, :], ln_st[k][0:n, q, :])
                i.then_inc(done["mean" + k], 1)

            def norm_apply(k, p, tiles, name, n=P):
                dve.wait_ge(done["rstd" + k], p + 1)
                for q, tile, dst in tiles:
                    i = v.tensor_scalar(dst, tile, ln_mv[k][0:n, q, 0:1], ln_rs[k][0:n, q:q + 1],
                                        ALU.subtract, ALU.mult)
                i.then_inc(done[name], 1)

            def norm1(p):
                dve.wait_ge(done["x_loaded"], (p + 1) * 16)
                norm_stats("1", [(q, x_tile(p, q)) for q in range(Q)])
                norm_mean("1", p, range(Q))
                dve.wait_ge(done["rstd1"], p + 1)
                before(dve, "h1", p)
                v.scalar_tensor_tensor(out=nb1[:], in0=ln_mv["1"][:, :, 0], scalar=-1.0, in1=ln_rs["1"][:],
                                       op0=ALU.mult, op1=ALU.mult).then_inc(done["nb1"], 1)

            def adjT_out(p):
                dve.wait_ge(done["adj_transposed"], 2 * (p + 1))
                v.tensor_copy(adjT(p, 1), pA[0][:]).then_inc(done["adjT"], 1)

            def agg_low(p):
                dve.wait_ge(done["agg_hi"], p + 1)
                before(dve, "w1_mm", p, Q)
                v.tensor_tensor(ag_lo[:], pA[0][:], ag_hi[:].bitcast(F32), ALU.subtract).then_inc(done["agg_lo"], 1)

            def hidden0_bias(p, *tiles):
                for q in tiles:
                    if q == 0:
                        before(dve, "w2_mm", p)
                    dve.wait_ge(done["w1_mm"], Q * p + q + 1)
                    v.tensor_tensor(hb[:, q, :], pA[1 - q % 2][:], b1_r[:], ALU.add).then_inc(done["hb"], 1)

            def hidden0_scale(p):
                dve.wait_ge(done["srs"], p + 1)
                for q in range(Q):
                    i = v.tensor_scalar(hb[:, q, :], hb[:, q, :], srs[:, q:q + 1], HID0 ** 0.5, ALU.mult, ALU.mult)
                i.then_inc(done["u0"], 1)

            def residual0(p):
                dve.wait_ge(done["w2_mm"], p + 1)
                dve.wait_ge(done["x_b2"], p + 1)
                v.tensor_tensor(x_pair(p), pA[1][:], x_pair(p), ALU.add).then_inc(done["x1"], 1)

            def norm2(p):
                dve.wait_ge(done["x1"], p + 1)
                norm_stats("2", [(q, x_tile(p, q)) for q in range(Q)])
                norm_mean("2", p, range(Q))

            def norm2_apply(p):
                before(dve, "h2_tr", p)
                norm_apply("2", p, [(q, x_tile(p, q), xn2[:, q * P:q * P + P]) for q in range(Q)], "xn2")

            def h2_low(p):
                dve.wait_ge(done["h2_hi"], p + 1)
                dve.wait_ge(done["h2_full"], p + 1)
                v.scalar_tensor_tensor(out=h2_lo[:], in0=pB[1][:], scalar=0.0, in1=h2_hi[:].bitcast(F32),
                                       op0=ALU.max, op1=ALU.subtract).then_inc(done["h2_lo"], 1)

            def dist_rows(p):
                dve.wait_ge(done["se_mm"], p + 1)
                before(dve, "dr", p)
                c = slice(CROSS, CROSS + 3 * DIMS)
                v.tensor_scalar(ds_x[c, :], pB[1][c, :], bse_c[c, 0:1], None, ALU.add).then_inc(done["ds_cross"], 1)

            def dist_operands(p):
                dve.wait_ge(done["ds_hi"], p + 1)
                before(dve, "dist_mm", p, 2)
                for k, (o, a, b) in enumerate(((dl, 0, CROSS + 3 * DIMS), (dr, CROSS, K_DIST))):
                    i = v.scalar_tensor_tensor(out=o[a:b, :], in0=ds_hi[a:b, :].bitcast(F32), scalar=minus_lo[a:b, k:k + 1],
                                               in1=ds_x[a:b, :], op0=ALU.mult, op1=ALU.add)
                i.then_inc(done["dr"], 1)

            def msg_bias(p):
                dve.wait_ge(done["msg_mm"], p + 1)
                before(dve, "nmp_mm", p)
                row = bmsg_r[:].rearrange("p (a d) -> p a d", a=1).broadcast_to([P, Q, D])
                v.tensor_tensor(msg_t[:].rearrange("p (q d) -> p q d", d=D), pB[2][:].rearrange("p (q d) -> p q d", d=D),
                                row, ALU.add).then_inc(done["msg_t"], 1)
                dve.wait_ge(done["msg_t"], p + 1)
                v.tensor_scalar(msg[:], msg_t[:], 0.0, None, ALU.max).then_inc(done["msg"], 1)

            def mask1(p, *graphs):
                for g in graphs:
                    dve.wait_ge(done["ex1"], 2 * p + g + 1)
                    v.tensor_tensor(ex1[:, g, :], ex1[:, g, :], adjT(p, g), ALU.mult).then_inc(done["amask1"], 1)

            def nmp_low(p):
                dve.wait_ge(done["nm_hi"], p + 1)
                v.tensor_tensor(nm_lo[:], pB[1][:], nm_hi[:].bitcast(F32), ALU.subtract).then_inc(done["nm_lo"], 1)

            def y1_low(p):
                dve.wait_ge(done["y1_full"], p + 1)
                v.tensor_tensor(y1_lo[:], y1_full[:], y1_hi[:].bitcast(F32), ALU.subtract).then_inc(done["y1_lo"], 1)

            def even_plus_odd(p):
                dve.wait_ge(done["y1_full"], p + 1)
                v.tensor_tensor(xs_full[:], y1_full[:, 0], y1_full[:, 1], ALU.add).then_inc(done["xs_full"], 1)

            def xs_low(p):
                dve.wait_ge(done["xs_hi"], p + 1)
                v.tensor_tensor(xs_lo[:], xs_full[:], xs_hi[:].bitcast(F32), ALU.subtract).then_inc(done["xs_lo"], 1)

            def conv_residual(p):
                dve.wait_ge(done["conv2_mm"], p + 1)
                dve.wait_ge(done["xc_base"], p + 1)
                xc = by_parity(xc_sum)
                v.scalar_tensor_tensor(out=xc, in0=pB[0][:].rearrange("p (r g i) -> p r g i", r=2, g=2), scalar=o2_c[:, 0:1],
                                       in1=xc, op0=ALU.add, op1=ALU.add).then_inc(done["xc_even"], 1)
                dve.wait_ge(done["xc_even"], p + 1)
                v.tensor_tensor(xc[:, 1], xc[:, 1], pB[0][:, 0:NODES].rearrange("p (g i) -> p g i", g=2), ALU.subtract).then_inc(done["xc_sum"], 1)

            def conv_low(p):
                dve.wait_ge(done["xc_hi"], p + 1)
                before(dve, "z_mm", p)
                v.scalar_tensor_tensor(out=xc_lo[:], in0=xc_sum[:], scalar=0.0, in1=xc_hi[:].bitcast(F32),
                                       op0=ALU.max, op1=ALU.subtract).then_inc(done["xc_lo"], 1)

            def gate_mix(p):
                dve.wait_ge(done["tr"], p + 1)
                dve.wait_ge(done["gh"], p + 1)
                before(dve, "gn", p)
                v.scalar_tensor_tensor(out=gm[:], in0=tr[:], scalar=1.0, in1=gh[:], op0=ALU.add,
                                       op1=ALU.mult).then_inc(done["gm1"], 1)
                dve.wait_ge(done["gm1"], p + 1)
                dve.wait_ge(done["gin_mm"], p + 1)
                v.tensor_tensor(gm[:], pB[1][:], gm[:], ALU.add).then_inc(done["gm"], 1)

            def gate_out(p):
                dve.wait_ge(done["gn"], p + 1)
                v.tensor_tensor(gd[:], h2_full[:], gn[:], ALU.subtract).then_inc(done["gd"], 1)
                dve.wait_ge(done["gd"], p + 1)
                dve.wait_ge(done["tz"], p + 1)
                v.scalar_tensor_tensor(out=gd[:], in0=tz[:], scalar=1.0, in1=gd[:], op0=ALU.add,
                                       op1=ALU.mult).then_inc(done["ge"], 1)
                dve.wait_ge(done["ge"], p + 1)
                before(dve, "go_tr", p)
                v.scalar_tensor_tensor(out=go[:], in0=gd[:], scalar=0.5, in1=gn[:], op0=ALU.mult,
                                       op1=ALU.add).then_inc(done["go"], 1)

            def residual1(p):
                dve.wait_ge(done["go_tr"], p + 1)
                v.tensor_tensor(x_pair(p), pB[2][:], x_pair(p), ALU.add).then_inc(done["x2"], 1)

            def joint_tiles(p):
                return [(0, x_tile(p, 0)[0:JOINTS, :]), (2, x_tile(p, 2)[0:JOINTS, :])]

            def joints_copy(p):
                dve.wait_ge(done["jq_mm"], p + 1)
                before(dve, "n0_mm", p)
                v.tensor_copy(jq[0:JP, :], pC[0:JP, 0:NS]).then_inc(done["jq"], 1)

            def norm3(p):
                dve.wait_ge(done["x2"], p + 1)
                norm_stats("3", joint_tiles(p), JOINTS)
                norm_mean("3", p, (0, 2), JOINTS)

            def norm3_apply(p):
                before(dve, "xs_mm", p)
                norm_apply("3", p, [(q, x, xj[32 * (q // 2):32 * (q // 2) + JOINTS, :]) for q, x in joint_tiles(p)],
                           "xn3", JOINTS)
                dve.wait_ge(done["xn3"], p + 1)
                v.tensor_scalar(xj[0:JP, :], xj[0:JP, :], 0.0, None, ALU.max).then_inc(done["xj"], 1)

            def degrees(p):
                dve.wait_ge(done["n0_mm"], p + 1)
                v.tensor_tensor(nsc[0:NS, :], pC[0:NS, 0:NS], same, ALU.mult).then_inc(done["nmask"], 1)
                dve.wait_ge(done["nmask"], p + 1)
                v.tensor_tensor(nmat[0:NS, :], nsc[0:NS, :], ident[0:NS, 0:NS], ALU.add).then_inc(done["nmat"], 1)
                dve.wait_ge(done["nmat"], p + 1)
                v.tensor_reduce(deg[0:NS, :], nmat[0:NS, :], AX.X, ALU.add).then_inc(done["dgz"], 1)
                dve.wait_ge(done["dgz"], 3 * p + 1)
                v.tensor_scalar(isz[0:NS, :], deg[0:NS, :], 0.0, None, ALU.is_equal).then_inc(done["dgz"], 1)
                dve.wait_ge(done["dgz"], 3 * p + 2)
                v.tensor_tensor(dsafe[0:NS, :], deg[0:NS, :], isz[0:NS, :], ALU.add).then_inc(done["dgz"], 1)

            def norm_rows(p):
                dve.wait_ge(done["dpw"], p + 1)
                v.tensor_tensor(dinv[0:NS, :], dpow[0:NS, :], isz[0:NS, :], ALU.mult).then_inc(done["dsf"], 1)
                dve.wait_ge(done["dsf"], p + 1)
                v.tensor_tensor(dinv[0:NS, :], dpow[0:NS, :], dinv[0:NS, :], ALU.subtract).then_inc(done["dinv"], 1)
                dve.wait_ge(done["dinv"], p + 1)
                v.tensor_scalar(nsc[0:NS, :], nmat[0:NS, :], dinv[0:NS, 0:1], None, ALU.mult).then_inc(done["nsc"], 1)

            def norm_cols(p):
                dve.wait_ge(done["n_tr"], p + 1)
                before(dve, "z2_mm", p)
                v.tensor_scalar(nT[0:NS, :], pC[0:NS, 0:NS], dinv[0:NS, 0:1], None, ALU.mult).then_inc(done["nT"], 1)

            def stack_copy(p):
                dve.wait_ge(done["xs_mm"], p + 1)
                before(dve, "t1_mm", p)
                v.tensor_copy(xs[0:NS, :], pC[0:NS, 0:D]).then_inc(done["xs"], 1)

            def hid_bias(p):
                dve.wait_ge(done["hid_mm"], p + 1)
                v.tensor_tensor(hid[:], pC[:, 0:C2 * NS].rearrange("p (c n) -> p c n", c=C2), hb_m[:], ALU.add
                                ).then_inc(done["hid"], 1)
                dve.wait_ge(done["hid"], p + 1)
                before(dve, "y_mm", p)
                v.tensor_scalar(hidr[:], hid[:], 0.0, None, ALU.max).then_inc(done["hidr"], 1)

            def z_bias(p):
                dve.wait_ge(done["z2_mm"], p + 1)
                v.tensor_tensor(zb[0:NS, :], pC[0:NS, 0:D], zb_m[:], ALU.add).then_inc(done["zb"], 1)
                dve.wait_ge(done["zb"], p + 1)
                before(dve, "fus_mm", p)
                v.tensor_scalar(zr[0:NS, :], zb[0:NS, :], 0.0, nw_row[0:NS, 0:1], ALU.max, ALU.mult
                                ).then_inc(done["zr"], 1)

            def residual2(p):
                dve.wait_ge(done["fus_mm"], p + 1)
                for a, (_, x) in enumerate(joint_tiles(p)):
                    i = v.tensor_tensor(x, pC[0:JOINTS, a * D:a * D + D], x, ALU.add)
                i.then_inc(done["x3"], 1)

            def norm4(p):
                dve.wait_ge(done["x3"], p + 1)
                norm_stats("4", [(q, x_tile(p, q)) for q in range(Q)])
                norm_mean("4", p, range(Q))

            def norm4_apply(p):
                before(dve, "h4_tr", p)
                norm_apply("4", p, [(q, x_tile(p, q), xn4[:, q * P:q * P + P]) for q in range(Q)], "xn4")

            def h3_bias(p):
                dve.wait_ge(done["e_mm"], 2 * p + 1)
                before(dve, "u3_mm", p)
                most = pD[1][:, 0:(Q - 1) * (D + 1)].rearrange("p (q d) -> p q d", d=D + 1)
                v.tensor_scalar(fcol[:, 0:Q - 1], most[:, :, D], fconst[:, 0:1], None, ALU.add)
                v.tensor_scalar(fcol[:, Q - 1:Q], pD[0][:, NODES + D:NODES + D + 1], fconst[:, 0:1], None, ALU.add)
                v.tensor_tensor(hx[:, Q - 1, 0:D], pD[0][:, NODES:NODES + D], b3_r[:], ALU.add).then_inc(done["fcol"], 1)
                row = b3_r[:].rearrange("p (a d) -> p a d", a=1).broadcast_to([P, Q - 1, D])
                v.tensor_tensor(hx[:, 0:Q - 1, 0:D], most[:, :, 0:D], row, ALU.add).then_inc(done["hx"], 1)

            def mask3(p, *graphs):
                for g in graphs:
                    dve.wait_ge(done["ex3"], Q * p + TILES * (g + 1))
                    v.tensor_tensor(ex3[:, g, :], ex3[:, g, :], adjT(p, g), ALU.mult).then_inc(done["u3"], 1)

            def attend_out(p):
                dve.wait_ge(done["u3_mm"], p + 1)
                for g in range(2):
                    src = pD[g][:, 0:TILES * (D + 1)].rearrange("p (q d) -> p q d", d=D + 1)
                    i = v.reciprocal(rec[:, g * TILES:(g + 1) * TILES], src[:, :, D])
                i.then_inc(done["rec"], 1)
                dve.wait_ge(done["rec"], p + 1)
                for q in range(Q):
                    g, nt = q // TILES, q % TILES
                    i = v.scalar_tensor_tensor(out=x_tile(p, q), in0=pD[g][:, nt * (D + 1):nt * (D + 1) + D],
                                               scalar=rec[:, q:q + 1], in1=x_tile(p, q), op0=ALU.mult, op1=ALU.add)
                i.then_inc(done["x4"], 1)

            def turn(l, a, b, c, d):
                def L(step, *args):
                    if l is not None:
                        step(l, *args)

                def A(step, *args):
                    if a is not None:
                        step(a, *args)

                def B(step, *args):
                    if b is not None:
                        step(b, *args)

                def C(step, *args):
                    if c is not None:
                        step(c, *args)

                def D(step, *args):
                    if d is not None:
                        step(d, *args)

                B(h2_low)
                A(small_weights)
                A(agg_low)
                C(residual1)
                B(dist_rows)
                A(hidden0_bias, 0, 1)
                C(norm3)
                B(dist_operands)
                B(y1_low)
                B(even_plus_odd)
                D(h3_bias)
                C(norm3_apply)
                C(joints_copy)
                B(msg_bias)
                B(xs_low)
                C(degrees)
                A(hidden0_bias, 2, 3)
                C(norm_rows)
                B(mask1, 0)
                C(stack_copy)
                C(norm_cols)
                A(hidden0_scale)
                C(hid_bias)
                B(mask1, 1)
                A(gate_weights)
                L(norm1)
                D(mask3, 0)
                A(conv2_low)
                D(mask3, 1)
                B(conv_residual)
                C(z_bias)
                B(nmp_low)
                B(conv_low)
                A(residual0)
                A(norm2)
                C(residual2)
                L(adjT_out)
                C(norm4)
                D(attend_out)
                A(norm2_apply)
                B(gate_mix)
                C(norm4_apply)
                B(gate_out)

            turns(dve, turn, {0: start1, 1: start3})

        @block.scalar
        def _(act):
            s = nc.scalar.activation
            def fusion_exp(p):
                if is_first(p):
                    act.wait_ge(prep1, 1)
                    s(fw[:], fwe[:], ACT.Exp).then_inc(fw_exp, 1)

            def conv2_high(p):
                if is_first(p):
                    act.wait_ge(conv2_scaled, 1)
                    s(c2_hi[:], raw_c2, ACT.Copy)
                    s(cs_hi[:], raw_cs, ACT.Copy).then_inc(conv2_hi, 1)

            act.wait_ge(first_loaded, 16 * len(first_weights))

            def adjT_out(p):
                act.wait_ge(done["adj_transposed"], 2 * p + 1)
                s(adjT(p, 0), pA[0][:], ACT.Copy).then_inc(done["adjT"], 1)

            def norm1_apply(p):
                act.wait_ge(done["nb1"], p + 1)
                before(act, "agg_mm", p)
                for q in range(Q):
                    i = s(h1[:, q * P:q * P + P], x_tile(p, q), ACT.Relu, scale=ln_rs["1"][:, q:q + 1], bias=nb1[:, q:q + 1])
                i.then_inc(done["h1"], 1)

            def agg_high(p):
                act.wait_ge(done["agg_mm"], p + 1)
                before(act, "w1_mm", p, Q)
                s(ag_hi[:], pA[0][:], ACT.Copy).then_inc(done["agg_hi"], 1)

            def squares(p, *tiles):
                if tiles[0] == 0:
                    before(act, "sve", p)
                for q in tiles:
                    act.wait_ge(done["hb"], Q * p + q + 1)
                    if q:
                        act.wait_ge(done["hsq"], Q * p + q)
                    s(hsq[:], hb[:, q, :], ACT.Square, accum_out=ssq[:, q:q + 1]).then_inc(done["hsq"], 1)

            def silu(p, *chunks):
                for c in chunks:
                    act.wait_ge(done["u_tr"], C0 * p + c + 1)
                    s(hb[:, :, c * P:c * P + P], pA[1 - c % 2][:].rearrange("p (q n) -> p q n", q=Q), ACT.Silu,
                      scale=rmsw_c[:, c:c + 1]).then_inc(done["sT"], 1)

            def h2_high(p):
                act.wait_ge(done["h2_tr"], p + 1)
                before(act, "z_mm", p)
                before(act, "gd", p)
                s(h2_hi[:], pB[1][:], ACT.Relu).then_inc(done["h2_hi"], 1)
                s(h2_full[:], pB[1][:], ACT.Relu).then_inc(done["h2_full"], 1)

            def conv1_out(p):
                act.wait_ge(done["conv1_mm"], p + 1)
                before(act, "conv2_mm", p)
                before(act, "y1_lo", p)
                before(act, "xs_full", p)
                for o, name in ((y1_hi, "y1_hi"), (y1_full, "y1_full")):
                    s(o[:, :, :, HALO:HALO + HALF], by_parity(pB[2]), ACT.Relu, scale=s1_c[:, 0:1], bias=o1_c[:, 0:1]
                      ).then_inc(done[name], 1)

            def xs_high(p):
                act.wait_ge(done["xs_full"], p + 1)
                before(act, "conv2_mm", p)
                s(xs_hi[:], xs_full[:], ACT.Copy).then_inc(done["xs_hi"], 1)

            def odd_copy(p):
                act.wait_ge(done["odd_mm"], p + 1)
                before(act, "xc_base", p)
                s(odd_s[:], pB[0][:, 0:2 * ODD_N].rearrange("p (g i) -> p g i", g=2), ACT.Copy
                  ).then_inc(done["odd_s"], 1)

            def dist_squares(p):
                act.wait_ge(done["se_mm"], p + 1)
                act.wait_ge(done["ds_cross"], p + 1)
                for a in (SQ_P, SQ_Q):
                    r = slice(a, a + 2 * DIMS)
                    i = s(ds_x[r, :], pB[1][r, :], ACT.Square, bias=bse_c[r, 0:1])
                i.then_inc(done["ds_sq"], 1)
                act.wait_ge(done["ds_sq"], p + 1)
                s(ds_hi[0:K_DIST, :], ds_x[0:K_DIST, :], ACT.Copy).then_inc(done["ds_hi"], 1)

            def exp1(p, *graphs):
                if graphs[0] == 0:
                    before(act, "nmp_mm", p)
                for g in graphs:
                    act.wait_ge(done["dist_mm"], 2 * p + g + 1)
                    s(ex1[:, g, :], pB[1 + g][:], ACT.Exp).then_inc(done["ex1"], 1)

            def exp_table(p):
                s(table_tick[:, 1:2], ones[:, 0:1], ACT.Exp)

            def silu_table(p):
                s(table_tick[:, 0:1], ones[:, 0:1], ACT.Silu)

            def nmp_high(p):
                act.wait_ge(done["nmp_mm"], p + 1)
                before(act, "z_mm", p)
                s(nm_hi[:], pB[1][:], ACT.Copy).then_inc(done["nm_hi"], 1)

            def conv_high(p):
                act.wait_ge(done["xc_sum"], p + 1)
                before(act, "z_mm", p)
                before(act, "xc_lo", p)
                s(xc_hi[:], xc_sum[:], ACT.Relu).then_inc(done["xc_hi"], 1)

            def gate_h(p):
                act.wait_ge(done["ghn_mm"], p + 1)
                before(act, "gm1", p)
                s(gh[:], pB[1][:], ACT.Identity, scale=0.5, bias=bhn_c[:, 0:1]).then_inc(done["gh"], 1)

            def gate_r(p):
                act.wait_ge(done["r_mm"], p + 1)
                before(act, "gm1", p)
                s(tr[:], pB[2][:], ACT.Tanh, scale=0.5, bias=brz_c[:, 0:1]).then_inc(done["tr"], 1)

            def gate_n(p):
                act.wait_ge(done["gm"], p + 1)
                before(act, "go", p)
                s(gn[:], gm[:], ACT.Tanh, bias=bih_c[:, 2:3]).then_inc(done["gn"], 1)

            def gate_z(p):
                act.wait_ge(done["z_mm"], p + 1)
                before(act, "ge", p)
                s(tz[:], pB[0][:], ACT.Tanh, scale=0.5, bias=brz_c[:, 1:2]).then_inc(done["tz"], 1)

            def t1_copy(p):
                act.wait_ge(done["t1_mm"], p + 1)
                before(act, "hid_mm", p)
                s(t1[:], pC[:, 0:NS], ACT.Copy).then_inc(done["t1"], 1)

            def y_copy(p):
                act.wait_ge(done["y_mm"], p + 1)
                before(act, "y_tr", p)
                s(yT[:], pC[:, 0:NS], ACT.Copy).then_inc(done["yT"], 1)

            def ys_copy(p):
                act.wait_ge(done["y_tr"], p + 1)
                before(act, "z2_mm", p)
                s(ys[0:NS, :], pC[0:NS, 0:P], ACT.Copy).then_inc(done["ys"], 1)

            def h4_out(p):
                act.wait_ge(done["h4_tr"], p + 1)
                before(act, "e_mm", p, 2)
                s(h4T[:], pD[0][:], ACT.Relu).then_inc(done["h4T"], 1)

            def exp3(p, *graphs):
                if graphs[0] == 0:
                    act.wait_ge(done["fcol"], p + 1)
                    before(act, "u3_mm", p)
                for g in graphs:
                    act.wait_ge(done["e_mm"], 2 * p + g + 1)
                    for mt in range(TILES):
                        s(ex3[:, g, mt * NODES:(mt + 1) * NODES], pD[g][:, 0:NODES], ACT.Exp,
                          bias=fcol[:, g * TILES + mt:g * TILES + mt + 1]).then_inc(done["ex3"], 1)

            def turn(l, a, b, c, d):
                def L(step, *args):
                    if l is not None:
                        step(l, *args)

                def A(step, *args):
                    if a is not None:
                        step(a, *args)

                def B(step, *args):
                    if b is not None:
                        step(b, *args)

                def C(step, *args):
                    if c is not None:
                        step(c, *args)

                def D(step, *args):
                    if d is not None:
                        step(d, *args)

                B(h2_high)
                A(silu_table)
                A(agg_high)
                D(exp_table)
                D(h4_out)
                B(dist_squares)
                B(conv1_out)
                B(exp1, 0)
                B(xs_high)
                A(squares, 0)
                B(odd_copy)
                A(squares, 1)
                D(exp3, 0)
                A(squares, 2, 3)
                D(exp3, 1)
                B(exp1, 1)
                A(conv2_high)
                C(t1_copy)
                A(silu, 0, 1)
                C(y_copy)
                A(silu, 2, 3)
                C(ys_copy)
                A(fusion_exp)
                B(nmp_high)
                L(norm1_apply)
                L(adjT_out)
                B(conv_high)
                B(gate_h)
                B(gate_r)
                B(gate_n)
                B(gate_z)

            turns(act, turn)

        @block.gpsimd
        def _(pool):
            g_ = nc.gpsimd
            g_.memset(jadj[:], 0.0)
            g_.memset(xj[:], 0.0)
            g_.memset(ones[:], 1.0).then_inc(pool_mem, 1)
            pool.wait_ge(pool_mem, 1)
            g_.memset(epsln[:], LN_EPS)
            g_.memset(epsrms[:], RMS_EPS * HID0)
            g_.memset(mhalf[:], -0.5).then_inc(pool_ready, 1)
            g_.memset(y1_hi[:].bitcast(F32), 0.0)
            g_.memset(y1_full[:], 0.0)
            g_.memset(ds_x[:], 0.0)
            g_.memset(dl[:].bitcast(F32), -0.5)
            g_.memset(dr[:].bitcast(F32), -0.5)
            g_.memset(hx[:], 1.0).then_inc(pool_mem, 1)
            pool.wait_ge(pool_mem, 2)

            pool.wait_ge(first_loaded, 16 * len(first_weights))
            g_.tensor_scalar(bnw[:, 0:1], bn1_c[:, 3:4], BN_EPS, None, ALU.add)
            g_.tensor_scalar(bnw[:, 1:2], bn2_c[:, 3:4], BN_EPS, None, ALU.add).then_inc(pool_mem, 1)
            pool.wait_ge(pool_mem, 3)
            g_.tensor_tensor(bnw[:, 0:2], bnw[:, 0:2], mhalf[:, 0:2], ALU.pow).then_inc(bn_roots, 1)
            g_.tensor_scalar(b3rep[:], ones[:], b3_c[:, 0:1], None, ALU.mult)
            g_.tensor_tensor(a12_c[:], a3_c[:, 0:1], a3_c[:, 1:2], ALU.add).then_inc(prep_g, 1)

            def scale_conv2(p):
                if is_first(p):
                    pool.wait_ge(conv2_in, 16)
                    pool.wait_ge(s2_out, 1)
                    taps = raw_c2.rearrange("p (k d) -> p k d", d=D)
                    row = s2_row[:].rearrange("p (a d) -> p a d", a=1).broadcast_to([P, TAPS, D])
                    g_.tensor_tensor(taps, taps, row, ALU.mult).then_inc(pool_mem, 1)
                    pool.wait_ge(pool_mem, 4)
                    both = raw_c2[:, D:].rearrange("p (j r d) -> p j r d", r=2, d=D)
                    g_.tensor_tensor(raw_cs.rearrange("p (j d) -> p j d", d=D), both[:, :, 0, :], both[:, :, 1, :], ALU.add
                                     ).then_inc(conv2_scaled, 1)

            def rstd(p, k):
                n = JOINTS if k == "3" else P
                qs = slice(0, Q, 2) if k == "3" else slice(0, Q)
                pool.wait_ge(done["mean" + k], p + 1)
                g_.tensor_tensor(ln_ve[k][0:n, qs], ln_mv[k][0:n, qs, 1], epsln[0:n, qs], ALU.add).then_inc(done["ve" + k], 1)
                pool.wait_ge(done["ve" + k], p + 1)
                g_.tensor_tensor(ln_rs[k][0:n, qs], ln_ve[k][0:n, qs], mhalf[0:n, qs], ALU.pow).then_inc(done["rstd" + k], 1)

            def adj_eps(p):
                at_first(pool, p, prep0)
                pool.wait_ge(done["adjT"], 2 * (p + 1))
                before(pool, "agg_mm", p)
                for g in range(2):
                    for t in range(TILES):
                        i = g_.tensor_tensor(adjE[:, g * TILES + t, :], adjT(p, g, t * NODES + t * P, P), epsI[:], ALU.add)
                i.then_inc(done["adjE"], 1)

            def x_bias(p):
                pool.wait_ge(done["h1"], p + 1)
                row = b2_r[:].rearrange("p (a d) -> p a d", a=1).broadcast_to([P, Q, D])
                xp = x_pair(p).rearrange("p (q d) -> p q d", d=D)
                g_.tensor_tensor(xp, xp, row, ALU.add).then_inc(done["x_b2"], 1)

            def rms(p):
                pool.wait_ge(done["hsq"], Q * (p + 1))
                g_.tensor_tensor(sve[:], ssq[:], epsrms[:], ALU.add).then_inc(done["sve"], 1)
                pool.wait_ge(done["sve"], p + 1)
                g_.tensor_tensor(srs[:], sve[:], mhalf[:, 0:Q], ALU.pow).then_inc(done["srs"], 1)

            def xc_base(p):
                pool.wait_ge(done["odd_s"], p + 1)
                pool.wait_ge(done["h2_full"], p + 1)
                before(pool, "xc_lo", p)
                xc, h = by_parity(xc_sum), by_parity(h2_full)
                g_.tensor_tensor(xc[:, 0], h[:, 0], odd_s[:, :, 0:HALF], ALU.add)
                g_.tensor_tensor(xc[:, 1], h[:, 1], odd_s[:, :, 1:HALF + 1], ALU.subtract).then_inc(done["xc_base"], 1)

            def degree_root(p):
                pool.wait_ge(done["dgz"], 3 * (p + 1))
                g_.tensor_tensor(dpow[0:NS, :], dsafe[0:NS, :], mhalf[0:NS, 0:1], ALU.pow).then_inc(done["dpw"], 1)

            def turn(l, a, b, c, d):
                def L(step, *args):
                    if l is not None:
                        step(l, *args)

                def A(step, *args):
                    if a is not None:
                        step(a, *args)

                def B(step, *args):
                    if b is not None:
                        step(b, *args)

                def C(step, *args):
                    if c is not None:
                        step(c, *args)

                def D(step, *args):
                    if d is not None:
                        step(d, *args)

                A(x_bias)
                C(rstd, "3")
                C(degree_root)
                B(xc_base)
                A(scale_conv2)
                A(rms)
                L(rstd, "1")
                A(rstd, "2")
                L(adj_eps)
                C(rstd, "4")

            turns(pool, turn)


def kernel(**inputs):
    import numpy as np
    import concourse.bacc as bacc
    from concourse.bass_utils import run_bass_kernel_spmd

    f = {k: np.asarray(v) for k, v in inputs.items()}
    consts = np.zeros((P, K_COLS), np.float32)
    consts[:, K_IDENT:K_IDENT + P] = np.eye(P)
    for i, (g, a, n) in enumerate(STACK):
        consts[32 * a + n, K_SEL + i] = 1
        consts[i, K_BACK + 32 * a + n] = 1
        consts[i, K_GRP + g] = 1
        for j, (g2, a2, _) in enumerate(STACK):
            consts[i, K_SAME + j] = g == g2 and a == a2
    L0, L1, L2, L3 = "L0_gnn_", "L1_gnn_", "L2_gnn_", "L3_gnn_"
    bn1, bn2 = (np.stack([f[L1 + bn + k] for k in "gbmv"]) for bn in ("bn1_", "bn2_"))
    w_se, b_se = np.zeros((D, P), np.float32), np.zeros((P, 1), np.float32)
    minus_lo = np.zeros((P, 2), np.float32)
    for k, at in enumerate((SQ_P, SQ_P + DIMS, CROSS, CROSS + DIMS, CROSS + 2 * DIMS, SQ_Q, SQ_Q + DIMS)):
        rows = slice(at, at + DIMS)
        w_se[:, rows], b_se[rows, 0] = f[L1 + "w_se"].T, f[L1 + "b_se"]
        minus_lo[rows] = [-(k in (1, 4)), -(k in (3, 6))]
    vectors = {"rms_w": f[L0 + "rms_weight"].reshape(C0, P).T, "bn1": bn1.T, "bn2": bn2.T,
               "b_ih": f[L1 + "b_ih"].reshape(3, P).T, "b_hh": f[L1 + "b_hh"].reshape(3, P).T,
               "l2_b1": f[L2 + "b1"].reshape(NG * C2, P).T, "b3": f[L3 + "W_b"].reshape(P, 1),
               "a3": f[L3 + "a_w"].reshape(2, P).T, "b_se": b_se, "minus_lo": minus_lo}
    laid = [
        f["x"], f["adj"], f[L0 + "epsilon"].reshape(1), f[L0 + "W1"], f[L0 + "b1"], f[L0 + "W2"],
        f[L0 + "b2"], w_se, f[L1 + "conv1_w"][:, :, 0].T,
        f[L1 + "conv2_w"].transpose(1, 2, 0).reshape(D, TAPS * D), f[L1 + "w_msg"].T, f[L1 + "b_msg"],
        f[L1 + "w_ih"].T, f[L1 + "w_hh"].T, f[L2 + "W1"], f[L2 + "W2"], f[L2 + "b2"],
        f[L2 + "fusion_w"], f[L3 + "W_w"], f[L3 + "W_w"].T, f[L3 + "W_b"], f[L3 + "a_b"], consts,
        np.concatenate([vectors[k] for k in VECTORS], 1),
    ]
    nc = bacc.Bacc("TRN2", target_bir_lowering=False, num_devices=1)
    arrays, args = {}, []
    for i, a in enumerate(laid):
        a = np.ascontiguousarray(a)
        arrays[f"in_{i}_dram"] = a
        args.append(nc.dram_tensor(f"in_{i}_dram", a.shape, mybir.dt.from_np(a.dtype), kind="ExternalInput").ap())
    args.append(nc.dram_tensor("out_dram", (GRAPHS, NODES, D), F32, kind="ExternalOutput").ap())
    build(nc, *args)
    r = run_bass_kernel_spmd(nc, [arrays], core_ids=[0])
    return r.results[0]["out_dram"]
```
